# Optimizing a Trainium2 kernel written in Bass

```python
import numpy as np
import jax
import jax.numpy as jnp

def _softmax(x, axis=-1):
    return jax.nn.softmax(x, axis=axis)

def _gelu(x):
    return jax.nn.gelu(x, approximate=True)

def _silu(x):
    return jax.nn.silu(x)

def _sigmoid(x):
    return jax.nn.sigmoid(x)

def _layernorm(x, axis=-1, eps=1e-05):
    m = jnp.mean(x, axis=axis, keepdims=True)
    v = jnp.var(x, axis=axis, keepdims=True)
    return (x - m) / jnp.sqrt(v + eps)

def _scatter_add(tgt, idx, src, axis=0):
    return tgt.at[idx].add(src)

def _segment_sum(src, seg, n):
    return jax.ops.segment_sum(src, seg, n)
kernel_name = 'mk_seq_preln_d1_jaxref_r4_1d669d'

def setup_inputs(seed: int=0):
    np.random.seed(seed)
    _w = jnp.asarray

    def _L0_attn_setup():
        import jax, jax.numpy as jnp
        import numpy as np
        from jax import lax
        D_STATE = 16
        DT_RANK = 64

        def _layernorm(x, g, b, eps=1e-05):
            mu = jnp.mean(x, axis=-1, keepdims=True)
            var = jnp.var(x, axis=-1, keepdims=True)
            return (x - mu) * lax.rsqrt(var + eps) * g + b

        def _causal_depthwise_conv(x, w, b):
            B, L, C = x.shape
            K = w.shape[-1]
            xc = jnp.transpose(x, (0, 2, 1))
            y = lax.conv_general_dilated(xc, w, window_strides=(1,), padding=[(K - 1, 0)], dimension_numbers=('NCH', 'OIH', 'NCH'), feature_group_count=C)
            return jnp.transpose(y + b[None, :, None], (0, 2, 1))

        def _selective_scan(u, delta, A, Bm, Cm, D):
            Bsz, L, Di = u.shape
            N = A.shape[-1]
            xs = (jnp.transpose(delta, (1, 0, 2)), jnp.transpose(Bm, (1, 0, 2)), jnp.transpose(Cm, (1, 0, 2)), jnp.transpose(u, (1, 0, 2)))

            def step(s, inp):
                d_t, B_t, C_t, u_t = inp
                dA = jnp.exp(d_t[..., None] * A)
                dBu = d_t[..., None] * B_t[:, None, :] * u_t[..., None]
                s = dA * s + dBu
                y_t = jnp.einsum('bdn,bn->bd', s, C_t)
                return (s, y_t)
            s0 = jnp.zeros((Bsz, Di, N), dtype=u.dtype)
            _, ys = lax.scan(step, s0, xs)
            y = jnp.transpose(ys, (1, 0, 2))
            return y + u * D

        def _mamba(h, W_in, conv_w, conv_b, W_xproj, W_dt, b_dt, A_log, D_param, W_out):
            xz = h @ W_in
            x_in, z = jnp.split(xz, 2, axis=-1)
            x_c = jax.nn.silu(_causal_depthwise_conv(x_in, conv_w, conv_b))
            dbc = x_c @ W_xproj
            dt, Bm, Cm = jnp.split(dbc, [DT_RANK, DT_RANK + D_STATE], axis=-1)
            delta = jax.nn.softplus(dt @ W_dt + b_dt)
            A = -jnp.exp(A_log)
            y = _selective_scan(x_c, delta, A, Bm, Cm, D_param)
            y = y * jax.nn.silu(z)
            return y @ W_out
        key = jax.random.key(seed)
        ks = jax.random.split(key, 10)
        B, L, d = (2, 256, 256)
        Di = 2 * d
        inp = {}
        inp['x'] = jax.random.normal(ks[0], (B, L, d), jnp.float32)
        inp['ln_g'] = jnp.ones((d,), jnp.float32)
        inp['ln_b'] = jnp.zeros((d,), jnp.float32)
        inp['W_in'] = jax.random.normal(ks[1], (d, 2 * Di), jnp.float32) / np.sqrt(d)
        inp['conv_w'] = jax.random.normal(ks[2], (Di, 1, 4), jnp.float32) * 0.5
        inp['conv_b'] = jnp.zeros((Di,), jnp.float32)
        inp['W_xproj'] = jax.random.normal(ks[3], (Di, DT_RANK + 2 * D_STATE), jnp.float32) / np.sqrt(Di)
        inp['W_dt'] = jax.random.normal(ks[4], (DT_RANK, Di), jnp.float32) / np.sqrt(DT_RANK)
        inp['b_dt'] = jax.random.normal(ks[5], (Di,), jnp.float32) * 0.1
        inp['A_log'] = jnp.log(jnp.broadcast_to(jnp.arange(1, D_STATE + 1, dtype=jnp.float32), (Di, D_STATE)))
        inp['D_param'] = jnp.ones((Di,), jnp.float32)
        inp['W_out'] = jax.random.normal(ks[6], (Di, d), jnp.float32) / np.sqrt(Di)
        return inp
    _L0_attn_in = _L0_attn_setup()

    def _L0_ffn_setup():
        import jax, jax.numpy as jnp
        import numpy as np
        D_MODEL = 256
        N_EXPERTS = 8
        TOP_K = 2
        LN_EPS = 1e-05
        key = jax.random.key(seed)
        ks = jax.random.split(key, 8)
        B, S, d, E = (2, 512, D_MODEL, N_EXPERTS)
        f = 2 * d
        s_in = 0.02
        return {'x': jax.random.normal(ks[0], (B, S, d), jnp.float32), 'Wg': jax.random.normal(ks[1], (d, E), jnp.float32) * s_in, 'bg': jnp.zeros((E,), jnp.float32), 'W1': jax.random.normal(ks[2], (E, d, f), jnp.float32) * s_in, 'b1': jnp.zeros((E, f), jnp.float32), 'W2': jax.random.normal(ks[3], (E, f, d), jnp.float32) * s_in, 'b2': jnp.zeros((E, d), jnp.float32), 'gamma': jnp.ones((d,), jnp.float32), 'beta': jnp.zeros((d,), jnp.float32)}
    _L0_ffn_in = _L0_ffn_setup()
    _d = {'L0_attn_x': _L0_attn_in['x'], 'L0_attn_ln_g': _L0_attn_in['ln_g'], 'L0_attn_ln_b': _L0_attn_in['ln_b'], 'L0_attn_W_in': _L0_attn_in['W_in'], 'L0_attn_conv_w': _L0_attn_in['conv_w'], 'L0_attn_conv_b': _L0_attn_in['conv_b'], 'L0_attn_W_xproj': _L0_attn_in['W_xproj'], 'L0_attn_W_dt': _L0_attn_in['W_dt'], 'L0_attn_b_dt': _L0_attn_in['b_dt'], 'L0_attn_A_log': _L0_attn_in['A_log'], 'L0_attn_D_param': _L0_attn_in['D_param'], 'L0_attn_W_out': _L0_attn_in['W_out'], 'L0_ffn_Wg': _L0_ffn_in['Wg'], 'L0_ffn_bg': _L0_ffn_in['bg'], 'L0_ffn_W1': _L0_ffn_in['W1'], 'L0_ffn_b1': _L0_ffn_in['b1'], 'L0_ffn_W2': _L0_ffn_in['W2'], 'L0_ffn_b2': _L0_ffn_in['b2'], 'L0_ffn_gamma': _L0_ffn_in['gamma'], 'L0_ffn_beta': _L0_ffn_in['beta']}
    _x0 = _d['L0_attn_x']
    _d['L0_attn_x'] = jax.random.normal(jax.random.fold_in(jax.random.key(seed), 1), (8, 1024, 256), dtype=_x0.dtype)
    del _x0
    return _d

def reference(L0_attn_x, L0_attn_ln_g, L0_attn_ln_b, L0_attn_W_in, L0_attn_conv_w, L0_attn_conv_b, L0_attn_W_xproj, L0_attn_W_dt, L0_attn_b_dt, L0_attn_A_log, L0_attn_D_param, L0_attn_W_out, L0_ffn_Wg, L0_ffn_bg, L0_ffn_W1, L0_ffn_b1, L0_ffn_W2, L0_ffn_b2, L0_ffn_gamma, L0_ffn_beta):

    def _L0_attn_ref(x, ln_g, ln_b, W_in, conv_w, conv_b, W_xproj, W_dt, b_dt, A_log, D_param, W_out):
        import jax, jax.numpy as jnp
        import numpy as np
        from jax import lax
        D_STATE = 16
        DT_RANK = 64

        def _layernorm(x, g, b, eps=1e-05):
            mu = jnp.mean(x, axis=-1, keepdims=True)
            var = jnp.var(x, axis=-1, keepdims=True)
            return (x - mu) * lax.rsqrt(var + eps) * g + b

        def _causal_depthwise_conv(x, w, b):
            B, L, C = x.shape
            K = w.shape[-1]
            xc = jnp.transpose(x, (0, 2, 1))
            y = lax.conv_general_dilated(xc, w, window_strides=(1,), padding=[(K - 1, 0)], dimension_numbers=('NCH', 'OIH', 'NCH'), feature_group_count=C)
            return jnp.transpose(y + b[None, :, None], (0, 2, 1))

        def _selective_scan(u, delta, A, Bm, Cm, D):
            Bsz, L, Di = u.shape
            N = A.shape[-1]
            xs = (jnp.transpose(delta, (1, 0, 2)), jnp.transpose(Bm, (1, 0, 2)), jnp.transpose(Cm, (1, 0, 2)), jnp.transpose(u, (1, 0, 2)))

            def step(s, inp):
                d_t, B_t, C_t, u_t = inp
                dA = jnp.exp(d_t[..., None] * A)
                dBu = d_t[..., None] * B_t[:, None, :] * u_t[..., None]
                s = dA * s + dBu
                y_t = jnp.einsum('bdn,bn->bd', s, C_t)
                return (s, y_t)
            s0 = jnp.zeros((Bsz, Di, N), dtype=u.dtype)
            _, ys = lax.scan(step, s0, xs)
            y = jnp.transpose(ys, (1, 0, 2))
            return y + u * D

        def _mamba(h, W_in, conv_w, conv_b, W_xproj, W_dt, b_dt, A_log, D_param, W_out):
            xz = h @ W_in
            x_in, z = jnp.split(xz, 2, axis=-1)
            x_c = jax.nn.silu(_causal_depthwise_conv(x_in, conv_w, conv_b))
            dbc = x_c @ W_xproj
            dt, Bm, Cm = jnp.split(dbc, [DT_RANK, DT_RANK + D_STATE], axis=-1)
            delta = jax.nn.softplus(dt @ W_dt + b_dt)
            A = -jnp.exp(A_log)
            y = _selective_scan(x_c, delta, A, Bm, Cm, D_param)
            y = y * jax.nn.silu(z)
            return y @ W_out
        h = _layernorm(x, ln_g, ln_b)
        return x + _mamba(h, W_in, conv_w, conv_b, W_xproj, W_dt, b_dt, A_log, D_param, W_out)

    def _L0_ffn_ref(x, Wg, bg, W1, b1, W2, b2, gamma, beta):
        import jax, jax.numpy as jnp
        import numpy as np
        D_MODEL = 256
        N_EXPERTS = 8
        TOP_K = 2
        LN_EPS = 1e-05
        logits = jnp.einsum('bsd,de->bse', x, Wg) + bg
        topk_vals, topk_idx = jax.lax.top_k(logits, TOP_K)
        topk_w = jax.nn.softmax(topk_vals, axis=-1)
        h = jax.nn.relu(jnp.einsum('bsd,edf->bsef', x, W1) + b1)
        eo = jnp.einsum('bsef,efd->bsed', h, W2) + b2
        sel = jnp.take_along_axis(eo, topk_idx[..., None], axis=2)
        mixed = jnp.sum(sel * topk_w[..., None], axis=2)
        y = mixed + x
        mu = jnp.mean(y, axis=-1, keepdims=True)
        var = jnp.mean(jnp.square(y - mu), axis=-1, keepdims=True)
        return gamma * (y - mu) * jax.lax.rsqrt(var + LN_EPS) + beta
    x = L0_attn_x
    x = x + _L0_attn_ref(_layernorm(x, axis=-1), L0_attn_ln_g, L0_attn_ln_b, L0_attn_W_in, L0_attn_conv_w, L0_attn_conv_b, L0_attn_W_xproj, L0_attn_W_dt, L0_attn_b_dt, L0_attn_A_log, L0_attn_D_param, L0_attn_W_out)
    x = x + _L0_ffn_ref(_layernorm(x, axis=-1), L0_ffn_Wg, L0_ffn_bg, L0_ffn_W1, L0_ffn_b1, L0_ffn_W2, L0_ffn_b2, L0_ffn_gamma, L0_ffn_beta)
    return x

_drawn_inputs = setup_inputs


def setup_inputs(seed=0):
    import zlib

    import numpy as np

    out = dict(_drawn_inputs(seed))
    spreads = {'L0_attn_ln_g': (1.0, 0.2),
     'L0_attn_ln_b': (0.0, 0.1),
     'L0_attn_conv_b': (0.0, 0.1),
     'L0_attn_D_param': (1.0, 0.2),
     'L0_ffn_bg': (0.0, 0.515),
     'L0_ffn_b1': (0.0, 0.8),
     'L0_ffn_b2': (0.0, 0.346),
     'L0_ffn_gamma': (1.0, 0.2),
     'L0_ffn_beta': (0.0, 0.1)}
    factors = {'L0_attn_b_dt': 3.025, 'L0_ffn_W1': 2.89}
    for name, (base, spread) in spreads.items():
        noise = np.random.default_rng([zlib.crc32(name.encode()), seed]).standard_normal(out[name].shape)
        drawn = base * np.exp(spread * noise) if base else spread * noise
        out[name] = jnp.asarray(drawn.astype(out[name].dtype))
    for name, factor in factors.items():
        out[name] = (out[name] * factor).astype(out[name].dtype)
    return out
```

```python
from contextlib import ExitStack

import concourse.bass as bass
from concourse import mybir

P = 128
CH = 512
NT = CH // P
EPS = 1e-5

ALU = mybir.AluOpType
ACT = mybir.ActivationFunctionType
AX = mybir.AxisListType
F32 = mybir.dt.float32
I32 = mybir.dt.int32
U32 = mybir.dt.uint32
B_TILES = 64


def wait(eng, sem, per, c, k):
    if isinstance(c, int):
        if per * c + k > 0:
            eng.wait_ge(sem, per * c + k)
    else:
        eng.wait_ge(sem, c * per + k)


def wait_apart(eng, passed, waits):
    for sem, per, c, k in waits:
        wait(eng, sem, per, c, k)
        if not isinstance(c, int):
            eng.sem_inc(passed, 1)


def mamba_moe_kernel(nc, x, ln_g, ln_b, W_in, conv_w, conv_b, W_xproj, W_dt, b_dt, A_log, D_param, W_out,
                     Wg, bg, W1, b1, W2, b2, gamma, beta, out):
    B, L, D = x.shape
    DI = W_in.shape[1] // 2
    G = DI // P
    KD = D // P
    N = A_log.shape[1]
    R = W_dt.shape[0]
    TAPS = conv_w.shape[2]
    HALO = TAPS - 1
    NC = B * L // CH
    assert L == 2 * CH and NC % 2 == 0 and NT == 4 and G == 4 and KD == 2 and R + 2 * N == 96
    E = Wg.shape[1]
    F = W1.shape[2]

    xf = x.rearrange("b l d -> (b l) d")
    x_t = xf.rearrange("(c i p) d -> c p i d", p=P, i=NT)
    x1_dram = nc.dram_tensor("x1_scratch", (B * L, D), F32, kind="Internal").ap()
    x1_t = x1_dram.rearrange("(c i p) d -> c p i d", p=P, i=NT)
    b_dram = nc.dram_tensor("b_scratch", (2, N, CH), F32, kind="Internal").ap()

    mamba_block(nc, x_t, x1_t, b_dram, ln_g, ln_b, W_in, conv_w, conv_b, W_xproj, W_dt, b_dt, A_log, D_param,
                W_out, NC, D, DI, G, KD, N, R, TAPS, HALO)
    REG = (B * L // P + 1) * P
    NTT = 2 * B * L // P + E - 1
    NTT += 1 - NTT % 2
    spare = NTT - 2 * B * L // P
    xf_t = nc.dram_tensor("xf_scratch", (NC, P, NT, D), F32, kind="Internal").ap()
    xs_dram = nc.dram_tensor("xs_scratch", (E * REG + spare * P, D), F32, kind="Internal").ap()
    eo_dram = nc.dram_tensor("eo_scratch", (NTT * P, D), F32, kind="Internal").ap()
    slots_dram = nc.dram_tensor("slots_scratch", (NC, P, 2, NT), U32, kind="Internal").ap()
    w_dram = nc.dram_tensor("w_scratch", (NC, P, 2, NT), F32, kind="Internal").ap()
    tab = nc.dram_tensor("tile_table", (1, 2, NTT), I32, kind="Internal").ap()
    route_block(nc, x1_t, xf_t, xs_dram, xs_dram[E * REG:, :], tab, slots_dram, w_dram, Wg, bg, NC, D, KD, E, REG,
                NTT)
    experts_block(nc, xs_dram, eo_dram, tab, W1, b1, W2, b2, D, KD, E, F, REG, NTT)
    combine_block(nc, x1_t, xf_t, eo_dram, slots_dram, w_dram, gamma, beta,
                  out.rearrange("b l d -> (b l) d").rearrange("(c i p) d -> c p i d", p=P, i=NT), NC, D)


def mamba_block(nc, x_t, x1_t, b_dram, ln_g, ln_b, W_in, conv_w, conv_b, W_xproj, W_dt, b_dt, A_log, D_param,
                W_out, NC, D, DI, G, KD, N, R, TAPS, HALO):
    NB = 8
    K_DT = 97
    SG = N * G
    with ExitStack() as ctx:
        def sb(name, shape):
            return ctx.enter_context(nc.sbuf_tensor(name, shape, F32))

        def sem(name):
            return ctx.enter_context(nc.semaphore(name))

        ident = sb("ident", [P, P])
        win = sb("win", [P, KD, 2 * DI])
        wxp = sb("wxp", [P, G, R + 2 * N])
        wdt = sb("wdt", [K_DT, DI])
        wout = sb("wout", [P, G, D])
        a_neg = sb("a_neg", [P, G, N])
        cw = sb("cw", [P, G, TAPS])
        cb = sb("cb", [P, G])
        dp = sb("dp", [P, G])
        lng = sb("lng", [P, KD])
        lnb = sb("lnb", [P, KD])
        taps = sb("taps", [P, G, TAPS, P])
        xb = sb("xb", [P, 2, NT, D])
        xl = sb("xl", [P, 2, NT, D])
        xn = sb("xn", [P, NT, D])
        h0 = sb("h0", [P, NT, D])
        st = sb("st", [P, 2, NT, 6])
        mv = sb("mv", [P, 2, NT, 2])
        ve = sb("ve", [P, 2, NT])
        rs = sb("rs", [P, 2, NT])
        mhalf = sb("mhalf", [P, NT])
        hT = sb("hT", [P, KD, CH])
        xin = sb("xin", [P, G, HALO + CH])
        zs = sb("zs", [P, 2, G, CH])
        xc = sb("xc", [P, 2, G, CH])
        dbc = sb("dbc", [K_DT, CH])
        cT = sb("cT", [P, 2, NT, N])
        sp = sb("sp", [P, G, CH])
        dl = sb("dl", [P, 2, G, CH])
        du = sb("du", [P, 2, G, CH])
        bb = sb("bb", [P, NB, CH])
        dbu = sb("dbu", [P, 2, G, CH])
        ss = sb("ss", [P, 2, G, CH])
        carry = sb("carry", [P, N, G])
        ya = sb("ya", [P, 2, NT, DI])
        yg = sb("yg", [P, G, CH])
        ps_a = ctx.enter_context(nc.psum_tensor("ps_a", [P, G, CH], F32))
        ps_s = ctx.enter_context(nc.psum_tensor("ps_s", [P, 2, DI], F32))
        ps_p = ctx.enter_context(nc.psum_tensor("ps_p", [P, 2, CH], F32))

        passed = sem("passed")
        w_in = sem("weights_loaded")
        zeroed = sem("zeroed")
        id_done = sem("identity_done")
        a_exp = sem("a_exp")
        const_done = sem("constants_done")
        x_in = [sem(f"x_loaded{i}") for i in range(2)]
        ln_step = sem("ln_step")
        rs_done = sem("rs_done")
        xl_done = sem("xl_done")
        proj_full = sem("proj_full")
        proj_act = sem("proj_evacuated_act")
        halo = sem("halo_set")
        u_done = sem("u_done")
        silu_z = sem("silu_z_done")
        sp_step = sem("softplus_step")
        sp_log = sem("softplus_log")
        dl_done = sem("delta_done")
        b_out = sem("b_stored")
        bb_in = [sem(f"b_row_loaded{i}") for i in range(NB)]
        du_done = sem("du_done")
        exp_done = sem("exp_done")
        dbu_done = sem("dbu_done")
        scan_done = sem("scan_done")
        carry_done = sem("carry_done")
        tr_done = sem("states_turned")
        sum_done = sem("sum_done")
        post_full = sem("post_full")
        post_dve = sem("post_evacuated")
        gate_done = sem("gate_done")
        x1_out = [sem(f"x1_stored{i}") for i in range(2)]

        NW = 11
        LAG = 2
        USES = [("h", 0, 7), ("h", 1, 8), ("x", 0, 10), ("x", 1, 11), ("x", 2, 12), ("x", 3, 13),
                ("conv", 0, 14), ("conv", 1, 15), ("conv", 2, 16), ("conv", 3, 17), ("z", 0, 18), ("z", 1, 19),
                ("dbc", 0, 20), ("z", 2, 21), ("dt", 0, 22), ("dt", 1, 23), ("dt", 2, 24), ("dt", 3, 25),
                ("c", 0, 26), ("z", 3, 27)]
        U_ALL = len(USES)

        def nth(kind, g=0):
            return [u[:2] for u in USES].index((kind, g)) + 1

        block = ctx.enter_context(nc.Block())

        def iterations(eng, body):
            body(0, 0, True, False)
            body(1, 1, False, False)
            body(2, 0, False, False)
            with eng.Fori(1, (NC - 2) // 2) as i:
                body(i * 2 + 1, 1, False, False)
                body(i * 2 + 2, 0, False, False)
            body(NC - 1, 1, False, True)

        @block.sync
        def _(sync):
            def load_x(q, par):
                wait_apart(sync, passed, [(xl_done, 1, q, -1)])
                sync.dma_start(xb[:, par], x_t[q] if isinstance(q, int) else
                               x_t[bass.ds(q, 1)].rearrange("c p i d -> (c p) i d")).then_inc(x_in[par], 16)

            def store_b(q, par):
                wait(sync, proj_act, U_ALL, q, nth("dbc"))
                for s in range(NB):
                    wait(sync, bb_in[s], 16 * (N // NB), q, -16 * (N // NB))
                sync.dma_start(b_dram[par], dbc[R:R + N, :]).then_inc(b_out, 16)

            def load_row(c, par, n):
                if n == 0:
                    wait(sync, b_out, 16, c, 16)
                wait(sync, dbu_done, SG, c, (n - NB + 1) * G)
                sync.dma_start(bb[:, n % NB], b_dram[par, n, :].partition_broadcast(P)).then_inc(bb_in[n % NB], 16)

            def store_x1(q, par):
                wait_apart(sync, passed, [(post_dve, 6, q, 6)])
                sync.dma_start(x1_t[q] if isinstance(q, int) else
                               x1_t[bass.ds(q, 1)].rearrange("c p i d -> (c p) i d"), xl[:, par]
                               ).then_inc(x1_out[par], 16)

            load_x(0, 0)
            for dst, src in (
                (win[:], W_in.rearrange("(k p) n -> p k n", p=P)),
                (lng[:], ln_g.rearrange("(k p) -> p k", p=P)),
                (lnb[:], ln_b.rearrange("(k p) -> p k", p=P)),
                (cw[:], conv_w.rearrange("(g p) o k -> p g (o k)", p=P)),
                (cb[:], conv_b.rearrange("(g p) -> p g", p=P)),
                (wxp[:], W_xproj.rearrange("(g p) n -> p g n", p=P)),
                (wdt[0:R, :], W_dt),
                (wdt[K_DT - 1:K_DT, :], b_dt.rearrange("(a n) -> a n", a=1)),
                (a_neg[:], A_log.rearrange("(g p) n -> p g n", p=P)),
                (dp[:], D_param.rearrange("(g p) -> p g", p=P)),
                (wout[:], W_out.rearrange("(g p) n -> p g n", p=P)),
            ):
                with nc.allow_non_contiguous_dma(reason="small weights"):
                    sync.dma_start(dst, src).then_inc(w_in, 16)
            store_b(0, 0)

            def body(c, par, first, last):
                if not last:
                    load_x(c + 1, 1 - par)
                for n in range(N):
                    load_row(c, par, n)
                    if n == 5 and not first:
                        store_x1(c - 1, 1 - par)
                if not last:
                    store_b(c + 1, 1 - par)

            iterations(sync, body)
            store_x1(NC - 1, 1)
            for par in range(2):
                sync.wait_ge(x1_out[par], 16 * NC // 2)

        @block.vector
        def _(dve):
            dve.memset(ident[:], 1.0).then_inc(zeroed, 1)
            dve.memset(mhalf[:], -0.5).then_inc(zeroed, 1)
            dve.memset(wdt[R:R + 2 * N, :], 0.0).then_inc(zeroed, 1)
            dve.memset(dbc[K_DT - 1:K_DT, :], 1.0).then_inc(zeroed, 1)

            def stats(q, src, row):
                for i in range(NT):
                    ins = dve.bn_stats(st[:, row, i, :], src[:, i, :])
                ins.then_inc(ln_step, 1)
                wait_apart(dve, passed, [(ln_step, 6, q, 3 * row + 1)])
                for i in range(NT):
                    ins = dve.bn_aggr(mv[:, row, i, :], st[:, row, i, :])
                ins.then_inc(ln_step, 1)

            def normalise(q, src, dst, row):
                wait(dve, rs_done, 4, q, 2 * row + 2)
                for i in range(NT):
                    ins = dve.tensor_scalar(dst[:, i, :], src[:, i, :], mv[:, row, i, 0:1], rs[:, row, i:i + 1],
                                            ALU.subtract, ALU.mult)
                ins.then_inc(ln_step, 1)

            def norm_a(q, par):
                if isinstance(q, int):
                    dve.wait_ge(x_in[par], 16 * (q // 2 + 1))
                else:
                    wait(dve, x_in[par], 8, q, 8 if par else 16)
                stats(q, xb[:, par], 0)

            def norm_b(q, par):
                wait(dve, xl_done, 1, q, 0)
                normalise(q, xb[:, par], xn, 0)
                wait(dve, ln_step, 6, q, 3)
                stats(q, xn, 1)

            def norm_c(q, par):
                wait(dve, proj_full, U_ALL, q, nth("h", 1) - U_ALL)
                normalise(q, xn, h0, 1)

            def add_xl(q, par):
                if isinstance(q, int):
                    if q >= 2:
                        dve.wait_ge(x1_out[par], 16 * (q // 2))
                else:
                    wait(dve, x1_out[par], 8, q, -8 if par else 0)
                dve.tensor_tensor(xl[:, par], xb[:, par], xn[:], ALU.add).then_inc(xl_done, 1)

            def scans(c, par, n, groups):
                for g in groups:
                    k = n * G + g
                    wait(dve, exp_done, SG, c, k + 1)
                    wait(dve, dbu_done, SG, c, k + 1)
                    if g == 0:
                        wait(dve, tr_done, N * NT, c, (n - 1) * NT)
                        if par == 1 and n == 0:
                            wait(dve, carry_done, N // 2, c, N // 2)
                    init = carry[:, n, g:g + 1] if par else 0.0
                    dve.tensor_tensor_scan(ss[:, n % 2, g, :], ps_a[:, g, :], dbu[:, n % 2, g, :], init,
                                           ALU.mult, ALU.add).then_inc(scan_done, 1)

            def save(c, n):
                wait(dve, scan_done, SG, c, n * G + G)
                dve.tensor_copy(carry[:, n, :], ss[:, n % 2, :, CH - 1]).then_inc(carry_done, 1)

            def sums(c, par, n, tiles):
                for i in tiles:
                    k = n * NT + i
                    wait(dve, tr_done, N * NT, c, k + 1)
                    if n == 0:
                        if i == 0:
                            wait(dve, proj_act, U_ALL, c, nth("c"))
                            wait(dve, post_full, 6, c, -6)
                        dve.tensor_scalar(ya[:, par, i, :], ps_s[:, k % 2, :], cT[:, par, i, n:n + 1], None,
                                          ALU.mult).then_inc(sum_done, 1)
                    else:
                        wait(dve, sum_done, N * NT, c, k - NT + 1)
                        dve.scalar_tensor_tensor(ya[:, par, i, :], ps_s[:, k % 2, :], cT[:, par, i, n:n + 1],
                                                 ya[:, par, i, :], ALU.mult, ALU.add).then_inc(sum_done, 1)

            def skip_gate(q, par, g):
                wait(dve, post_full, 6, q, g + 1)
                if g == 0:
                    wait(dve, post_full, 6, q, 0)
                dve.scalar_tensor_tensor(yg[:, g, :], xc[:, par, g, :], dp[:, g:g + 1], ps_p[:, g % 2, :],
                                         ALU.mult, ALU.add).then_inc(post_dve, 1)

            def gate(q, par, g):
                wait(dve, post_dve, 6, q, g + 1)
                if g == 0:
                    wait(dve, silu_z, 1, q, 1)
                dve.tensor_tensor(yg[:, g, :], yg[:, g, :], zs[:, par, g, :], ALU.mult).then_inc(gate_done, 1)

            def residual(q, par, j):
                wait(dve, post_full, 6, q, 5 + j)
                wait(dve, xl_done, 1, q, 1)
                dve.tensor_tensor(xl[:, par, 2 * j:2 * j + 2, :],
                                  ps_p[:, j, :].rearrange("p (i d) -> p i d", d=D),
                                  xl[:, par, 2 * j:2 * j + 2, :], ALU.add).then_inc(post_dve, 1)

            dve.wait_ge(w_in, 16 * NW)
            dve.wait_ge(a_exp, 1)
            dve.wait_ge(id_done, 1)
            dve.tensor_scalar(a_neg[:], a_neg[:], -1.0, None, ALU.mult).then_inc(const_done, 1)
            for g in range(G):
                for k in range(TAPS):
                    ins = dve.tensor_scalar(taps[:, g, k, :], ident[:], cw[:, g, k:k + 1], None, ALU.mult)
            ins.then_inc(const_done, 1)
            norm_a(0, 0)
            norm_b(0, 0)
            norm_c(0, 0)
            add_xl(0, 0)

            def body(c, par, first, last):
                for s in range(2 * N):
                    n, tiles = s // 2, (0, 1) if s % 2 == 0 else (2, 3)
                    scans(c, par, n, tiles)
                    if n > 0:
                        sums(c, par, n - 1, tiles)
                    elif not first:
                        sums(c - 1, 1 - par, N - 1, tiles)
                    if par == 0 and s % 2:
                        save(c, n)
                    if not first:
                        if s in (2, 3):
                            for g in (2 * s - 4, 2 * s - 3):
                                skip_gate(c - 1, 1 - par, g)
                            for g in (2 * s - 4, 2 * s - 3):
                                gate(c - 1, 1 - par, g)
                        if s in (6, 7):
                            residual(c - 1, 1 - par, s - 6)
                    if not last:
                        if s == 0:
                            norm_a(c + 1, 1 - par)
                        if s == 2:
                            norm_b(c + 1, 1 - par)
                        if s == 4:
                            norm_c(c + 1, 1 - par)
                        if s == 10:
                            add_xl(c + 1, 1 - par)

            iterations(dve, body)
            sums(NC - 1, 1, N - 1, range(NT))
            for g in range(G):
                skip_gate(NC - 1, 1, g)
                gate(NC - 1, 1, g)
            residual(NC - 1, 1, 0)
            residual(NC - 1, 1, 1)

        @block.gpsimd
        def _(pool):
            pool.wait_ge(zeroed, 1)
            pool.affine_select(out=ident[:], in_=ident[:], compare_op=ALU.is_equal, fill=0.0, base=0,
                               pattern=[[-1, P]], channel_multiplier=1).then_inc(id_done, 1)

            def times_u(q, par, g):
                wait(pool, sp_log, G, q, g + 1)
                pool.tensor_tensor(dl[:, par, g, :], dl[:, par, g, :], sp[:, g, :], ALU.add).then_inc(dl_done, 1)
                wait(pool, dl_done, G, q, g + 1)
                pool.tensor_tensor(du[:, par, g, :], dl[:, par, g, :], xc[:, par, g, :], ALU.mult
                                   ).then_inc(du_done, 1)

            def times_b(c, par, n):
                wait(pool, bb_in[n % NB], 16 * (N // NB), c, 16 * (n // NB + 1))
                if n == 0:
                    wait(pool, du_done, G, c, G)
                for g in range(G):
                    wait(pool, scan_done, SG, c, (n - 2) * G + g + 1)
                    pool.tensor_tensor(dbu[:, n % 2, g, :], du[:, par, g, :], bb[:, n % NB, :], ALU.mult
                                       ).then_inc(dbu_done, 1)

            def inv_std(q, row):
                wait_apart(pool, passed, [(ln_step, 6, q, 3 * row + 2)])
                pool.tensor_scalar(ve[:, row, :], mv[:, row, :, 1], EPS, None, ALU.add).then_inc(rs_done, 1)
                wait(pool, rs_done, 4, q, 2 * row + 1)
                pool.tensor_tensor(rs[:, row, :], ve[:, row, :], mhalf[:], ALU.pow).then_inc(rs_done, 1)

            pool.wait_ge(zeroed, 4)
            inv_std(0, 0)
            inv_std(0, 1)
            for g in range(G):
                times_u(0, 0, g)

            def body(c, par, first, last):
                for n in range(N):
                    times_b(c, par, n)
                    if not last and n in (1, 2):
                        inv_std(c + 1, n - 1)
                    if not last and n >= N - 2:
                        for g in (2 * (n - N + 2), 2 * (n - N + 2) + 1):
                            times_u(c + 1, 1 - par, g)

            iterations(pool, body)

        @block.scalar
        def _(act):
            def set_halo(q, par):
                wait(act, proj_full, U_ALL, q, nth("conv", 3) - U_ALL)
                if par == 0:
                    act.memzero(xin[:, :, 0:HALO]).then_inc(halo, 1)
                else:
                    act.copy(xin[:, :, 0:HALO], xin[:, :, CH:CH + HALO]).then_inc(halo, 1)

            def empty(q, par, u):
                kind, g, _ = USES[u]
                wait(act, proj_full, U_ALL, q, u + 1)
                src = ps_p[:, u % 2, :]
                if kind == "h":
                    act.activation(hT[:, g, :], src, ACT.Identity, bias=lnb[:, g:g + 1], scale=lng[:, g:g + 1]
                                   ).then_inc(proj_act, 1)
                elif kind == "x":
                    if g == 0:
                        wait(act, halo, 1, q, 1)
                    act.copy(xin[:, g, HALO:], src).then_inc(proj_act, 1)
                elif kind == "z":
                    if g == 0:
                        wait(act, gate_done, G, q, -G)
                    act.copy(zs[:, par, g, :], src).then_inc(proj_act, 1)
                elif kind == "conv":
                    if g == 0:
                        wait(act, post_dve, 6, q, 4 - 12)
                        wait(act, du_done, G, q, -G)
                    act.activation(xc[:, par, g, :], src, ACT.Identity, bias=cb[:, g:g + 1]).then_inc(proj_act, 1)
                elif kind == "dbc":
                    wait(act, b_out, 16, q, 0)
                    act.copy(dbc[0:R + 2 * N, :], src[0:R + 2 * N, :]).then_inc(proj_act, 1)
                elif kind == "dt":
                    if g == 0:
                        wait(act, exp_done, SG, q, -SG)
                        wait(act, dl_done, G, q, 0)
                        wait(act, du_done, G, q, -G)
                    t = sp[:, g, :]
                    act.activation(dl[:, par, g, :], src, ACT.Relu).then_inc(sp_step, 1)
                    act.activation(t, src, ACT.Abs).then_inc(proj_act, 1)
                    wait(act, proj_act, U_ALL, q, u + 1)
                    act.activation(t, t, ACT.Exp, scale=-1.0).then_inc(sp_step, 1)
                    wait(act, sp_step, 2 * G, q, 2 * g + 2)
                    act.activation(t, t, ACT.Ln, bias=1.0).then_inc(sp_log, 1)
                else:
                    wait(act, sum_done, N * NT, q, -N * NT)
                    act.copy(cT[:, par], src[:, 0:NT * 96].rearrange("p (i n) -> p i n", n=96)[:, :, R + N:]
                             ).then_inc(proj_act, 1)

            def silu_u(q, par):
                wait(act, proj_act, U_ALL, q, nth("conv", 3))
                act.activation(xc[:, par], xc[:, par], ACT.Silu).then_inc(u_done, 1)

            def silu_gate(q, par):
                wait(act, proj_act, U_ALL, q, nth("z", 3))
                act.activation(zs[:, par], zs[:, par], ACT.Silu).then_inc(silu_z, 1)

            def exps(c, par, n, groups):
                for g in groups:
                    wait(act, scan_done, SG, c, (n - 1) * G + g + 1)
                    act.activation(ps_a[:, g, :], dl[:, par, g, :], ACT.Exp, scale=a_neg[:, g, n:n + 1]
                                   ).then_inc(exp_done, 1)

            act.wait_ge(w_in, 16 * NW)
            act.activation(a_neg[:], a_neg[:], ACT.Exp).then_inc(a_exp, 1)
            act.wait_ge(const_done, 1)
            set_halo(0, 0)
            for u, (kind, g, _) in enumerate(USES):
                empty(0, 0, u)
                if (kind, g) == ("conv", 3):
                    silu_u(0, 0)

            def pieces(c, par, first, last, s):
                for u, (kind, g, at) in enumerate(USES):
                    if at + LAG != s:
                        continue
                    if not last:
                        if u == 0:
                            set_halo(c + 1, 1 - par)
                        empty(c + 1, 1 - par, u)
                    if (kind, g) == ("conv", 3):
                        if not last:
                            silu_u(c + 1, 1 - par)
                        silu_gate(c, par)

            def body(c, par, first, last):
                for n in range(N):
                    if n == 0:
                        wait(act, dl_done, G, c, G)
                    for half in range(2):
                        pieces(c, par, first, last, 2 * n + half)
                        exps(c, par, n, (2 * half, 2 * half + 1))

            iterations(act, body)

        @block.tensor
        def _(pe):
            def project(q, par, u, after_post=True):
                kind, g, _ = USES[u]
                if u >= 2 or not after_post:
                    wait(pe, proj_act, U_ALL, q, u - 1)
                else:
                    wait(pe, post_dve, 6, q, 5 + u - 12)
                dst = ps_p[:, u % 2, :]
                if kind == "h":
                    if g == 0:
                        wait(pe, ln_step, 6, q, 6)
                    for i in range(NT):
                        ins = pe.transpose(dst[:, i * P:(i + 1) * P], h0[:, i, g * P:(g + 1) * P], ident[:])
                elif kind in "xz":
                    if (kind, g) == ("x", 0):
                        wait(pe, proj_act, U_ALL, q, nth("h", 1))
                    m = g * P + (DI if kind == "z" else 0)
                    for k in range(KD):
                        ins = pe.matmul(dst, win[:, k, m:m + P], hT[:, k, :], start=(k == 0), stop=(k == KD - 1))
                elif kind == "conv":
                    wait(pe, proj_act, U_ALL, q, nth("x", g))
                    for k in range(TAPS):
                        ins = pe.matmul(dst, taps[:, g, k, :], xin[:, g, k:k + CH],
                                        start=(k == 0), stop=(k == TAPS - 1))
                elif kind == "dbc":
                    wait(pe, u_done, 1, q, 1)
                    for k in range(G):
                        ins = pe.matmul(dst[0:96, :], wxp[:, k, :], xc[:, par, k, :],
                                        start=(k == 0), stop=(k == G - 1))
                elif kind == "dt":
                    if g == 0:
                        wait(pe, proj_act, U_ALL, q, nth("dbc"))
                    ins = pe.matmul(dst, wdt[:, g * P:(g + 1) * P], dbc[:], start=True, stop=True)
                else:
                    for i in range(NT):
                        ins = pe.transpose(dst[:, i * 96:(i + 1) * 96], dbc[0:96, i * P:(i + 1) * P],
                                           ident[0:96, 0:96])
                ins.then_inc(proj_full, 1)

            def turn(c, par, n, tiles):
                if 0 in tiles:
                    wait(pe, scan_done, SG, c, n * G + G)
                for i in tiles:
                    k = n * NT + i
                    wait(pe, sum_done, N * NT, c, k - 1)
                    for g in range(G):
                        ins = pe.transpose(ps_s[:, k % 2, g * P:(g + 1) * P], ss[:, n % 2, g, i * P:(i + 1) * P],
                                           ident[:])
                    ins.then_inc(tr_done, 1)

            def turn_back(q, par, g, proj_between):
                if g == 0:
                    wait(pe, sum_done, N * NT, q, N * NT)
                if g >= 2:
                    wait(pe, post_dve, 6, q, g - 1)
                elif proj_between:
                    wait(pe, proj_act, U_ALL, q, 2 * U_ALL - 1 + g)
                else:
                    wait(pe, post_dve, 6, q, g - 1)
                for i in range(NT):
                    ins = pe.transpose(ps_p[:, g % 2, i * P:(i + 1) * P], ya[:, par, i, g * P:(g + 1) * P], ident[:])
                ins.then_inc(post_full, 1)

            def project_out(q, par, j):
                wait(pe, post_dve, 6, q, 3 + j)
                if j == 0:
                    wait(pe, gate_done, G, q, G)
                for i in (2 * j, 2 * j + 1):
                    for g in range(G):
                        ins = pe.matmul(ps_p[:, j, (i % 2) * D:(i % 2 + 1) * D], yg[:, g, i * P:(i + 1) * P],
                                        wout[:, g, :], start=(g == 0), stop=(g == G - 1))
                ins.then_inc(post_full, 1)

            pe.wait_ge(w_in, 16 * NW)
            pe.wait_ge(zeroed, 4)
            pe.wait_ge(id_done, 1)
            pe.wait_ge(const_done, 2)
            for u in range(U_ALL):
                project(0, 0, u, False)

            def body(c, par, first, last):
                for s in range(2 * N):
                    if not first and s in (1, 2):
                        turn_back(c - 1, 1 - par, 2 * s - 2, True)
                        turn_back(c - 1, 1 - par, 2 * s - 1, True)
                    if not first and s in (4, 5):
                        project_out(c - 1, 1 - par, s - 4)
                    if not last:
                        for u, (_, _, at) in enumerate(USES):
                            if at == s:
                                project(c + 1, 1 - par, u, not first)
                    turn(c, par, s // 2, (0, 1) if s % 2 == 0 else (2, 3))

            iterations(pe, body)
            for g in range(G):
                turn_back(NC - 1, 1, g, False)
            for j in range(2):
                project_out(NC - 1, 1, j)


def wait_slot(eng, sem, c, par, more=0):
    if isinstance(c, int):
        v = 16 * (c // 2 + 1 + more)
        if v > 0:
            eng.wait_ge(sem, v)
    else:
        wait(eng, sem, 8, c, (8 if par else 16) + 16 * more)


def rows_of(t, c):
    return t[c] if isinstance(c, int) else t[bass.ds(c, 1)].rearrange("c p i d -> (c p) i d")


def route_block(nc, x1_t, xf_t, xs_dram, zero_dram, tab, slots_dram, w_dram, Wg, bg, NC, D, KD, E, REG, NTT):
    KR = 21
    KT = 23
    SC = 8
    with ExitStack() as ctx:
        def sb(name, shape, dt=F32):
            return ctx.enter_context(nc.sbuf_tensor(name, shape, dt))

        def sem(name):
            return ctx.enter_context(nc.semaphore(name))

        ident = sb("r_ident", [P, P])
        below = sb("below", [P, P])
        ones = sb("ones", [P, P])
        wg = sb("wg", [P, KD, E])
        bgb = sb("bgb", [P, E])
        first = sb("first", [P, NT, E])
        run = sb("run", [P, E])
        mhalf = sb("r_mhalf", [P, NT])
        zero = sb("zero", [P, D])
        x1 = sb("r_x1", [P, 2, NT, D])
        xn = sb("r_xn", [P, 2, NT, D])
        xT = sb("r_xT", [P, KD, CH])
        st = sb("r_st", [P, NT, 6])
        mv = sb("r_mv", [P, NT, 2])
        ve = sb("r_ve", [P, NT])
        rs = sb("r_rs", [P, NT])
        lg = sb("lg", [P, NT, E])
        eq = sb("eq", [P, NT, E])
        cn = sb("cn", [P, NT, E])
        sel = sb("sel", [P, 2, NT, E])
        both = sb("both", [P, NT, E])
        mx = sb("mx", [P, 2, NT])
        ex = sb("ex", [P, NT])
        wt = sb("wt", [P, 2, 2, NT])
        slot = sb("slot", [P, NT, E])
        pick = sb("pick", [P, 2, NT, E])
        slf = sb("slf", [P, 2, NT])
        sli = sb("sli", [P, 2, 2, NT], U32)
        sla = sb("sla", [P, NC, 2 * NT])
        reg = sb("reg", [P, E])
        move = sb("move", [P, E])
        dmove = sb("dmove", [P, E])
        part = sb("part", [P, 2 * NT * NC, E])
        shift = sb("shift", [P, NC, 2 * NT])
        slp = sb("slp", [P, NC, 2 * NT], U32)
        ps_x = ctx.enter_context(nc.psum_tensor("r_ps_x", [P, KD, CH], F32))
        ps_l = ctx.enter_context(nc.psum_tensor("r_ps_l", [P, CH], F32))
        ps_r = ctx.enter_context(nc.psum_tensor("r_ps_r", [P, CH], F32))
        ps_t = ctx.enter_context(nc.psum_tensor("r_ps_t", [P, CH], F32))
        ji = sb("ji", [P, B_TILES], I32)
        jf = sb("jf", [P, B_TILES])
        over = sb("over", [P, E, B_TILES])
        cnt = sb("cnt", [P, E])
        base = sb("base", [P, E])
        nt = sb("nt", [P, E])
        end = sb("end", [P, E])
        skip = sb("skip", [P, E])
        ti = sb("ti", [P, NTT], I32)
        tf = sb("tf", [P, NTT])
        cmp = sb("cmp", [P, NTT, E])
        wcmp = sb("wcmp", [P, NTT, E])
        eid = sb("eid", [P, NTT])
        row = sb("row", [P, NTT])
        tabi = sb("tabi", [P, 2, NTT], I32)
        padf = sb("padf", [P, E])
        padi = sb("padi", [P, E], U32)
        pf = sb("pf", [P, 1])
        pi = sb("pi", [P, 1], I32)

        passed = sem("r_passed")
        w_in = sem("r_weights_loaded")
        made = sem("r_masks_made")
        mem = sem("r_memsets")
        x_in = [sem(f"r_x1_loaded{i}") for i in range(2)]
        xn_out = [sem(f"xf_stored{i}") for i in range(2)]
        sl_out = [sem(f"slots_stored{i}") for i in range(2)]
        scat = [sem(f"rows_scattered{i}") for i in range(2)]
        zero_out = sem("zero_rows_stored")
        stat = sem("r_stats")
        rs_done = sem("r_rs")
        xn_done = sem("xn_done")
        turned = sem("r_turned")
        copied = sem("r_copied")
        logit = sem("logits_done")
        step = sem("route_step")
        e_done = sem("e_done")
        ranked = sem("ranked")
        tabs = sem("table_step")
        tab_out = sem("table_stored")

        block = ctx.enter_context(nc.Block())

        def chunks(eng, body):
            for c in range(4):
                body(c, c % 2)
            with eng.Fori(2, NC // 2) as i:
                body(i * 2, 0)
                body(i * 2 + 1, 1)

        @block.sync
        def _(sync):
            with nc.allow_non_contiguous_dma(reason="small weights"):
                sync.dma_start(wg[:], Wg.rearrange("(k p) e -> p k e", p=P)).then_inc(w_in, 16)
                sync.dma_start(bgb[:], bg.partition_broadcast(P)).then_inc(w_in, 16)
            sync.wait_ge(mem, 5)
            for i in range(zero_dram.shape[0] // P):
                sync.dma_start(zero_dram[i * P:(i + 1) * P, :], zero[:]).then_inc(zero_out, 16)

            def body(c, par):
                wait_apart(sync, passed, [(xn_done, 1, c, -1)])
                sync.dma_start(x1[:, par], rows_of(x1_t, c)).then_inc(x_in[par], 16)
                wait_apart(sync, passed, [(xn_done, 1, c, 1)])
                sync.dma_start(rows_of(xf_t, c), xn[:, par]).then_inc(xn_out[par], 16)
                wait_apart(sync, passed, [(step, KR, c, KR)])
                sync.dma_start(rows_of(w_dram, c), wt[:, par]).then_inc(sl_out[par], 16)

            chunks(sync, body)
            sync.wait_ge(zero_out, 16 * (zero_dram.shape[0] // P))
            for par in range(2):
                sync.wait_ge(xn_out[par], 16 * NC // 2)
                sync.wait_ge(sl_out[par], 16 * NC // 2)
            sync.wait_ge(tabs, KT)
            sync.dma_start(tab, tabi[0:1]).then_inc(tab_out, 16)
            sync.dma_start(slots_dram.rearrange("c p k i -> p c (k i)"), slp[:]).then_inc(tab_out, 16)
            sync.wait_ge(tab_out, 32)

        @block.vector
        def _(dve):
            dve.memset(ident[:], 1.0).then_inc(mem, 1)
            dve.memset(below[:], 1.0).then_inc(mem, 1)
            dve.memset(ones[:], 1.0).then_inc(mem, 1)
            dve.memset(mhalf[:], -0.5).then_inc(mem, 1)
            dve.memset(zero[:], 0.0).then_inc(mem, 1)
            dve.memset(first[:], 1.0).then_inc(mem, 1)
            dve.wait_ge(mem, 6)
            dve.memset(first[:, :, 0], 0.0).then_inc(mem, 1)
            for e in range(E):
                dve.memset(run[:, e:e + 1], float(e * REG)).then_inc(mem, 1)
                dve.memset(reg[:, e:e + 1], float(e * REG)).then_inc(mem, 1)
            dve.wait_ge(mem, 7 + 2 * E)
            dve.wait_ge(w_in, 32)

            def body(c, par):
                wait_slot(dve, x_in[par], c, par)
                for i in range(NT):
                    ins = dve.bn_stats(st[:, i, :], x1[:, par, i, :])
                ins.then_inc(stat, 1)
                wait_apart(dve, passed, [(stat, 2, c, 1)])
                for i in range(NT):
                    ins = dve.bn_aggr(mv[:, i, :], st[:, i, :])
                ins.then_inc(stat, 1)
                wait(dve, rs_done, 2, c, 2)
                wait_slot(dve, xn_out[par], c, par, -1)
                if isinstance(c, int):
                    if c >= 2:
                        dve.wait_ge(scat[par], 16 * SC * (c // 2))
                else:
                    wait(dve, scat[par], 8 * SC, c, -8 * SC if par else 0)
                for i in range(NT):
                    ins = dve.tensor_scalar(xn[:, par, i, :], x1[:, par, i, :], mv[:, i, 0:1], rs[:, i:i + 1],
                                            ALU.subtract, ALU.mult)
                ins.then_inc(xn_done, 1)

                count = [0]

                def link(ins):
                    count[0] += 1
                    ins.then_inc(step, 1)
                    wait(dve, step, KR, c, count[0])

                wait(dve, logit, 1, c, 1)
                link(dve.tensor_tensor(lg[:], ps_l[:, 0:NT * E].rearrange("p (i e) -> p i e", e=E),
                                       bgb[:].unsqueeze(1).broadcast_to([P, NT, E]), ALU.add))
                for k in range(2):
                    link(dve.tensor_reduce(mx[:, k, :], lg[:], AX.X, ALU.max))
                    link(dve.tensor_tensor(eq[:], lg[:], mx[:, k, :].unsqueeze(2).broadcast_to([P, NT, E]),
                                           ALU.is_equal))
                    link(dve.tensor_tensor_scan(cn[:].rearrange("p i e -> p (i e)"),
                                                first[:].rearrange("p i e -> p (i e)"),
                                                eq[:].rearrange("p i e -> p (i e)"), 0.0, ALU.mult, ALU.add))
                    link(dve.scalar_tensor_tensor(sel[:, k], cn[:], 1.0, eq[:], ALU.is_equal, ALU.mult))
                    if k == 0:
                        link(dve.scalar_tensor_tensor(lg[:], sel[:, 0], -3e38, lg[:], ALU.mult, ALU.add))
                link(dve.tensor_tensor(both[:], sel[:, 0], sel[:, 1], ALU.add))
                assert count[0] == 11
                link(dve.tensor_tensor(ex[:], mx[:, 1, :], mx[:, 0, :], ALU.subtract))
                wait(dve, e_done, 1, c, 1)
                link(dve.tensor_scalar(ve[:], ex[:], 1.0, None, ALU.add))
                if isinstance(c, int):
                    if c >= 2:
                        dve.wait_ge(sl_out[par], 16 * (c // 2))
                else:
                    wait(dve, sl_out[par], 8, c, -8 if par else 0)
                link(dve.reciprocal(wt[:, par, 0, :], ve[:]))
                link(dve.tensor_tensor(wt[:, par, 1, :], wt[:, par, 0, :], ex[:], ALU.mult))
                wait(dve, ranked, 1, c, 1)
                link(dve.tensor_tensor(slot[:], ps_r[:, 0:NT * E].rearrange("p (i e) -> p i e", e=E),
                                       run[:].unsqueeze(1).broadcast_to([P, NT, E]), ALU.add))
                link(dve.tensor_tensor(run[:], ps_t[:, 0:E], run[:], ALU.add))
                for k in range(2):
                    ins = dve.tensor_tensor(pick[:, k], sel[:, k], slot[:], ALU.mult)
                link(ins)
                for k in range(2):
                    ins = dve.tensor_reduce(slf[:, k, :], pick[:, k], AX.X, ALU.add)
                link(ins)
                link(dve.tensor_copy(sli[:, par], slf[:]))
                link(dve.tensor_copy(sla[:, c, :] if isinstance(c, int) else
                                     sla[:, bass.ds(c, 1), :].rearrange("p c k -> p (c k)"),
                                     slf[:].rearrange("p k i -> p (k i)")))
                assert count[0] == KR, count

            chunks(dve, body)

            count = [0]

            def link(ins):
                count[0] += 1
                ins.then_inc(tabs, 1)
                dve.wait_ge(tabs, count[0])

            dve.wait_ge(made, 6)
            link(dve.tensor_copy(jf[:], ji[:]))
            link(dve.tensor_copy(tf[:], ti[:]))
            link(dve.tensor_copy(pf[:], pi[:]))
            link(dve.tensor_scalar(padf[:], run[:], pf[:], None, ALU.add))
            link(dve.tensor_copy(padi[:], padf[:]))
            link(dve.tensor_tensor(cnt[:], run[:], reg[:], ALU.subtract))
            link(dve.tensor_tensor(over[:], cnt[:].unsqueeze(2).broadcast_to([P, E, B_TILES]),
                                   jf[:].unsqueeze(1).broadcast_to([P, E, B_TILES]), ALU.is_gt))
            link(dve.tensor_reduce(nt[:], over[:], AX.X, ALU.add))
            link(dve.tensor_tensor_scan(end[:], ones[:, 0:E], nt[:], 0.0, ALU.mult, ALU.add))
            link(dve.tensor_scalar(skip[:], nt[:], float(-P), float(REG), ALU.mult, ALU.add))
            link(dve.tensor_tensor(cmp[:], end[:].unsqueeze(1).broadcast_to([P, NTT, E]),
                                   tf[:].unsqueeze(2).broadcast_to([P, NTT, E]), ALU.is_le))
            link(dve.tensor_reduce(eid[:], cmp[:], AX.X, ALU.add))
            link(dve.tensor_tensor(wcmp[:], cmp[:], skip[:].unsqueeze(1).broadcast_to([P, NTT, E]), ALU.mult))
            link(dve.tensor_reduce(row[:], wcmp[:], AX.X, ALU.add))
            link(dve.tensor_scalar(tabi[:, 1, :], eid[:], float(E - 1), None, ALU.min))
            link(dve.scalar_tensor_tensor(tabi[:, 0, :], tf[:], float(P), row[:], ALU.mult, ALU.add))
            link(dve.tensor_tensor(move[:], end[:], nt[:], ALU.subtract))
            link(dve.scalar_tensor_tensor(move[:], move[:], float(P), reg[:], ALU.mult, ALU.subtract))
            dve.tensor_copy(dmove[:, 0:1], move[:, 0:1])
            link(dve.tensor_tensor(dmove[:, 1:E], move[:, 1:E], move[:, 0:E - 1], ALU.subtract))
            slots = sla[:].rearrange("p c k -> p (c k)")
            full = [P, 2 * NT * NC, E]
            link(dve.tensor_tensor(part[:], slots.unsqueeze(2).broadcast_to(full),
                                   reg[:].unsqueeze(1).broadcast_to(full), ALU.is_ge))
            link(dve.tensor_tensor(part[:], part[:], dmove[:].unsqueeze(1).broadcast_to(full), ALU.mult))
            link(dve.tensor_reduce(shift[:].rearrange("p c k -> p (c k)"), part[:], AX.X, ALU.add))
            dve.tensor_tensor(slp[:], sla[:], shift[:], ALU.add).then_inc(tabs, 1)
            assert count[0] + 1 == KT

        @block.gpsimd
        def _(pool):
            pool.wait_ge(mem, 2)
            pool.affine_select(out=ident[:], in_=ident[:], compare_op=ALU.is_equal, fill=0.0, base=0,
                               pattern=[[-1, P]], channel_multiplier=1).then_inc(made, 1)
            pool.affine_select(out=below[:], in_=below[:], compare_op=ALU.is_ge, fill=0.0, base=-1,
                               pattern=[[1, P]], channel_multiplier=-1).then_inc(made, 1)
            pool.iota(ji[:], pattern=[[P, B_TILES]], base=0, channel_multiplier=0).then_inc(made, 1)
            pool.iota(ti[:], pattern=[[1, NTT]], base=0, channel_multiplier=0).then_inc(made, 1)
            pool.iota(pi[:], pattern=[[0, 1]], base=0, channel_multiplier=1).then_inc(made, 1)
            pool.wait_ge(mem, 7 + 2 * E)
            pool.engine_nop().then_inc(made, 1)

            def body(c, par):
                wait_apart(pool, passed, [(stat, 2, c, 2)])
                pool.tensor_scalar(ve[:], mv[:, :, 1], EPS, None, ALU.add).then_inc(rs_done, 1)
                wait(pool, rs_done, 2, c, 1)
                pool.tensor_tensor(rs[:], ve[:], mhalf[:], ALU.pow).then_inc(rs_done, 1)
                wait_apart(pool, passed, [(step, KR, c, KR)])
                for i in range(NT):
                    for k in range(2):
                        pool.indirect_dma_start(
                            out=xs_dram, out_offset=bass.IndirectOffsetOnAxis(ap=sli[:, par, k, i:i + 1], axis=0),
                            in_=xn[:, par, i, :], in_offset=None).then_inc(scat[par], 16)

            chunks(pool, body)
            pool.wait_ge(tabs, 5)
            for e in range(E):
                pool.indirect_dma_start(
                    out=xs_dram, out_offset=bass.IndirectOffsetOnAxis(ap=padi[:, e:e + 1], axis=0),
                    in_=zero[:], in_offset=None).then_inc(scat[0], 16)
            pool.wait_ge(scat[0], 16 * (SC * NC // 2 + E))
            pool.wait_ge(scat[1], 16 * SC * NC // 2)

        @block.scalar
        def _(act):
            def body(c, par):
                for k in range(KD):
                    wait(act, turned, KD, c, k + 1)
                    if k == 0:
                        wait(act, logit, 1, c, 0)
                    act.copy(xT[:, k, :], ps_x[:, k, :]).then_inc(copied, 1)
                wait(act, step, KR, c, 12)
                act.activation(ex[:], ex[:], ACT.Exp).then_inc(e_done, 1)

            chunks(act, body)

        @block.tensor
        def _(pe):
            pe.wait_ge(w_in, 32)
            pe.wait_ge(made, 2)
            pe.wait_ge(mem, 3)

            def body(c, par):
                wait(pe, xn_done, 1, c, 1)
                for k in range(KD):
                    wait(pe, copied, KD, c, k + 1 - KD)
                    for i in range(NT):
                        ins = pe.transpose(ps_x[:, k, i * P:(i + 1) * P], xn[:, par, i, k * P:(k + 1) * P], ident[:])
                    ins.then_inc(turned, 1)
                wait(pe, copied, KD, c, KD)
                wait(pe, step, KR, c, 1 - KR)
                for i in range(NT):
                    for k in range(KD):
                        ins = pe.matmul(ps_l[:, i * E:(i + 1) * E], xT[:, k, i * P:(i + 1) * P], wg[:, k, :],
                                        start=(k == 0), stop=(k == KD - 1))
                ins.then_inc(logit, 1)
                wait(pe, step, KR, c, 11)
                pe.matmul(ps_r[:, 0:NT * E], below[:], both[:].rearrange("p i e -> p (i e)"), start=True, stop=False)
                for d in range(1, NT):
                    pe.matmul(ps_r[:, d * E:NT * E], ones[:],
                              both[:, 0:NT - d, :].rearrange("p i e -> p (i e)"), start=False, stop=(d == NT - 1))
                for i in range(NT):
                    ins = pe.matmul(ps_t[:, 0:E], ones[:], both[:, i, :], start=(i == 0), stop=(i == NT - 1))
                ins.then_inc(ranked, 1)

            chunks(pe, body)


def experts_block(nc, xs_dram, eo_dram, tab, W1, b1, W2, b2, D, KD, E, F, REG, NTT):
    KF = F // P
    with ExitStack() as ctx:
        def sb(name, shape, dt=F32):
            return ctx.enter_context(nc.sbuf_tensor(name, shape, dt))

        def sem(name):
            return ctx.enter_context(nc.semaphore(name))

        ident = sb("e_ident", [P, P])
        w1 = sb("w1", [P, KD, E * F])
        w2 = sb("w2", [P, E * KF * D])
        b1b = sb("b1b", [P, E * F])
        b2b = sb("b2b", [P, E * D])
        tabs = sb("tabs", [1, 2 * NTT], I32)
        xt = sb("xt", [P, 2, D])
        xT = sb("xT", [P, 2, KD * P])
        hb = sb("hb", [P, 2, F])
        hT = sb("hT2", [P, 2, F])
        ot = sb("ot", [P, 2, D])
        ps_x = ctx.enter_context(nc.psum_tensor("e_ps_x", [P, 2, CH], F32))
        ps_h = ctx.enter_context(nc.psum_tensor("e_ps_h", [P, 2, F], F32))
        ps_t = ctx.enter_context(nc.psum_tensor("e_ps_t", [P, 2, F], F32))
        ps_o = ctx.enter_context(nc.psum_tensor("e_ps_o", [P, 2, CH], F32))

        passed = sem("e_passed")
        w_in = sem("e_weights_loaded")
        made = sem("e_ident_made")
        x_in = [sem(f"rows_loaded{i}") for i in range(2)]
        o_out = [sem(f"rows_stored{i}") for i in range(2)]
        x_turned = sem("x_turned")
        x_copied = sem("x_copied")
        h_full = sem("h_full")
        h_done = sem("h_done")
        h_turned = sem("h_turned")
        h_relu = sem("h_relu")
        o_full = sem("o_full")
        o_done = sem("o_done")
        NW = 4 + KD

        block = ctx.enter_context(nc.Block())

        def steps(eng, body, lag):
            for s in range(lag + 2):
                body(s, s % 2)
            n = NTT - lag - 2
            assert n % 2 == 0
            with eng.Fori(0, n // 2) as i:
                body(i * 2 + lag + 2, lag % 2)
                body(i * 2 + lag + 3, (lag + 1) % 2)
            for s in range(NTT, NTT + lag):
                body(s, s % 2)

        def real(t):
            return not isinstance(t, int) or 0 <= t < NTT

        def tile_loaded(eng, sem, t, par, more=0):
            wait_slot(eng, sem, t, par, more)

        @block.sync
        def _(sync):
            sync.dma_start(tabs[:], tab.rearrange("a k n -> a (k n)")).then_inc(w_in, 16)
            for k in range(KD):
                sync.dma_start(w1[:, k, :].rearrange("p (e f) -> p e f", e=E),
                               W1[:, k * P:(k + 1) * P, :].rearrange("e p f -> p e f")).then_inc(w_in, 16)
            sync.dma_start(w2[:].rearrange("p (e k d) -> p e k d", e=E, k=KF),
                           W2.rearrange("e (k p) d -> p e k d", p=P)).then_inc(w_in, 16)
            sync.dma_start(b1b[:], b1.rearrange("e f -> (e f)").partition_broadcast(P)).then_inc(w_in, 16)
            sync.dma_start(b2b[:], b2.rearrange("e d -> (e d)").partition_broadcast(P)).then_inc(w_in, 16)
            sync.wait_ge(w_in, 16 * NW)

            def body(t, par):
                off = sync.value_load(tabs[0:1, bass.ds(t, 1)], min_val=0, max_val=xs_dram.shape[0] - P)
                wait_apart(sync, passed, [(x_turned, 1, t, -1)])
                sync.dma_start(xt[:, par, :], xs_dram[bass.ds(off, P), :]).then_inc(x_in[par], 16)

            steps(sync, lambda s, par: body(s, par) if real(s) else None, 3)

        @block.scalar
        def _(act):
            act.wait_ge(w_in, 16 * NW)

            def body(s, par):
                if real(s):
                    wait(act, x_turned, 1, s, 1)
                    wait(act, h_full, 1, s, -1)
                    act.copy(xT[:, par, :], ps_x[:, par, 0:KD * P]).then_inc(x_copied, 1)
                if real(s - 2):
                    t = s - 2
                    wait(act, h_turned, 1, t, 1)
                    wait(act, o_full, 1, t, -1)
                    act.activation(hT[:, par, :], ps_t[:, par, :], ACT.Relu).then_inc(h_relu, 1)
                if real(s - 3):
                    t = s - 3
                    wait(act, o_done, 1, t, 1)
                    act.dma_start(eo_dram[t * P:(t + 1) * P, :] if isinstance(t, int) else
                                  eo_dram[bass.ds(t * P, P), :], ot[:, 1 - par, :]).then_inc(o_out[1 - par], 16)

            steps(act, body, 3)
            act.wait_ge(o_out[0], 16 * ((NTT + 1) // 2))
            act.wait_ge(o_out[1], 16 * (NTT // 2))

        @block.vector
        def _(dve):
            dve.memset(ident[:], 1.0).then_inc(made, 1)
            dve.wait_ge(w_in, 16 * NW)

            def body(s, par):
                if real(s - 1):
                    t = s - 1
                    wait(dve, h_full, 1, t, 1)
                    wait(dve, h_turned, 1, t, -1)
                    e = dve.value_load(tabs[0:1, bass.ds(t + NTT, 1)], min_val=0, max_val=E - 1)
                    dve.tensor_tensor(hb[:, 1 - par, :], ps_h[:, 1 - par, :], b1b[:, bass.ds(e * F, F)], ALU.add
                                      ).then_inc(h_done, 1)
                if real(s - 3):
                    t = s - 3
                    wait(dve, o_full, 1, t, 1)
                    wait_slot(dve, o_out[1 - par], t, 1 - par, -1)
                    e = dve.value_load(tabs[0:1, bass.ds(t + NTT, 1)], min_val=0, max_val=E - 1)
                    dve.tensor_tensor(ot[:, 1 - par, :], ps_o[:, 1 - par, 0:D], b2b[:, bass.ds(e * D, D)], ALU.add
                                      ).then_inc(o_done, 1)

            steps(dve, body, 3)

        @block.gpsimd
        def _(pool):
            pool.wait_ge(made, 1)
            pool.affine_select(out=ident[:], in_=ident[:], compare_op=ALU.is_equal, fill=0.0, base=0,
                               pattern=[[-1, P]], channel_multiplier=1).then_inc(made, 1)

        @block.tensor
        def _(pe):
            pe.wait_ge(made, 2)
            pe.wait_ge(w_in, 16 * NW)

            def body(s, par):
                if real(s):
                    wait_slot(pe, x_in[par], s, par)
                    wait(pe, x_copied, 1, s, -1)
                    for k in range(KD):
                        ins = pe.transpose(ps_x[:, par, k * P:(k + 1) * P], xt[:, par, k * P:(k + 1) * P], ident[:])
                    ins.then_inc(x_turned, 1)
                if real(s - 1):
                    t = s - 1
                    wait(pe, x_copied, 1, t, 1)
                    wait(pe, h_done, 1, t, -1)
                    e = pe.value_load(tabs[0:1, bass.ds(t + NTT, 1)], min_val=0, max_val=E - 1)
                    for k in range(KD):
                        ins = pe.matmul(ps_h[:, 1 - par, :], xT[:, 1 - par, k * P:(k + 1) * P],
                                        w1[:, k, bass.ds(e * F, F)], start=(k == 0), stop=(k == KD - 1))
                    ins.then_inc(h_full, 1)
                if real(s - 2):
                    t = s - 2
                    wait(pe, h_done, 1, t, 1)
                    wait(pe, h_relu, 1, t, -1)
                    for k in range(KF):
                        ins = pe.transpose(ps_t[:, par, k * P:(k + 1) * P], hb[:, par, k * P:(k + 1) * P], ident[:])
                    ins.then_inc(h_turned, 1)
                if real(s - 3):
                    t = s - 3
                    wait(pe, h_relu, 1, t, 1)
                    wait(pe, o_done, 1, t, -1)
                    e = pe.value_load(tabs[0:1, bass.ds(t + NTT, 1)], min_val=0, max_val=E - 1)
                    for k in range(KF):
                        ins = pe.matmul(ps_o[:, 1 - par, 0:D], hT[:, 1 - par, k * P:(k + 1) * P],
                                        w2[:, bass.ds((e * KF + k) * D, D)], start=(k == 0), stop=(k == KF - 1))
                    ins.then_inc(o_full, 1)

            steps(pe, body, 3)


def combine_block(nc, x1_t, xf_t, eo_dram, slots_dram, w_dram, gamma, beta, out_t, NC, D):
    with ExitStack() as ctx:
        def sb(name, shape, dt=F32):
            return ctx.enter_context(nc.sbuf_tensor(name, shape, dt))

        def sem(name):
            return ctx.enter_context(nc.semaphore(name))

        gm = sb("gm", [P, D])
        bt = sb("bt", [P, D])
        mhalf = sb("c_mhalf", [P, NT])
        x1 = sb("c_x1", [P, 2, NT, D])
        xf = sb("c_xf", [P, 2, NT, D])
        si = sb("c_si", [P, 2, 2, NT], U32)
        wt = sb("c_wt", [P, 2, 2, NT])
        ge = sb("ge", [P, 2, 2, NT, D])
        st = sb("c_st", [P, NT, 6])
        mv = sb("c_mv", [P, NT, 2])
        ve = sb("c_ve", [P, NT])
        rs = sb("c_rs", [P, NT])

        passed = sem("c_passed")
        w_in = sem("c_weights_loaded")
        mem = sem("c_memset")
        x_in = [sem(f"c_loaded{i}") for i in range(2)]
        g_in = [sem(f"gathered{i}") for i in range(2)]
        o_out = [sem(f"c_stored{i}") for i in range(2)]
        mixed = sem("mixed")
        stat = sem("c_stats")
        rs_done = sem("c_rs_done")
        scaled = sem("scaled")
        biased = sem("biased")
        done = sem("c_done")
        LD = 4

        block = ctx.enter_context(nc.Block())

        def chunks(eng, body):
            for c in range(4):
                body(c, c % 2)
            with eng.Fori(2, NC // 2) as i:
                body(i * 2, 0)
                body(i * 2 + 1, 1)

        def wait_loads(eng, sem, c, par, per, more=0):
            if isinstance(c, int):
                if c // 2 + 1 + more > 0:
                    eng.wait_ge(sem, 16 * per * (c // 2 + 1 + more))
            else:
                wait(eng, sem, 8 * per, c, (8 * per if par else 16 * per) + 16 * per * more)

        @block.sync
        def _(sync):
            sync.dma_start(gm[:], gamma.partition_broadcast(P)).then_inc(w_in, 16)
            sync.dma_start(bt[:], beta.partition_broadcast(P)).then_inc(w_in, 16)

            def body(c, par):
                wait_apart(sync, passed, [(o_out[par], 8, c, -8 if par else 0), (done, 1, c, -1)])
                sync.dma_start(si[:, par], rows_of(slots_dram, c)).then_inc(x_in[par], 16)
                sync.dma_start(wt[:, par], rows_of(w_dram, c)).then_inc(x_in[par], 16)
                sync.dma_start(xf[:, par], rows_of(xf_t, c)).then_inc(x_in[par], 16)
                sync.dma_start(x1[:, par], rows_of(x1_t, c)).then_inc(x_in[par], 16)

            chunks(sync, body)

        @block.gpsimd
        def _(pool):
            pool.wait_ge(w_in, 32)
            pool.wait_ge(mem, 1)

            def gather(c, par):
                wait_apart(pool, passed, [(x_in[par], 8 * LD, c, 8 * LD if par else 16 * LD), (done, 1, c, -1)])
                for i in range(NT):
                    for k in range(2):
                        pool.indirect_dma_start(
                            out=ge[:, par, k, i, :], out_offset=None, in_=eo_dram,
                            in_offset=bass.IndirectOffsetOnAxis(ap=si[:, par, k, i:i + 1], axis=0)
                        ).then_inc(g_in[par], 16)

            def body(c, par):
                gather(c, par)
                for i in range(NT):
                    ins = pool.tensor_tensor(x1[:, par, i, :], x1[:, par, i, :], bt[:], ALU.add)
                ins.then_inc(biased, 1)
                wait_apart(pool, passed, [(stat, 2, c, 2)])
                pool.tensor_scalar(ve[:], mv[:, :, 1], EPS, None, ALU.add).then_inc(rs_done, 1)
                wait(pool, rs_done, 2, c, 1)
                pool.tensor_tensor(rs[:], ve[:], mhalf[:], ALU.pow).then_inc(rs_done, 1)

            chunks(pool, body)

        @block.vector
        def _(dve):
            dve.memset(mhalf[:], -0.5).then_inc(mem, 1)
            dve.wait_ge(w_in, 32)

            def body(c, par):
                wait_loads(dve, x_in[par], c, par, LD)
                wait_loads(dve, g_in[par], c, par, 8)
                for k in range(2):
                    for i in range(NT):
                        ins = dve.scalar_tensor_tensor(xf[:, par, i, :], ge[:, par, k, i, :],
                                                       wt[:, par, k, i:i + 1], xf[:, par, i, :], ALU.mult, ALU.add)
                    ins.then_inc(mixed, 1)
                    wait(dve, mixed, 2, c, k + 1)
                for i in range(NT):
                    ins = dve.bn_stats(st[:, i, :], xf[:, par, i, :])
                ins.then_inc(stat, 1)
                wait_apart(dve, passed, [(stat, 2, c, 1)])
                for i in range(NT):
                    ins = dve.bn_aggr(mv[:, i, :], st[:, i, :])
                ins.then_inc(stat, 1)
                wait(dve, stat, 2, c, 2)
                for i in range(NT):
                    ins = dve.scalar_tensor_tensor(xf[:, par, i, :], xf[:, par, i, :], mv[:, i, 0:1], gm[:],
                                                   ALU.subtract, ALU.mult)
                ins.then_inc(scaled, 1)
                wait(dve, scaled, 1, c, 1)
                wait(dve, rs_done, 2, c, 2)
                wait(dve, biased, 1, c, 1)
                for i in range(NT):
                    ins = dve.scalar_tensor_tensor(x1[:, par, i, :], xf[:, par, i, :], rs[:, i:i + 1],
                                                   x1[:, par, i, :], ALU.mult, ALU.add)
                ins.then_inc(done, 1)

            chunks(dve, body)

        @block.scalar
        def _(act):
            def body(c, par):
                wait(act, done, 1, c, 1)
                act.dma_start(rows_of(out_t, c), x1[:, par]).then_inc(o_out[par], 16)

            chunks(act, body)
            for par in range(2):
                act.wait_ge(o_out[par], 16 * NC // 2)


_INS = ['L0_attn_x', 'L0_attn_ln_g', 'L0_attn_ln_b', 'L0_attn_W_in', 'L0_attn_conv_w', 'L0_attn_conv_b',
        'L0_attn_W_xproj', 'L0_attn_W_dt', 'L0_attn_b_dt', 'L0_attn_A_log', 'L0_attn_D_param', 'L0_attn_W_out',
        'L0_ffn_Wg', 'L0_ffn_bg', 'L0_ffn_W1', 'L0_ffn_b1', 'L0_ffn_W2', 'L0_ffn_b2', 'L0_ffn_gamma',
        'L0_ffn_beta']
_OUTS = [((8, 1024, 256), 'float32')]


def kernel(**inputs):
    import numpy as _np
    import concourse.bacc as _bacc
    from concourse import mybir as _mybir
    from concourse.bass_utils import run_bass_kernel_spmd as _run

    nc = _bacc.Bacc("TRN2", target_bir_lowering=False, num_devices=1)
    arrays, args = {}, []
    for name in _INS:
        a = _np.ascontiguousarray(inputs[name])
        arrays[f"in_{name}_dram"] = a
        args.append(nc.dram_tensor(f"in_{name}_dram", a.shape, _mybir.dt.from_np(a.dtype), kind="ExternalInput").ap())
    for i, (shape, dtype) in enumerate(_OUTS):
        dt = _mybir.dt.from_np(_np.dtype(dtype))
        args.append(nc.dram_tensor(f"out_{i}_dram", shape, dt, kind="ExternalOutput").ap())
    mamba_moe_kernel(nc, *args)
    r = _run(nc, [arrays], core_ids=[0])
    got = tuple(r.results[0][f"out_{i}_dram"] for i in range(len(_OUTS)))
    return got[0]
```

```python
from contextlib import ExitStack

import concourse.bass as bass
from concourse import mybir

P = 128
CH = 512
NT = CH // P
EPS = 1e-5

ALU = mybir.AluOpType
ACT = mybir.ActivationFunctionType
AX = mybir.AxisListType
F32 = mybir.dt.float32
I32 = mybir.dt.int32
U32 = mybir.dt.uint32


def wait(eng, sem, per, c, k):
    if isinstance(c, int):
        if per * c + k > 0:
            eng.wait_ge(sem, per * c + k)
    else:
        eng.wait_ge(sem, c * per + k)


def wait_apart(eng, passed, waits):
    for sem, per, c, k in waits:
        wait(eng, sem, per, c, k)
        if not isinstance(c, int):
            eng.sem_inc(passed, 1)


def mamba_moe_kernel(nc, x, ln_g, ln_b, W_in, conv_w, conv_b, W_xproj, W_dt, b_dt, A_log, D_param, W_out,
                     Wg, bg, W1, b1, W2, b2, gamma, beta, out):
    B, L, D = x.shape
    DI = W_in.shape[1] // 2
    G = DI // P
    KD = D // P
    N = A_log.shape[1]
    R = W_dt.shape[0]
    TAPS = conv_w.shape[2]
    HALO = TAPS - 1
    NC = B * L // CH
    assert L == 2 * CH and NC % 2 == 0 and NT == 4 and G == 4 and KD == 2 and R + 2 * N == 96

    xf = x.rearrange("b l d -> (b l) d")
    x_t = xf.rearrange("(c i p) d -> c p i d", p=P, i=NT)
    x1_dram = nc.dram_tensor("x1_scratch", (B * L, D), F32, kind="Internal").ap()
    x1_t = x1_dram.rearrange("(c i p) d -> c p i d", p=P, i=NT)
    b_dram = nc.dram_tensor("b_scratch", (2, N, CH), F32, kind="Internal").ap()

    mamba_block(nc, x_t, x1_t, b_dram, ln_g, ln_b, W_in, conv_w, conv_b, W_xproj, W_dt, b_dt, A_log, D_param,
                W_out, NC, D, DI, G, KD, N, R, TAPS, HALO)
    moe_block(nc, x1_t, out.rearrange("b l d -> (b l) d").rearrange("(c i p) d -> c p i d", p=P, i=NT),
              Wg, bg, W1, b1, W2, b2, gamma, beta, NC, D, KD)


def mamba_block(nc, x_t, x1_t, b_dram, ln_g, ln_b, W_in, conv_w, conv_b, W_xproj, W_dt, b_dt, A_log, D_param,
                W_out, NC, D, DI, G, KD, N, R, TAPS, HALO):
    NB = 8
    K_DT = 97
    SG = N * G
    with ExitStack() as ctx:
        def sb(name, shape):
            return ctx.enter_context(nc.sbuf_tensor(name, shape, F32))

        def sem(name):
            return ctx.enter_context(nc.semaphore(name))

        ident = sb("ident", [P, P])
        win = sb("win", [P, KD, 2 * DI])
        wxp = sb("wxp", [P, G, R + 2 * N])
        wdt = sb("wdt", [K_DT, DI])
        wout = sb("wout", [P, G, D])
        a_neg = sb("a_neg", [P, G, N])
        cw = sb("cw", [P, G, TAPS])
        cb = sb("cb", [P, G])
        dp = sb("dp", [P, G])
        lng = sb("lng", [P, KD])
        lnb = sb("lnb", [P, KD])
        taps = sb("taps", [P, G, TAPS, P])
        xb = sb("xb", [P, 2, NT, D])
        xl = sb("xl", [P, 2, NT, D])
        xn = sb("xn", [P, NT, D])
        h0 = sb("h0", [P, NT, D])
        st = sb("st", [P, 2, NT, 6])
        mv = sb("mv", [P, 2, NT, 2])
        ve = sb("ve", [P, 2, NT])
        rs = sb("rs", [P, 2, NT])
        mhalf = sb("mhalf", [P, NT])
        hT = sb("hT", [P, KD, CH])
        xin = sb("xin", [P, G, HALO + CH])
        zs = sb("zs", [P, 2, G, CH])
        xc = sb("xc", [P, 2, G, CH])
        dbc = sb("dbc", [K_DT, CH])
        cT = sb("cT", [P, 2, NT, N])
        sp = sb("sp", [P, G, CH])
        dl = sb("dl", [P, 2, G, CH])
        du = sb("du", [P, 2, G, CH])
        bb = sb("bb", [P, NB, CH])
        dbu = sb("dbu", [P, 2, G, CH])
        ss = sb("ss", [P, 2, G, CH])
        carry = sb("carry", [P, N, G])
        ya = sb("ya", [P, 2, NT, DI])
        yg = sb("yg", [P, G, CH])
        ps_a = ctx.enter_context(nc.psum_tensor("ps_a", [P, G, CH], F32))
        ps_s = ctx.enter_context(nc.psum_tensor("ps_s", [P, 2, DI], F32))
        ps_p = ctx.enter_context(nc.psum_tensor("ps_p", [P, 2, CH], F32))

        passed = sem("passed")
        w_in = sem("weights_loaded")
        zeroed = sem("zeroed")
        id_done = sem("identity_done")
        a_exp = sem("a_exp")
        const_done = sem("constants_done")
        x_in = [sem(f"x_loaded{i}") for i in range(2)]
        ln_step = sem("ln_step")
        rs_done = sem("rs_done")
        xl_done = sem("xl_done")
        proj_full = sem("proj_full")
        proj_act = sem("proj_evacuated_act")
        halo = sem("halo_set")
        u_done = sem("u_done")
        silu_z = sem("silu_z_done")
        sp_step = sem("softplus_step")
        sp_log = sem("softplus_log")
        dl_done = sem("delta_done")
        b_out = sem("b_stored")
        bb_in = [sem(f"b_row_loaded{i}") for i in range(NB)]
        du_done = sem("du_done")
        exp_done = sem("exp_done")
        dbu_done = sem("dbu_done")
        scan_done = sem("scan_done")
        carry_done = sem("carry_done")
        tr_done = sem("states_turned")
        sum_done = sem("sum_done")
        post_full = sem("post_full")
        post_dve = sem("post_evacuated")
        gate_done = sem("gate_done")
        x1_out = [sem(f"x1_stored{i}") for i in range(2)]

        NW = 11
        LAG = 3
        USES = [("h", 0, 0), ("h", 1, 0), ("x", 0, 1), ("x", 1, 2), ("x", 2, 5), ("x", 3, 6),
                ("conv", 0, 7), ("conv", 1, 9), ("conv", 2, 11), ("conv", 3, 13), ("dbc", 0, 19), ("c", 0, 21),
                ("dt", 0, 21), ("dt", 1, 22), ("dt", 2, 23), ("dt", 3, 24),
                ("z", 0, 25), ("z", 1, 26), ("z", 2, 27), ("z", 3, 28)]
        PARTS = {"conv": 2, "dbc": 2}
        SILU = 17
        LOG = 28
        U_ALL = len(USES)

        def nth(kind, g=0):
            return [u[:2] for u in USES].index((kind, g)) + 1

        block = ctx.enter_context(nc.Block())

        def iterations(eng, body):
            for c in range(3):
                body(c, c % 2)
            with eng.Fori(1, (NC - 4) // 2) as i:
                body(i * 2 + 1, 1)
                body(i * 2 + 2, 0)
            for c in range(NC - 3, NC):
                body(c, c % 2)

        def there(c, d):
            return not isinstance(c, int) or 0 <= c + d < NC

        @block.sync
        def _(sync):
            def load_x(q, par):
                wait_apart(sync, passed, [(xl_done, 1, q, -1)])
                sync.dma_start(xb[:, par], x_t[q] if isinstance(q, int) else
                               x_t[bass.ds(q, 1)].rearrange("c p i d -> (c p) i d")).then_inc(x_in[par], 16)

            def store_b(q, par):
                wait(sync, proj_act, U_ALL, q, nth("dbc"))
                for s in range(NB):
                    wait(sync, bb_in[s], 16 * (N // NB), q, -16 * (N // NB))
                sync.dma_start(b_dram[par], dbc[R:R + N, :]).then_inc(b_out, 16)

            def load_row(c, par, n):
                if n == 0:
                    wait(sync, b_out, 16, c, 16)
                wait(sync, dbu_done, SG, c, (n - NB + 1) * G)
                sync.dma_start(bb[:, n % NB], b_dram[par, n, :].partition_broadcast(P)).then_inc(bb_in[n % NB], 16)

            def store_x1(q, par):
                wait_apart(sync, passed, [(post_dve, 6, q, 6)])
                sync.dma_start(x1_t[q] if isinstance(q, int) else
                               x1_t[bass.ds(q, 1)].rearrange("c p i d -> (c p) i d"), xl[:, par]
                               ).then_inc(x1_out[par], 16)

            load_x(0, 0)
            for dst, src in (
                (win[:], W_in.rearrange("(k p) n -> p k n", p=P)),
                (lng[:], ln_g.rearrange("(k p) -> p k", p=P)),
                (lnb[:], ln_b.rearrange("(k p) -> p k", p=P)),
                (cw[:], conv_w.rearrange("(g p) o k -> p g (o k)", p=P)),
                (cb[:], conv_b.rearrange("(g p) -> p g", p=P)),
                (wxp[:], W_xproj.rearrange("(g p) n -> p g n", p=P)),
                (wdt[0:R, :], W_dt),
                (wdt[K_DT - 1:K_DT, :], b_dt.rearrange("(a n) -> a n", a=1)),
                (a_neg[:], A_log.rearrange("(g p) n -> p g n", p=P)),
                (dp[:], D_param.rearrange("(g p) -> p g", p=P)),
                (wout[:], W_out.rearrange("(g p) n -> p g n", p=P)),
            ):
                with nc.allow_non_contiguous_dma(reason="small weights"):
                    sync.dma_start(dst, src).then_inc(w_in, 16)
            load_x(1, 1)
            store_b(0, 0)

            def body(c, par):
                if there(c, 2):
                    load_x(c + 2, par)
                for n in range(N):
                    load_row(c, par, n)
                    if n == 12:
                        if there(c, -1):
                            store_x1(c - 1, 1 - par)
                if there(c, 1):
                    store_b(c + 1, 1 - par)

            iterations(sync, body)
            store_x1(NC - 1, 1)
            for par in range(2):
                sync.wait_ge(x1_out[par], 16 * NC // 2)

        @block.vector
        def _(dve):
            dve.memset(ident[:], 1.0).then_inc(zeroed, 1)
            dve.memset(mhalf[:], -0.5).then_inc(zeroed, 1)
            dve.memset(wdt[R:R + 2 * N, :], 0.0).then_inc(zeroed, 1)
            dve.memset(dbc[K_DT - 1:K_DT, :], 1.0).then_inc(zeroed, 1)

            def stats(q, src, row):
                for i in range(NT):
                    ins = dve.bn_stats(st[:, row, i, :], src[:, i, :])
                ins.then_inc(ln_step, 1)
                wait_apart(dve, passed, [(ln_step, 6, q, 3 * row + 1)])
                for i in range(NT):
                    ins = dve.bn_aggr(mv[:, row, i, :], st[:, row, i, :])
                ins.then_inc(ln_step, 1)

            def normalise(q, src, dst, row):
                wait(dve, rs_done, 4, q, 2 * row + 2)
                for i in range(NT):
                    ins = dve.tensor_scalar(dst[:, i, :], src[:, i, :], mv[:, row, i, 0:1], rs[:, row, i:i + 1],
                                            ALU.subtract, ALU.mult)
                ins.then_inc(ln_step, 1)

            def norm_a(q, par):
                if isinstance(q, int):
                    dve.wait_ge(x_in[par], 16 * (q // 2 + 1))
                else:
                    wait(dve, x_in[par], 8, q, 8 if par else 16)
                stats(q, xb[:, par], 0)

            def norm_b(q, par):
                wait(dve, xl_done, 1, q, 0)
                normalise(q, xb[:, par], xn, 0)
                wait(dve, ln_step, 6, q, 3)
                stats(q, xn, 1)

            def norm_c(q, par):
                wait(dve, proj_full, U_ALL, q, nth("h", 1) - U_ALL)
                normalise(q, xn, h0, 1)

            def add_xl(q, par):
                if isinstance(q, int):
                    if q >= 2:
                        dve.wait_ge(x1_out[par], 16 * (q // 2))
                else:
                    wait(dve, x1_out[par], 8, q, -8 if par else 0)
                dve.tensor_tensor(xl[:, par], xb[:, par], xn[:], ALU.add).then_inc(xl_done, 1)

            def scans(c, par, n, groups):
                for g in groups:
                    k = n * G + g
                    wait(dve, exp_done, SG, c, k + 1)
                    wait(dve, dbu_done, SG, c, k + 1)
                    if g == 0:
                        wait(dve, tr_done, N * NT, c, (n - 1) * NT)
                        if par == 1 and n == 0:
                            wait(dve, carry_done, N // 2, c, N // 2)
                    init = carry[:, n, g:g + 1] if par else 0.0
                    dve.tensor_tensor_scan(ss[:, n % 2, g, :], ps_a[:, g, :], dbu[:, n % 2, g, :], init,
                                           ALU.mult, ALU.add).then_inc(scan_done, 1)

            def save(c, n):
                wait(dve, scan_done, SG, c, n * G + G)
                dve.tensor_copy(carry[:, n, :], ss[:, n % 2, :, CH - 1]).then_inc(carry_done, 1)

            def sums(c, par, n, tiles):
                for i in tiles:
                    k = n * NT + i
                    wait(dve, tr_done, N * NT, c, k + 1)
                    if n == 0:
                        if i == 0:
                            wait(dve, proj_act, U_ALL, c, nth("c"))
                            wait(dve, post_full, 6, c, -6)
                        dve.tensor_scalar(ya[:, par, i, :], ps_s[:, k % 2, :], cT[:, par, i, n:n + 1], None,
                                          ALU.mult).then_inc(sum_done, 1)
                    else:
                        wait(dve, sum_done, N * NT, c, k - NT + 1)
                        dve.scalar_tensor_tensor(ya[:, par, i, :], ps_s[:, k % 2, :], cT[:, par, i, n:n + 1],
                                                 ya[:, par, i, :], ALU.mult, ALU.add).then_inc(sum_done, 1)

            def skip_gate(q, par, g):
                wait(dve, post_full, 6, q, g + 1)
                if g == 0:
                    wait(dve, post_full, 6, q, 0)
                dve.scalar_tensor_tensor(yg[:, g, :], xc[:, par, g, :], dp[:, g:g + 1], ps_p[:, g % 2, :],
                                         ALU.mult, ALU.add).then_inc(post_dve, 1)

            def gate(q, par, g):
                wait(dve, post_dve, 6, q, g + 1)
                if g == 0:
                    wait(dve, silu_z, 1, q, 1)
                dve.tensor_tensor(yg[:, g, :], yg[:, g, :], zs[:, par, g, :], ALU.mult).then_inc(gate_done, 1)

            def residual(q, par, j):
                wait(dve, post_full, 6, q, 5 + j)
                wait(dve, xl_done, 1, q, 1)
                dve.tensor_tensor(xl[:, par, 2 * j:2 * j + 2, :],
                                  ps_p[:, j, :].rearrange("p (i d) -> p i d", d=D),
                                  xl[:, par, 2 * j:2 * j + 2, :], ALU.add).then_inc(post_dve, 1)

            dve.wait_ge(w_in, 16 * NW)
            dve.wait_ge(a_exp, 1)
            dve.wait_ge(id_done, 1)
            dve.tensor_scalar(a_neg[:], a_neg[:], -1.0, None, ALU.mult).then_inc(const_done, 1)
            for g in range(G):
                for k in range(TAPS):
                    ins = dve.tensor_scalar(taps[:, g, k, :], ident[:], cw[:, g, k:k + 1], None, ALU.mult)
            ins.then_inc(const_done, 1)
            norm_a(0, 0)
            norm_b(0, 0)
            norm_c(0, 0)
            add_xl(0, 0)
            norm_a(1, 1)
            norm_b(1, 1)
            norm_c(1, 1)

            def body(c, par):
                for s in range(2 * N):
                    n, tiles = s // 2, (0, 1) if s % 2 == 0 else (2, 3)
                    scans(c, par, n, tiles)
                    if n > 0:
                        sums(c, par, n - 1, tiles)
                    elif there(c, -1):
                        sums(c - 1, 1 - par, N - 1, tiles)
                    if par == 0 and s % 2:
                        save(c, n)
                    if there(c, -1):
                        if s in (3, 4):
                            for g in (2 * s - 6, 2 * s - 5):
                                skip_gate(c - 1, 1 - par, g)
                            for g in (2 * s - 6, 2 * s - 5):
                                gate(c - 1, 1 - par, g)
                        if s in (17, 19):
                            residual(c - 1, 1 - par, (s - 17) // 2)
                    if there(c, 1):
                        if s == 24:
                            add_xl(c + 1, 1 - par)
                    if there(c, 2):
                        if s == 20:
                            norm_a(c + 2, par)
                        if s == 25:
                            norm_b(c + 2, par)
                        if s == 28:
                            norm_c(c + 2, par)

            iterations(dve, body)
            sums(NC - 1, 1, N - 1, range(NT))
            for g in range(G):
                skip_gate(NC - 1, 1, g)
                gate(NC - 1, 1, g)
            residual(NC - 1, 1, 0)
            residual(NC - 1, 1, 1)

        @block.gpsimd
        def _(pool):
            pool.wait_ge(zeroed, 1)
            pool.affine_select(out=ident[:], in_=ident[:], compare_op=ALU.is_equal, fill=0.0, base=0,
                               pattern=[[-1, P]], channel_multiplier=1).then_inc(id_done, 1)

            def add_log(q, par, g):
                if g == 0:
                    wait(pool, sp_log, 1, q, 1)
                pool.tensor_tensor(dl[:, par, g, :], dl[:, par, g, :], sp[:, g, :], ALU.add).then_inc(dl_done, 1)

            def times_u(q, par, g):
                wait(pool, dl_done, G, q, g + 1)
                pool.tensor_tensor(du[:, par, g, :], dl[:, par, g, :], xc[:, par, g, :], ALU.mult
                                   ).then_inc(du_done, 1)

            def times_b(c, par, n):
                wait(pool, bb_in[n % NB], 16 * (N // NB), c, 16 * (n // NB + 1))
                if n == 0:
                    wait(pool, du_done, G, c, G)
                for g in range(G):
                    wait(pool, scan_done, SG, c, (n - 2) * G + g + 1)
                    pool.tensor_tensor(dbu[:, n % 2, g, :], du[:, par, g, :], bb[:, n % NB, :], ALU.mult
                                       ).then_inc(dbu_done, 1)

            def inv_std(q, row):
                wait_apart(pool, passed, [(ln_step, 6, q, 3 * row + 2)])
                pool.tensor_scalar(ve[:, row, :], mv[:, row, :, 1], EPS, None, ALU.add).then_inc(rs_done, 1)
                wait(pool, rs_done, 4, q, 2 * row + 1)
                pool.tensor_tensor(rs[:, row, :], ve[:, row, :], mhalf[:], ALU.pow).then_inc(rs_done, 1)

            pool.wait_ge(zeroed, 4)
            inv_std(0, 0)
            inv_std(0, 1)
            inv_std(1, 0)
            inv_std(1, 1)
            for g in range(G):
                add_log(0, 0, g)
            for g in range(G):
                times_u(0, 0, g)

            def body(c, par):
                for n in range(N):
                    times_b(c, par, n)
                    if there(c, 2) and n in (11, 13):
                        inv_std(c + 2, (n - 11) // 2)
                    if there(c, 1):
                        if n >= N - 2:
                            for g in (2 * (n - N + 2), 2 * (n - N + 2) + 1):
                                add_log(c + 1, 1 - par, g)
                        if n == N - 1:
                            for g in range(G):
                                times_u(c + 1, 1 - par, g)

            iterations(pool, body)

        @block.scalar
        def _(act):
            def set_halo(q, par):
                wait(act, proj_full, U_ALL, q, nth("conv", 3) - U_ALL)
                if par == 0:
                    act.memzero(xin[:, :, 0:HALO]).then_inc(halo, 1)
                else:
                    act.copy(xin[:, :, 0:HALO], xin[:, :, CH:CH + HALO]).then_inc(halo, 1)

            def empty(q, par, u):
                kind, g, _ = USES[u]
                wait(act, proj_full, U_ALL, q, u + 1)
                src = ps_p[:, u % 2, :]
                if kind == "h":
                    act.activation(hT[:, g, :], src, ACT.Identity, bias=lnb[:, g:g + 1], scale=lng[:, g:g + 1]
                                   ).then_inc(proj_act, 1)
                elif kind == "x":
                    if g == 0:
                        wait(act, halo, 1, q, 1)
                    act.copy(xin[:, g, HALO:], src).then_inc(proj_act, 1)
                elif kind == "z":
                    if g == 0:
                        wait(act, gate_done, G, q, -G)
                    act.copy(zs[:, par, g, :], src).then_inc(proj_act, 1)
                elif kind == "conv":
                    if g == 0:
                        wait(act, post_dve, 6, q, 4 - 12)
                        wait(act, du_done, G, q, -G)
                    act.activation(xc[:, par, g, :], src, ACT.Identity, bias=cb[:, g:g + 1]).then_inc(proj_act, 1)
                elif kind == "dbc":
                    wait(act, b_out, 16, q, 0)
                    act.copy(dbc[0:R + 2 * N, :], src[0:R + 2 * N, :]).then_inc(proj_act, 1)
                elif kind == "dt":
                    if g == 0:
                        wait(act, exp_done, SG, q, -SG)
                        wait(act, dl_done, G, q, 0)
                        wait(act, du_done, G, q, -G)
                    t = sp[:, g, :]
                    act.activation(dl[:, par, g, :], src, ACT.Relu).then_inc(sp_step, 1)
                    act.activation(t, src, ACT.Abs).then_inc(proj_act, 1)
                    wait(act, proj_act, U_ALL, q, u + 1)
                    act.activation(t, t, ACT.Exp, scale=-1.0).then_inc(sp_step, 1)
                else:
                    wait(act, sum_done, N * NT, q, -N * NT)
                    act.copy(cT[:, par], src[:, 0:NT * 96].rearrange("p (i n) -> p i n", n=96)[:, :, R + N:]
                             ).then_inc(proj_act, 1)

            def log_term(q):
                wait(act, sp_step, 2 * G, q, 2 * G)
                act.activation(sp[:], sp[:], ACT.Ln, bias=1.0).then_inc(sp_log, 1)

            def silu_u(q, par):
                wait(act, proj_act, U_ALL, q, nth("conv", 3))
                act.activation(xc[:, par], xc[:, par], ACT.Silu).then_inc(u_done, 1)

            def silu_gate(q, par):
                wait(act, proj_act, U_ALL, q, nth("z", 3))
                act.activation(zs[:, par], zs[:, par], ACT.Silu).then_inc(silu_z, 1)

            def exps(c, par, n, groups):
                for g in groups:
                    wait(act, scan_done, SG, c, (n - 1) * G + g + 1)
                    act.activation(ps_a[:, g, :], dl[:, par, g, :], ACT.Exp, scale=a_neg[:, g, n:n + 1]
                                   ).then_inc(exp_done, 1)

            act.wait_ge(w_in, 16 * NW)
            act.activation(a_neg[:], a_neg[:], ACT.Exp).then_inc(a_exp, 1)
            act.wait_ge(const_done, 1)
            set_halo(0, 0)
            for u, (kind, g, _) in enumerate(USES):
                empty(0, 0, u)
                if (kind, g) == ("conv", 3):
                    silu_u(0, 0)
                if (kind, g) == ("dt", 3):
                    log_term(0)

            def pieces(c, par, s):
                for u, (kind, g, at) in enumerate(USES):
                    if at + PARTS.get(kind, 1) - 1 + LAG == s and there(c, 1):
                        if u == 0:
                            set_halo(c + 1, 1 - par)
                        empty(c + 1, 1 - par, u)
                if s == SILU:
                    if there(c, 1):
                        silu_u(c + 1, 1 - par)
                    silu_gate(c, par)
                if s == LOG and there(c, 1):
                    log_term(c + 1)

            def body(c, par):
                for s in range(2 * N):
                    pieces(c, par, s)
                    if s < 2:
                        wait(act, dl_done, G, c, 2 * s + 2)
                    exps(c, par, s // 2, (0, 1) if s % 2 == 0 else (2, 3))

            iterations(act, body)

        @block.tensor
        def _(pe):
            def project(q, par, u, part, parts, post):
                kind, g, _ = USES[u]
                if part == 0:
                    if post and u in (nth("x", 2) - 1, nth("x", 3) - 1):
                        wait(pe, post_dve, 6, q, 3 + g - 2 - 12)
                    elif post and u in (nth("dbc") - 1, nth("c") - 1):
                        wait(pe, post_dve, 6, q, 5 + (kind == "c") - 12)
                    else:
                        wait(pe, proj_act, U_ALL, q, u - 1)
                dst = ps_p[:, u % 2, :]
                if kind == "h":
                    if g == 0:
                        wait(pe, ln_step, 6, q, 6)
                    for i in range(NT):
                        ins = pe.transpose(dst[:, i * P:(i + 1) * P], h0[:, i, g * P:(g + 1) * P], ident[:])
                elif kind in "xz":
                    if (kind, g) == ("x", 0):
                        wait(pe, proj_act, U_ALL, q, nth("h", 1))
                    m = g * P + (DI if kind == "z" else 0)
                    for k in range(KD):
                        ins = pe.matmul(dst, win[:, k, m:m + P], hT[:, k, :], start=(k == 0), stop=(k == KD - 1))
                elif kind == "conv":
                    if part == 0:
                        wait(pe, proj_act, U_ALL, q, nth("x", g))
                    for k in range(TAPS * part // parts, TAPS * (part + 1) // parts):
                        ins = pe.matmul(dst, taps[:, g, k, :], xin[:, g, k:k + CH],
                                        start=(k == 0), stop=(k == TAPS - 1))
                elif kind == "dbc":
                    if part == 0:
                        wait(pe, u_done, 1, q, 1)
                    for k in range(G * part // parts, G * (part + 1) // parts):
                        ins = pe.matmul(dst[0:96, :], wxp[:, k, :], xc[:, par, k, :],
                                        start=(k == 0), stop=(k == G - 1))
                elif kind == "dt":
                    ins = pe.matmul(dst, wdt[:, g * P:(g + 1) * P], dbc[:], start=True, stop=True)
                else:
                    wait(pe, proj_act, U_ALL, q, nth("dbc"))
                    for i in range(NT):
                        ins = pe.transpose(dst[:, i * 96:(i + 1) * 96], dbc[0:96, i * P:(i + 1) * P],
                                           ident[0:96, 0:96])
                if part == parts - 1:
                    ins.then_inc(proj_full, 1)

            def turn(c, par, n, tiles):
                if 0 in tiles:
                    wait(pe, scan_done, SG, c, n * G + G)
                for i in tiles:
                    k = n * NT + i
                    wait(pe, sum_done, N * NT, c, k - 1)
                    for g in range(G):
                        ins = pe.transpose(ps_s[:, k % 2, g * P:(g + 1) * P], ss[:, n % 2, g, i * P:(i + 1) * P],
                                           ident[:])
                    ins.then_inc(tr_done, 1)

            def turn_back(q, par, g, taken):
                if g == 0:
                    wait(pe, sum_done, N * NT, q, N * NT)
                wait(pe, *taken)
                for i in range(NT):
                    ins = pe.transpose(ps_p[:, g % 2, i * P:(i + 1) * P], ya[:, par, i, g * P:(g + 1) * P], ident[:])
                ins.then_inc(post_full, 1)

            def project_out(q, i, taken):
                j = i // 2
                if i == 0:
                    wait(pe, gate_done, G, q, G)
                if i % 2 == 0:
                    wait(pe, *taken)
                for g in range(G):
                    ins = pe.matmul(ps_p[:, j, (i % 2) * D:(i % 2 + 1) * D], yg[:, g, i * P:(i + 1) * P],
                                    wout[:, g, :], start=(g == 0), stop=(g == G - 1))
                if i % 2:
                    ins.then_inc(post_full, 1)

            pe.wait_ge(w_in, 16 * NW)
            pe.wait_ge(zeroed, 4)
            pe.wait_ge(id_done, 1)
            pe.wait_ge(const_done, 2)
            for u in range(U_ALL):
                project(0, 0, u, 0, 1, False)

            def body(c, par):
                post, proj = there(c, -1), there(c, 1)
                for s in range(2 * N):
                    if post and s == 3:
                        for g in range(2):
                            turn_back(c - 1, 1 - par, g,
                                      (proj_act, U_ALL, c, U_ALL + nth("x", g) if proj else U_ALL - 1 + g))
                    if post and s == 4:
                        for g in range(2, 4):
                            turn_back(c - 1, 1 - par, g, (post_dve, 6, c - 1, g - 1))
                    if post and 15 <= s < 19:
                        j = (s - 15) // 2
                        project_out(c - 1, s - 15, (proj_act, U_ALL, c, U_ALL + nth("conv", 2 + j)) if proj else
                                    (post_dve, 6, c - 1, 3 + j))
                    for u, (kind, _, at) in enumerate(USES):
                        parts = PARTS.get(kind, 1)
                        if at <= s < at + parts and proj:
                            project(c + 1, 1 - par, u, s - at, parts, post)
                    turn(c, par, s // 2, (0, 1) if s % 2 == 0 else (2, 3))

            iterations(pe, body)
            for g in range(G):
                turn_back(NC - 1, 1, g, (post_dve, 6, NC - 1, g - 1))
            for i in range(NT):
                project_out(NC - 1, i, (post_dve, 6, NC - 1, 3 + i // 2))


def rows_of(t, c):
    return t[c] if isinstance(c, int) else t[bass.ds(c, 1)].rearrange("c p i d -> (c p) i d")


def wait_slot(eng, sem, t, ring, slot, per=16, more=0):
    if isinstance(t, int):
        v = per * (t // ring + 1 + more)
        if v > 0:
            eng.wait_ge(sem, v)
    else:
        wait(eng, sem, per // ring, t, per * (1 + more) - per // ring * slot)


def moe_block(nc, x1_t, out_t, Wg, bg, W1, b1, W2, b2, gamma, beta, NC, D, KD):
    E = Wg.shape[1]
    F = W1.shape[2]
    KF = F // P
    GC = 4
    NG = NC // GC
    GT = GC * NT
    T = NC * NT
    XW = D + 2
    REG = (T + 1) * P
    NTT = 2 * T + E - 1
    LAG = 3
    RING = 4
    NTT += (LAG + 2 - NTT) % RING
    PADS = E + NTT - 2 * T
    KR = 22
    KT = 12
    SC = 2 * NT
    x1_rows, XIN = x1_t, 2
    xs_dram = nc.dram_tensor("xs_scratch", (E * REG + (PADS - E) * P, XW), F32, kind="Internal").ap()
    eo_dram = nc.dram_tensor("eo_scratch", ((2 * T + PADS) * P, D), F32, kind="Internal").ap()
    eo_t = eo_dram[0:2 * T * P, :].rearrange("(k c i p) d -> k c p i d", k=2, i=NT, p=P)
    with ExitStack() as ctx:
        def sb(name, shape, dt=F32):
            return ctx.enter_context(nc.sbuf_tensor(name, shape, dt))

        def sem(name):
            return ctx.enter_context(nc.semaphore(name))

        ident = sb("e_ident", [P, P])
        below = sb("below", [P, P])
        ones = sb("ones", [P, P])
        wg = sb("wg", [P, KD, E])
        bgb = sb("bgb", [P, E])
        gm = sb("gm", [P, D])
        bt = sb("bt", [P, D])
        w1 = sb("w1", [P, KD, E * F])
        w2 = sb("w2", [P, E * KF * D])
        b1b = sb("b1b", [P, E * F])
        b2b = sb("b2b", [P, E * D])
        mhalf = sb("r_mhalf", [P, NT])
        xn = sb("r_xn", [P, NC, NT, D])
        x1 = sb("r_x1", [P, 2, NT, D])
        big = sb("big", [P, max(4 * NT, PADS) * XW])
        st = sb("r_st", [P, 2, NT, 6])
        mv = sb("r_mv", [P, 2, NT, 2])
        ve = sb("r_ve", [P, 2, NT])
        rs = sb("r_rs", [P, 2, NT])
        idf = sb("idf", [P, 2, NC * NT])
        run = sb("run", [P, E])
        reg = sb("reg", [P, E])
        tabi = sb("tabi", [P, 2, NTT], I32)
        sli = sb("sli", [P, 2, GT], U32)
        wt = sb("wt", [P, 2, GT])
        xt = sb("xt", [P, RING, XW])
        meta = sb("meta", [P, RING, 2])
        idx = sb("idx", [P, 2, 1], U32)
        pool_a = sb("tiles", [P, 2 * (KD * P + D + D)])
        pool_b = sb("hidden", [P, 2 * 2 * F])
        xT = pool_a[:, 0:2 * KD * P].rearrange("p (b n) -> p b n", b=2)
        ot = pool_a[:, 2 * KD * P:2 * KD * P + 2 * D].rearrange("p (b n) -> p b n", b=2)
        ow = pool_a[:, 2 * KD * P + 2 * D:].rearrange("p (b n) -> p b n", b=2)
        hb = pool_b[:, 0:2 * F].rearrange("p (b n) -> p b n", b=2)
        hT = pool_b[:, 2 * F:].rearrange("p (b n) -> p b n", b=2)
        W = GT * E
        lg, eq, cn, slot, both, first, cum, excl = (pool_a[:, j * W:(j + 1) * W].rearrange("p (i e) -> p i e", e=E)
                                                    for j in range(8))
        sel = pool_a[:, 8 * W:10 * W].rearrange("p (k i e) -> p k i e", k=2, e=E)
        pick = pool_a[:, 10 * W:12 * W].rearrange("p (k i e) -> p k i e", k=2, e=E)
        rT = pool_b[:, 0:KD * CH].rearrange("p (k n) -> p k n", k=KD)
        tot, start = (pool_b[:, KD * CH + j * W:KD * CH + (j + 1) * W].rearrange("p (e i) -> p e i", e=E)
                      for j in range(2))
        small = pool_b[:, KD * CH + 2 * W:]
        mx = small[:, 0:2 * GT].rearrange("p (k i) -> p k i", k=2)
        ex = small[:, 2 * GT:3 * GT]
        den = small[:, 3 * GT:4 * GT]
        slf = small[:, 4 * GT:6 * GT].rearrange("p (k i) -> p k i", k=2)
        xflat = x1[:].rearrange("p b i d -> p (b i d)")
        over = xflat[:, 0:E * T].rearrange("p (e t) -> p e t", e=E)
        cmp = xflat[:, E * T:E * (T + NTT)].rearrange("p (t e) -> p t e", e=E)
        stage = big[:, 0:4 * NT * XW].rearrange("p (b k i w) -> p b k i w", b=2, k=2, w=XW)
        pads = big[:, 0:PADS * XW].rearrange("p (j w) -> p j w", w=XW)
        ee = big[:, 0:4 * NT * D].rearrange("p (b k i d) -> p b k i d", b=2, k=2, d=D)
        ji = sb("ji", [P, T], I32)
        jf = sb("jf", [P, T])
        cnt = sb("cnt", [P, E])
        ntl = sb("ntl", [P, E])
        end = sb("end", [P, E])
        skip = sb("skip", [P, E])
        ti = sb("ti", [P, NTT], I32)
        tf = sb("tf", [P, NTT])
        eid = sb("eid", [P, NTT])
        row = sb("row", [P, NTT])
        padf = sb("padf", [P, E])
        padi = sb("padi", [P, E], U32)
        pf = sb("pf", [P, 1])
        pi = sb("pi", [P, 1], I32)
        qi = sb("qi", [P, PADS], I32)
        idi = sb("idi", [P, 2, NC * NT], I32)

        ps_x = ctx.enter_context(nc.psum_tensor("e_ps_x", [P, 2, CH], F32))
        ps_h = ctx.enter_context(nc.psum_tensor("e_ps_h", [P, 2, F], F32))
        ps_t = ctx.enter_context(nc.psum_tensor("e_ps_t", [P, 2, F], F32))
        ps_o = ctx.enter_context(nc.psum_tensor("e_ps_o", [P, 2, CH], F32))
        ps_l, ps_r, ps_n = ps_h[:, 0, :], ps_t[:, 0, :], ps_o[:, 0, :]

        passed = sem("e_passed")
        r_in = sem("router_loaded")
        w_in = sem("experts_loaded")
        made = sem("masks_made")
        mem = sem("memsets")
        x_in = [sem(f"m_x1_loaded{i}") for i in range(2)]
        stat = sem("stats")
        rs_done = sem("m_rs_done")
        xn_done = sem("xn_done")
        turned = sem("xn_turned")
        copied = sem("xn_copied")
        kept = sem("xn_kept")
        logit = sem("logits_done")
        step = sem("route_step")
        e_done = sem("e_done")
        ranked = sem("ranked")
        staged = sem("rows_staged")
        scat = [sem(f"rows_scattered{i}") for i in range(2)]
        tabs = sem("table_step")
        pad_done = sem("pads_made")
        pad_out = sem("pads_stored")
        pad_scat = sem("pads_scattered")
        t_in = [sem(f"tile_loaded{i}") for i in range(RING)]
        x_turned = sem("x_turned")
        x_copied = sem("x_copied")
        h_full = sem("h_full")
        h_done = sem("h_done")
        h_turned = sem("h_turned")
        h_relu = sem("h_relu")
        o_full = sem("o_full")
        o_done = sem("o_done")
        o_weighed = sem("o_weighed")
        idx_done = sem("idx_done")
        t_out = [sem(f"tile_stored{i}") for i in range(2)]
        c_in = [sem(f"c_loaded{i}") for i in range(2)]
        o_out = [sem(f"out_stored{i}") for i in range(2)]
        summed = sem("summed")
        c_stat = sem("c_stats")
        c_rs = sem("c_rs_done")
        scaled = sem("scaled")
        biased = sem("biased")
        done = sem("c_done")
        LD = 3

        block = ctx.enter_context(nc.Block())

        def groups(eng, body):
            body(0)
            body(1)
            with eng.Fori(2, NG) as j:
                body(j)

        def chunks(eng, body):
            for c in range(4):
                body(c, c % 2)
            with eng.Fori(2, NC // 2) as i:
                body(i * 2, 0)
                body(i * 2 + 1, 1)

        def tiles(eng, body):
            for s in range(LAG + 2):
                body(s, s % RING)
            with eng.Fori(0, (NTT - LAG - 2) // RING) as i:
                for r in range(LAG + 2, LAG + 2 + RING):
                    body(i * RING + r, r % RING)
            for s in range(NTT, NTT + LAG):
                body(s, s % RING)

        def real(t):
            return not isinstance(t, int) or 0 <= t < NTT

        def at(t, c):
            return t[:, c] if isinstance(c, int) else t[:, bass.ds(c, 1)].rearrange("p c i d -> p (c i) d")

        @block.sync
        def _(sync):
            with nc.allow_non_contiguous_dma(reason="small weights"):
                sync.dma_start(wg[:], Wg.rearrange("(k p) e -> p k e", p=P)).then_inc(r_in, 16)
                sync.dma_start(bgb[:], bg.partition_broadcast(P)).then_inc(r_in, 16)

            def load_x1(j):
                for q in range(GC):
                    wait_apart(sync, passed, [(turned, KD, j * GC + q, -KD), (kept, 1, j * GC + q, -1)])
                    sync.dma_start(x1[:, q % 2], rows_of(x1_t, j * GC + q)).then_inc(x_in[q % 2], 16)

            groups(sync, load_x1)

            sync.wait_ge(pad_done, 3)
            for j in range(E, PADS):
                r = E * REG + (j - E) * P
                sync.dma_start(xs_dram[r:r + P, :], pads[:, j, :]).then_inc(pad_out, 16)
            sync.wait_ge(pad_out, 16 * (PADS - E))
            sync.wait_ge(pad_scat, 16 * E)
            for par in range(2):
                sync.wait_ge(scat[par], 16 * SC * NC // 2)
            sync.wait_ge(tabs, KT)

            def load_tile(t, slot):
                off = sync.value_load(tabi[0:1, 0, bass.ds(t, 1)], min_val=0, max_val=xs_dram.shape[0] - P)
                wait_apart(sync, passed, [(x_copied, 1, t, 1 - RING)])
                sync.dma_start(xt[:, slot, :], xs_dram[bass.ds(off, P), :]).then_inc(t_in[slot], 16)

            tiles(sync, lambda s, slot: load_tile(s, slot) if real(s) else None)

            sync.wait_ge(t_out[0], 16 * ((NTT + 1) // 2))
            sync.wait_ge(t_out[1], 16 * (NTT // 2))

            def load_chunk(c, par):
                wait_apart(sync, passed, [(o_out[par], 8, c, -8 if par else 0), (summed, 2, c, -3)])
                for k in range(2):
                    sync.dma_start(ee[:, par, k], rows_of(eo_t[k], c)).then_inc(c_in[par], 16)
                sync.dma_start(x1[:, par], rows_of(x1_t, c)).then_inc(c_in[par], 16)

            chunks(sync, load_chunk)

        @block.vector
        def _(dve):
            dve.memset(ident[:], 1.0).then_inc(mem, 1)
            dve.memset(below[:], 1.0).then_inc(mem, 1)
            dve.memset(ones[:], 1.0).then_inc(mem, 1)
            dve.memset(mhalf[:], -0.5).then_inc(mem, 1)
            dve.memset(first, 1.0).then_inc(mem, 1)
            dve.memset(start, 1.0).then_inc(mem, 1)
            dve.wait_ge(mem, 6)
            dve.memset(first[:, :, 0], 0.0).then_inc(mem, 1)
            dve.memset(start[:, :, 0], 0.0).then_inc(mem, 1)
            for e in range(E):
                dve.memset(run[:, e:e + 1], float(e * REG)).then_inc(mem, 1)
                dve.memset(reg[:, e:e + 1], float(e * REG)).then_inc(mem, 1)
            dve.wait_ge(mem, 8 + 2 * E)
            dve.wait_ge(made, 6)
            dve.tensor_copy(idf[:], idi[:]).then_inc(mem, 1)
            dve.wait_ge(r_in, 32)

            def stats(c, par):
                wait_slot(dve, x_in[par], c, 2, par)
                for i in range(NT):
                    ins = dve.bn_stats(st[:, par, i, :], x1[:, par, i, :])
                ins.then_inc(stat, 1)
                wait_apart(dve, passed, [(stat, 2, c, 1)])
                for i in range(NT):
                    ins = dve.bn_aggr(mv[:, par, i, :], st[:, par, i, :])
                ins.then_inc(stat, 1)

            def normalise(c, par):
                wait(dve, rs_done, 2, c, 2)
                for i in range(NT):
                    ins = dve.tensor_scalar(x1[:, par, i, :], x1[:, par, i, :], mv[:, par, i, 0:1],
                                            rs[:, par, i:i + 1], ALU.subtract, ALU.mult)
                ins.then_inc(xn_done, 1)

            def route(j):
                count = [0]

                def link(ins):
                    count[0] += 1
                    ins.then_inc(step, 1)
                    wait(dve, step, KR, j, count[0])

                wait(dve, logit, GC, j, GC)
                link(dve.tensor_tensor(lg, ps_l[:, 0:W].rearrange("p (i e) -> p i e", e=E),
                                       bgb[:].unsqueeze(1).broadcast_to([P, GT, E]), ALU.add))
                for k in range(2):
                    link(dve.tensor_reduce(mx[:, k, :], lg, AX.X, ALU.max))
                    link(dve.tensor_tensor(eq, lg, mx[:, k, :].unsqueeze(2).broadcast_to([P, GT, E]),
                                           ALU.is_equal))
                    link(dve.tensor_tensor_scan(cn.rearrange("p i e -> p (i e)"),
                                                first.rearrange("p i e -> p (i e)"),
                                                eq.rearrange("p i e -> p (i e)"), 0.0, ALU.mult, ALU.add))
                    link(dve.scalar_tensor_tensor(sel[:, k], cn, 1.0, eq, ALU.is_equal, ALU.mult))
                    if k == 0:
                        link(dve.scalar_tensor_tensor(lg, sel[:, 0], -3e38, lg, ALU.mult, ALU.add))
                link(dve.tensor_tensor(both, sel[:, 0], sel[:, 1], ALU.add))
                assert count[0] == 11
                link(dve.tensor_tensor(ex, mx[:, 1, :], mx[:, 0, :], ALU.subtract))
                wait(dve, ranked, 1, j, 1)
                link(dve.tensor_copy(tot, ps_n[:, 0:W].rearrange("p (i e) -> p e i", e=E)))
                link(dve.tensor_tensor_scan(cum.rearrange("p i e -> p (i e)"),
                                            start.rearrange("p e i -> p (e i)"),
                                            tot.rearrange("p e i -> p (e i)"), 0.0, ALU.mult, ALU.add))
                cum_ei = cum.rearrange("p i e -> p (i e)").rearrange("p (e i) -> p e i", e=E)
                dve.tensor_tensor(excl.rearrange("p i e -> p e i"), cum_ei, tot, ALU.subtract)
                wait(dve, e_done, 1, j, 1)
                link(dve.tensor_scalar(den, ex, 1.0, None, ALU.add))
                link(dve.tensor_tensor(excl, excl, run[:].unsqueeze(1).broadcast_to([P, GT, E]), ALU.add))
                dve.tensor_tensor(slot, ps_r[:, 0:W].rearrange("p (i e) -> p i e", e=E), excl, ALU.add)
                link(dve.tensor_tensor(run[:], cum_ei[:, :, GT - 1], run[:], ALU.add))
                for k in range(2):
                    ins = dve.tensor_tensor(pick[:, k], sel[:, k], slot, ALU.mult)
                link(ins)
                for k in range(2):
                    ins = dve.tensor_reduce(slf[:, k, :], pick[:, k], AX.X, ALU.add)
                link(ins)
                wait(dve, staged, GC, j, 0)
                for par in range(2):
                    wait(dve, scat[par], 16 * SC * GC // 2, j, 0)
                link(dve.reciprocal(wt[:, 0, :], den))
                link(dve.tensor_tensor(wt[:, 1, :], wt[:, 0, :], ex, ALU.mult))
                link(dve.tensor_copy(sli[:], slf))
                assert count[0] == KR, count

            def group(j):
                stats(j * GC, 0)
                for q in range(GC):
                    if q + 1 < GC:
                        stats(j * GC + q + 1, (q + 1) % 2)
                    normalise(j * GC + q, q % 2)
                route(j)

            groups(dve, group)

            count = [0]

            def link(ins):
                count[0] += 1
                ins.then_inc(tabs, 1)
                dve.wait_ge(tabs, count[0])

            dve.tensor_copy(jf[:], ji[:])
            dve.tensor_copy(tf[:], ti[:])
            dve.tensor_tensor(cnt[:], run[:], reg[:], ALU.subtract)
            link(dve.tensor_copy(pf[:], pi[:]))
            link(dve.tensor_scalar(padf[:], run[:], pf[:], None, ALU.add))
            link(dve.tensor_copy(padi[:], padf[:]))
            link(dve.tensor_tensor(over, cnt[:].unsqueeze(2).broadcast_to([P, E, T]),
                                   jf[:].unsqueeze(1).broadcast_to([P, E, T]), ALU.is_gt))
            link(dve.tensor_reduce(ntl[:], over, AX.X, ALU.add))
            link(dve.tensor_tensor_scan(end[:], ones[:, 0:E], ntl[:], 0.0, ALU.mult, ALU.add))
            link(dve.tensor_scalar(skip[:], ntl[:], float(-P), float(REG), ALU.mult, ALU.add))
            link(dve.tensor_tensor(cmp, end[:].unsqueeze(1).broadcast_to([P, NTT, E]),
                                   tf[:].unsqueeze(2).broadcast_to([P, NTT, E]), ALU.is_le))
            link(dve.tensor_reduce(eid[:], cmp, AX.X, ALU.add))
            link(dve.tensor_tensor(cmp, cmp, skip[:].unsqueeze(1).broadcast_to([P, NTT, E]), ALU.mult))
            link(dve.tensor_reduce(row[:], cmp, AX.X, ALU.add))
            dve.tensor_scalar(tabi[:, 1, :], eid[:], float(E - 1), None, ALU.min)
            link(dve.scalar_tensor_tensor(tabi[:, 0, :], tf[:], float(P), row[:], ALU.mult, ALU.add))
            assert count[0] == KT, count

            for par in range(2):
                dve.wait_ge(scat[par], 16 * SC * NC // 2)
            dve.memset(pads, 0.0).then_inc(pad_done, 1)
            dve.wait_ge(pad_done, 1)
            dve.tensor_copy(pads[:, :, D + 1], qi[:]).then_inc(pad_done, 1)

            dve.wait_ge(w_in, 16 * (5 + KD))

            def tile_step(s, slot):
                par = slot % 2
                if real(s - 1):
                    t = s - 1
                    e = dve.value_load(tabi[0:1, 1, bass.ds(t, 1)], min_val=0, max_val=E - 1)
                    wait(dve, h_full, 1, t, 1)
                    wait(dve, h_turned, 1, t, -1)
                    dve.tensor_tensor(hb[:, 1 - par, :], ps_h[:, 1 - par, :], b1b[:, bass.ds(e * F, F)], ALU.add
                                      ).then_inc(h_done, 1)
                if real(s - 3):
                    t = s - 3
                    e = dve.value_load(tabi[0:1, 1, bass.ds(t, 1)], min_val=0, max_val=E - 1)
                    wait_slot(dve, t_out[1 - par], t, 2, 1 - par, more=-1)
                    wait(dve, x_copied, 1, t, 1)
                    dve.tensor_copy(idx[:, 1 - par, :], meta[:, (slot + 1) % RING, 1:]).then_inc(idx_done, 1)
                    wait(dve, o_full, 1, t, 1)
                    wait(dve, o_weighed, 1, t, -1)
                    dve.tensor_tensor(ot[:, 1 - par, :], ps_o[:, 1 - par, 0:D], b2b[:, bass.ds(e * D, D)], ALU.add
                                      ).then_inc(o_done, 1)

            tiles(dve, tile_step)

            def combine(c, par):
                wait(dve, summed, 2, c, 1)
                dve.tensor_tensor(ee[:, par, 0], ee[:, par, 0], at(xn, c), ALU.add).then_inc(summed, 1)
                wait(dve, summed, 2, c, 2)
                for i in range(NT):
                    ins = dve.bn_stats(st[:, par, i, :], ee[:, par, 0, i, :])
                ins.then_inc(c_stat, 1)
                wait_apart(dve, passed, [(c_stat, 2, c, 1)])
                for i in range(NT):
                    ins = dve.bn_aggr(mv[:, par, i, :], st[:, par, i, :])
                ins.then_inc(c_stat, 1)
                wait(dve, c_stat, 2, c, 2)
                for i in range(NT):
                    ins = dve.scalar_tensor_tensor(ee[:, par, 1, i, :], ee[:, par, 0, i, :], mv[:, par, i, 0:1],
                                                   gm[:], ALU.subtract, ALU.mult)
                ins.then_inc(scaled, 1)

            def finish(c, par):
                wait(dve, scaled, 1, c, 1)
                wait(dve, c_rs, 2, c, 2)
                wait(dve, biased, 1, c, 1)
                for i in range(NT):
                    ins = dve.scalar_tensor_tensor(x1[:, par, i, :], ee[:, par, 1, i, :], rs[:, par, i:i + 1],
                                                   x1[:, par, i, :], ALU.mult, ALU.add)
                ins.then_inc(done, 1)

            def both_steps(c, par):
                combine(c, par)
                finish(c, par)

            chunks(dve, both_steps)

        @block.gpsimd
        def _(pool):
            pool.iota(ji[:], pattern=[[P, T]], base=0, channel_multiplier=0).then_inc(made, 1)
            pool.iota(ti[:], pattern=[[1, NTT]], base=0, channel_multiplier=0).then_inc(made, 1)
            pool.iota(pi[:], pattern=[[0, 1]], base=0, channel_multiplier=1).then_inc(made, 1)
            pool.iota(idi[:].rearrange("p k t -> p (k t)"), pattern=[[P, 2 * T]], base=0, channel_multiplier=1
                      ).then_inc(made, 1)
            pool.iota(qi[:], pattern=[[P, PADS]], base=2 * T * P, channel_multiplier=1).then_inc(made, 1)
            pool.wait_ge(mem, 2)
            pool.affine_select(out=ident[:], in_=ident[:], compare_op=ALU.is_equal, fill=0.0, base=0,
                               pattern=[[-1, P]], channel_multiplier=1).then_inc(made, 1)
            pool.affine_select(out=below[:], in_=below[:], compare_op=ALU.is_ge, fill=0.0, base=-1,
                               pattern=[[1, P]], channel_multiplier=-1).then_inc(made, 1)
            pool.wait_ge(mem, 4)

            def inv_std(c, par, stat, rs_done):
                wait_apart(pool, passed, [(stat, 2, c, 2)])
                pool.tensor_scalar(ve[:, par, :], mv[:, par, :, 1], EPS, None, ALU.add).then_inc(rs_done, 1)
                wait(pool, rs_done, 2, c, 1)
                pool.tensor_tensor(rs[:, par, :], ve[:, par, :], mhalf[:], ALU.pow).then_inc(rs_done, 1)

            def scatter(j, q):
                wait_apart(pool, passed, [(step, KR, j, KR), (staged, GC, j, q + 1)])
                for i in range(NT):
                    for k in range(2):
                        pool.indirect_dma_start(
                            out=xs_dram,
                            out_offset=bass.IndirectOffsetOnAxis(ap=sli[:, k, q * NT + i:q * NT + i + 1], axis=0),
                            in_=stage[:, q % 2, k, i, :], in_offset=None).then_inc(scat[q % 2], 16)

            def group(j):
                for q in range(GC):
                    inv_std(j * GC + q, q % 2, stat, rs_done)
                    if not isinstance(j, int) or j > 0:
                        scatter(j - 1, q)

            groups(pool, group)
            for q in range(GC):
                scatter(NG - 1, q)
            pool.wait_ge(tabs, 3)
            pool.wait_ge(pad_done, 2)
            pool.engine_nop().then_inc(pad_done, 1)
            for e in range(E):
                pool.indirect_dma_start(
                    out=xs_dram, out_offset=bass.IndirectOffsetOnAxis(ap=padi[:, e:e + 1], axis=0),
                    in_=pads[:, e, :], in_offset=None).then_inc(pad_scat, 16)

            def store_tile(s, slot):
                if real(s - 3):
                    t, par = s - 3, slot % 2
                    wait_apart(pool, passed, [(o_weighed, 1, t, 1), (idx_done, 1, t, 1)])
                    pool.indirect_dma_start(
                        out=eo_dram, out_offset=bass.IndirectOffsetOnAxis(ap=idx[:, 1 - par, :], axis=0),
                        in_=ow[:, 1 - par, :], in_offset=None).then_inc(t_out[1 - par], 16)

            tiles(pool, store_tile)

            pool.wait_ge(w_in, 16 * (5 + KD))

            def combine(c, par):
                wait_slot(pool, c_in[par], c, 2, par, per=16 * LD)
                pool.tensor_tensor(ee[:, par, 0], ee[:, par, 0], ee[:, par, 1], ALU.add).then_inc(summed, 1)
                for i in range(NT):
                    ins = pool.tensor_tensor(x1[:, par, i, :], x1[:, par, i, :], bt[:], ALU.add)
                ins.then_inc(biased, 1)
                inv_std(c, par, c_stat, c_rs)

            chunks(pool, combine)

        @block.scalar
        def _(act):
            for k in range(KD):
                act.dma_start(w1[:, k, :].rearrange("p (e f) -> p e f", e=E),
                              W1[:, k * P:(k + 1) * P, :].rearrange("e p f -> p e f")).then_inc(w_in, 16)
            act.dma_start(w2[:].rearrange("p (e k d) -> p e k d", e=E, k=KF),
                          W2.rearrange("e (k p) d -> p e k d", p=P)).then_inc(w_in, 16)
            act.dma_start(b1b[:], b1.rearrange("e f -> (e f)").partition_broadcast(P)).then_inc(w_in, 16)
            act.dma_start(b2b[:], b2.rearrange("e d -> (e d)").partition_broadcast(P)).then_inc(w_in, 16)
            act.dma_start(gm[:], gamma.partition_broadcast(P)).then_inc(w_in, 16)
            act.dma_start(bt[:], beta.partition_broadcast(P)).then_inc(w_in, 16)
            act.wait_ge(mem, 9 + 2 * E)

            def stage_rows(j, q):
                par, c = q % 2, j * GC + q
                if q == 0:
                    wait(act, step, KR, j, KR)
                wait(act, kept, 1, c, 1)
                wait_slot(act, scat[par], c, 2, par, per=16 * SC, more=-1)
                for k in range(2):
                    act.copy(stage[:, par, k, :, 0:D], at(xn, c))
                act.copy(stage[:, par, :, :, D], wt[:, :, q * NT:(q + 1) * NT])
                act.copy(stage[:, par, :, :, D + 1], idf[:, :, bass.ds(c * NT, NT)]).then_inc(staged, 1)

            def group(j):
                for q in range(GC):
                    c = j * GC + q
                    if not isinstance(j, int) or j > 0:
                        stage_rows(j - 1, q)
                    wait(act, xn_done, 1, c, 1)
                    act.copy(at(xn, c), x1[:, q % 2]).then_inc(kept, 1)
                    for k in range(KD):
                        wait(act, turned, KD, c, k + 1)
                        if k == 0:
                            wait(act, logit, 1, c, 0)
                        act.copy(rT[:, k, :], ps_x[:, k, :]).then_inc(copied, 1)
                wait(act, step, KR, j, 12)
                act.activation(ex, ex, ACT.Exp).then_inc(e_done, 1)

            groups(act, group)
            for q in range(GC):
                stage_rows(NG - 1, q)

            def tile_step(s, slot):
                par = slot % 2
                if real(s):
                    wait(act, x_turned, 1, s, 1)
                    wait(act, idx_done, 1, s, 1 - RING)
                    wait(act, o_weighed, 1, s, 1 - RING)
                    act.copy(meta[:, slot, :], xt[:, slot, D:])
                    wait(act, h_full, 1, s, -1)
                    act.copy(xT[:, par, :], ps_x[:, par, 0:KD * P]).then_inc(x_copied, 1)
                if real(s - 2):
                    t = s - 2
                    wait(act, h_turned, 1, t, 1)
                    wait(act, o_full, 1, t, -1)
                    act.activation(hT[:, par, :], ps_t[:, par, :], ACT.Relu).then_inc(h_relu, 1)
                if real(s - 3):
                    t = s - 3
                    wait(act, o_done, 1, t, 1)
                    wait_slot(act, t_out[1 - par], t, 2, 1 - par, more=-1)
                    wait(act, x_copied, 1, t, 1)
                    act.mul(ow[:, 1 - par, :], ot[:, 1 - par, :], meta[:, (slot + 1) % RING, 0:1]
                            ).then_inc(o_weighed, 1)

            act.wait_ge(tabs, KT)
            tiles(act, tile_step)

            def store(c, par):
                wait(act, done, 1, c, 1)
                act.dma_start(rows_of(out_t, c), x1[:, par]).then_inc(o_out[par], 16)

            chunks(act, store)
            for par in range(2):
                act.wait_ge(o_out[par], 16 * NC // 2)

        @block.tensor
        def _(pe):
            pe.wait_ge(r_in, 32)
            pe.wait_ge(made, 7)
            pe.wait_ge(mem, 3)

            def group(j):
                for q in range(GC):
                    c = j * GC + q
                    wait(pe, xn_done, 1, c, 1)
                    for k in range(KD):
                        wait(pe, copied, KD, c, k + 1 - KD)
                        for i in range(NT):
                            ins = pe.transpose(ps_x[:, k, i * P:(i + 1) * P], x1[:, q % 2, i, k * P:(k + 1) * P],
                                               ident[:])
                        ins.then_inc(turned, 1)
                    wait(pe, copied, KD, c, KD)
                    if q == 0:
                        wait(pe, step, KR, j, 1 - KR)
                    for i in range(NT):
                        m = (q * NT + i) * E
                        for k in range(KD):
                            ins = pe.matmul(ps_l[:, m:m + E], rT[:, k, i * P:(i + 1) * P], wg[:, k, :],
                                            start=(k == 0), stop=(k == KD - 1))
                    ins.then_inc(logit, 1)
                wait(pe, step, KR, j, 11)
                pe.matmul(ps_r[:, 0:W], below[:], both.rearrange("p i e -> p (i e)"), start=True, stop=True)
                pe.matmul(ps_n[:, 0:W], ones[:], both.rearrange("p i e -> p (i e)"), start=True, stop=True
                          ).then_inc(ranked, 1)

            groups(pe, group)
            pe.wait_ge(step, KR * NG)
            pe.wait_ge(tabs, KT)
            pe.wait_ge(w_in, 16 * (5 + KD))

            def tile_step(s, slot):
                par = slot % 2
                if real(s):
                    wait_slot(pe, t_in[slot], s, RING, slot)
                    wait(pe, x_copied, 1, s, -1)
                    for k in range(KD):
                        ins = pe.transpose(ps_x[:, par, k * P:(k + 1) * P], xt[:, slot, k * P:(k + 1) * P], ident[:])
                    ins.then_inc(x_turned, 1)
                if real(s - 1):
                    t = s - 1
                    e = pe.value_load(tabi[0:1, 1, bass.ds(t, 1)], min_val=0, max_val=E - 1)
                    wait(pe, x_copied, 1, t, 1)
                    wait(pe, h_done, 1, t, -1)
                    for k in range(KD):
                        ins = pe.matmul(ps_h[:, 1 - par, :], xT[:, 1 - par, k * P:(k + 1) * P],
                                        w1[:, k, bass.ds(e * F, F)], start=(k == 0), stop=(k == KD - 1))
                    ins.then_inc(h_full, 1)
                if real(s - 2):
                    t = s - 2
                    wait(pe, h_done, 1, t, 1)
                    wait(pe, h_relu, 1, t, -1)
                    for k in range(KF):
                        ins = pe.transpose(ps_t[:, par, k * P:(k + 1) * P], hb[:, par, k * P:(k + 1) * P], ident[:])
                    ins.then_inc(h_turned, 1)
                if real(s - 3):
                    t = s - 3
                    e = pe.value_load(tabi[0:1, 1, bass.ds(t, 1)], min_val=0, max_val=E - 1)
                    wait(pe, h_relu, 1, t, 1)
                    wait(pe, o_done, 1, t, -1)
                    for k in range(KF):
                        ins = pe.matmul(ps_o[:, 1 - par, 0:D], hT[:, 1 - par, k * P:(k + 1) * P],
                                        w2[:, bass.ds((e * KF + k) * D, D)], start=(k == 0), stop=(k == KF - 1))
                    ins.then_inc(o_full, 1)

            tiles(pe, tile_step)


_INS = ['L0_attn_x', 'L0_attn_ln_g', 'L0_attn_ln_b', 'L0_attn_W_in', 'L0_attn_conv_w', 'L0_attn_conv_b',
        'L0_attn_W_xproj', 'L0_attn_W_dt', 'L0_attn_b_dt', 'L0_attn_A_log', 'L0_attn_D_param', 'L0_attn_W_out',
        'L0_ffn_Wg', 'L0_ffn_bg', 'L0_ffn_W1', 'L0_ffn_b1', 'L0_ffn_W2', 'L0_ffn_b2', 'L0_ffn_gamma',
        'L0_ffn_beta']
_OUTS = [((8, 1024, 256), 'float32')]


def kernel(**inputs):
    import numpy as _np
    import concourse.bacc as _bacc
    from concourse import mybir as _mybir
    from concourse.bass_utils import run_bass_kernel_spmd as _run

    nc = _bacc.Bacc("TRN2", target_bir_lowering=False, num_devices=1)
    arrays, args = {}, []
    for name in _INS:
        a = _np.ascontiguousarray(inputs[name])
        arrays[f"in_{name}_dram"] = a
        args.append(nc.dram_tensor(f"in_{name}_dram", a.shape, _mybir.dt.from_np(a.dtype), kind="ExternalInput").ap())
    for i, (shape, dtype) in enumerate(_OUTS):
        dt = _mybir.dt.from_np(_np.dtype(dtype))
        args.append(nc.dram_tensor(f"out_{i}_dram", shape, dt, kind="ExternalOutput").ap())
    mamba_moe_kernel(nc, *args)
    r = _run(nc, [arrays], core_ids=[0])
    got = tuple(r.results[0][f"out_{i}_dram"] for i in range(len(_OUTS)))
    return got[0]
```

```python
from contextlib import ExitStack

import concourse.bass as bass
from concourse import mybir

P = 128
CH = 512
NT = CH // P
EPS = 1e-5

ALU = mybir.AluOpType
ACT = mybir.ActivationFunctionType
AX = mybir.AxisListType
F32 = mybir.dt.float32
I32 = mybir.dt.int32
U32 = mybir.dt.uint32


def wait(eng, sem, per, c, k):
    if isinstance(c, int):
        if per * c + k > 0:
            eng.wait_ge(sem, per * c + k)
    else:
        eng.wait_ge(sem, c * per + k)


def wait_apart(eng, passed, waits):
    for sem, per, c, k in waits:
        wait(eng, sem, per, c, k)
        if not isinstance(c, int):
            eng.sem_inc(passed, 1)


def mamba_moe_kernel(nc, x, ln_g, ln_b, W_in, conv_w, conv_b, W_xproj, W_dt, b_dt, A_log, D_param, W_out,
                     Wg, bg, W1, b1, W2, b2, gamma, beta, out):
    B, L, D = x.shape
    DI = W_in.shape[1] // 2
    G = DI // P
    KD = D // P
    N = A_log.shape[1]
    R = W_dt.shape[0]
    TAPS = conv_w.shape[2]
    HALO = TAPS - 1
    NC = B * L // CH
    assert L == 2 * CH and NC % 2 == 0 and NT == 4 and G == 4 and KD == 2 and R + 2 * N == 96

    xf = x.rearrange("b l d -> (b l) d")
    x_t = xf.rearrange("(c i p) d -> c p i d", p=P, i=NT)
    x1_dram = nc.dram_tensor("x1_scratch", (B * L, D), F32, kind="Internal").ap()
    x1_t = x1_dram.rearrange("(c i p) d -> c p i d", p=P, i=NT)
    b_dram = nc.dram_tensor("b_scratch", (2, N, CH), F32, kind="Internal").ap()

    mamba_block(nc, x_t, x1_t, b_dram, ln_g, ln_b, W_in, conv_w, conv_b, W_xproj, W_dt, b_dt, A_log, D_param,
                W_out, NC, D, DI, G, KD, N, R, TAPS, HALO)
    moe_block(nc, x1_t, out.rearrange("b l d -> (b l) d").rearrange("(c i p) d -> c p i d", p=P, i=NT),
              Wg, bg, W1, b1, W2, b2, gamma, beta, NC, D, KD)


def mamba_block(nc, x_t, x1_t, b_dram, ln_g, ln_b, W_in, conv_w, conv_b, W_xproj, W_dt, b_dt, A_log, D_param,
                W_out, NC, D, DI, G, KD, N, R, TAPS, HALO):
    NB = 8
    K_DT = 97
    SG = N * G
    with ExitStack() as ctx:
        def sb(name, shape):
            return ctx.enter_context(nc.sbuf_tensor(name, shape, F32))

        def sem(name):
            return ctx.enter_context(nc.semaphore(name))

        ident = sb("ident", [P, P])
        win = sb("win", [P, KD, 2 * DI])
        wxp = sb("wxp", [P, G, R + 2 * N])
        wdt = sb("wdt", [K_DT, DI])
        wout = sb("wout", [P, G, D])
        a_neg = sb("a_neg", [P, G, N])
        cw = sb("cw", [P, G, TAPS])
        cb = sb("cb", [P, G])
        dp = sb("dp", [P, G])
        lng = sb("lng", [P, KD])
        lnb = sb("lnb", [P, KD])
        taps = sb("taps", [P, G, TAPS, P])
        xb = sb("xb", [P, 2, NT, D])
        xl = sb("xl", [P, 2, NT, D])
        xn = sb("xn", [P, NT, D])
        h0 = sb("h0", [P, NT, D])
        st = sb("st", [P, 2, NT, 6])
        mv = sb("mv", [P, 2, NT, 2])
        ve = sb("ve", [P, 2, NT])
        rs = sb("rs", [P, 2, NT])
        mhalf = sb("mhalf", [P, NT])
        hT = sb("hT", [P, KD, CH])
        xin = sb("xin", [P, G, HALO + CH])
        zs = sb("zs", [P, 2, G, CH])
        xc = sb("xc", [P, 2, G, CH])
        dbc = sb("dbc", [K_DT, CH])
        cT = sb("cT", [P, 2, NT, N])
        sp = sb("sp", [P, G, CH])
        dl = sb("dl", [P, 2, G, CH])
        du = sb("du", [P, 2, G, CH])
        bb = sb("bb", [P, NB, CH])
        dbu = sb("dbu", [P, 2, G, CH])
        ss = sb("ss", [P, 2, G, CH])
        carry = sb("carry", [P, N, G])
        ya = sb("ya", [P, 2, NT, DI])
        yg = sb("yg", [P, G, CH])
        ps_a = ctx.enter_context(nc.psum_tensor("ps_a", [P, G, CH], F32))
        ps_s = ctx.enter_context(nc.psum_tensor("ps_s", [P, 2, DI], F32))
        ps_p = ctx.enter_context(nc.psum_tensor("ps_p", [P, 2, CH], F32))

        passed = sem("passed")
        w_in = sem("weights_loaded")
        zeroed = sem("zeroed")
        id_done = sem("identity_done")
        a_exp = sem("a_exp")
        const_done = sem("constants_done")
        x_in = [sem(f"x_loaded{i}") for i in range(2)]
        ln_step = sem("ln_step")
        rs_done = sem("rs_done")
        xl_done = sem("xl_done")
        proj_full = sem("proj_full")
        proj_act = sem("proj_evacuated_act")
        halo = sem("halo_set")
        u_done = sem("u_done")
        silu_z = sem("silu_z_done")
        sp_step = sem("softplus_step")
        sp_log = sem("softplus_log")
        dl_done = sem("delta_done")
        b_out = sem("b_stored")
        bb_in = [sem(f"b_row_loaded{i}") for i in range(NB)]
        du_done = sem("du_done")
        exp_done = sem("exp_done")
        dbu_done = sem("dbu_done")
        scan_done = sem("scan_done")
        carry_done = sem("carry_done")
        tr_done = sem("states_turned")
        sum_done = sem("sum_done")
        post_full = sem("post_full")
        post_dve = sem("post_evacuated")
        gate_done = sem("gate_done")
        x1_out = [sem(f"x1_stored{i}") for i in range(2)]

        NW = 11
        LAG = 3
        USES = [("h", 0, 0), ("h", 1, 0), ("x", 0, 1), ("x", 1, 2), ("x", 2, 6), ("x", 3, 7),
                ("conv", 0, 8), ("conv", 1, 10), ("conv", 2, 12), ("conv", 3, 14), ("dbc", 0, 20), ("c", 0, 22),
                ("dt", 0, 22), ("dt", 1, 23), ("dt", 2, 24), ("dt", 3, 25),
                ("z", 0, 26), ("z", 1, 27), ("z", 2, 28), ("z", 3, 29)]
        PARTS = {"conv": 2, "dbc": 2}
        SILU_U, SILU_Z = 20, 16
        LOG = 29
        ADD_LOG = 27
        BACK = (3, 5)
        SKIP = (4, 6)
        W_OUT = 16
        RESIDUAL = (19, 21)
        NORM = (15, 25, 29)
        ADD_X = 12
        GATE = (3, 4)
        U_ALL = len(USES)

        def nth(kind, g=0):
            return [u[:2] for u in USES].index((kind, g)) + 1

        block = ctx.enter_context(nc.Block())

        def iterations(eng, body):
            for c in range(3):
                body(c, c % 2)
            with eng.Fori(1, (NC - 4) // 2) as i:
                body(i * 2 + 1, 1)
                body(i * 2 + 2, 0)
            for c in range(NC - 3, NC):
                body(c, c % 2)

        def there(c, d):
            return not isinstance(c, int) or 0 <= c + d < NC

        @block.sync
        def _(sync):
            def load_x(q, par):
                wait_apart(sync, passed, [(xl_done, 1, q, -1)])
                sync.dma_start(xb[:, par], x_t[q] if isinstance(q, int) else
                               x_t[bass.ds(q, 1)].rearrange("c p i d -> (c p) i d")).then_inc(x_in[par], 16)

            def store_b(q, par):
                wait(sync, proj_act, U_ALL, q, nth("dbc"))
                for s in range(NB):
                    wait(sync, bb_in[s], 16 * (N // NB), q, -16 * (N // NB))
                sync.dma_start(b_dram[par], dbc[R:R + N, :]).then_inc(b_out, 16)

            def load_row(c, par, n):
                if n == 0:
                    wait(sync, b_out, 16, c, 16)
                wait(sync, dbu_done, SG, c, (n - NB + 1) * G)
                sync.dma_start(bb[:, n % NB], b_dram[par, n, :].partition_broadcast(P)).then_inc(bb_in[n % NB], 16)

            def store_x1(q, par):
                wait_apart(sync, passed, [(post_dve, 6, q, 6)])
                sync.dma_start(x1_t[q] if isinstance(q, int) else
                               x1_t[bass.ds(q, 1)].rearrange("c p i d -> (c p) i d"), xl[:, par]
                               ).then_inc(x1_out[par], 16)

            load_x(0, 0)
            for dst, src in (
                (win[:], W_in.rearrange("(k p) n -> p k n", p=P)),
                (lng[:], ln_g.rearrange("(k p) -> p k", p=P)),
                (lnb[:], ln_b.rearrange("(k p) -> p k", p=P)),
                (cw[:], conv_w.rearrange("(g p) o k -> p g (o k)", p=P)),
                (cb[:], conv_b.rearrange("(g p) -> p g", p=P)),
                (wxp[:], W_xproj.rearrange("(g p) n -> p g n", p=P)),
                (wdt[0:R, :], W_dt),
                (wdt[K_DT - 1:K_DT, :], b_dt.rearrange("(a n) -> a n", a=1)),
                (a_neg[:], A_log.rearrange("(g p) n -> p g n", p=P)),
                (dp[:], D_param.rearrange("(g p) -> p g", p=P)),
                (wout[:], W_out.rearrange("(g p) n -> p g n", p=P)),
            ):
                with nc.allow_non_contiguous_dma(reason="small weights"):
                    sync.dma_start(dst, src).then_inc(w_in, 16)
            load_x(1, 1)
            store_b(0, 0)

            def body(c, par):
                if there(c, 2):
                    load_x(c + 2, par)
                for n in range(N):
                    load_row(c, par, n)
                    if n == 12:
                        if there(c, -1):
                            store_x1(c - 1, 1 - par)
                if there(c, 1):
                    store_b(c + 1, 1 - par)

            iterations(sync, body)
            store_x1(NC - 1, 1)
            for par in range(2):
                sync.wait_ge(x1_out[par], 16 * NC // 2)

        @block.vector
        def _(dve):
            dve.memset(ident[:], 1.0).then_inc(zeroed, 1)
            dve.memset(mhalf[:], -0.5).then_inc(zeroed, 1)
            dve.memset(wdt[R:R + 2 * N, :], 0.0).then_inc(zeroed, 1)
            dve.memset(dbc[K_DT - 1:K_DT, :], 1.0).then_inc(zeroed, 1)

            def stats(q, src, row):
                for i in range(NT):
                    ins = dve.bn_stats(st[:, row, i, :], src[:, i, :])
                ins.then_inc(ln_step, 1)
                wait_apart(dve, passed, [(ln_step, 6, q, 3 * row + 1)])
                for i in range(NT):
                    ins = dve.bn_aggr(mv[:, row, i, :], st[:, row, i, :])
                ins.then_inc(ln_step, 1)

            def normalise(q, src, dst, row):
                wait(dve, rs_done, 4, q, 2 * row + 2)
                for i in range(NT):
                    ins = dve.tensor_scalar(dst[:, i, :], src[:, i, :], mv[:, row, i, 0:1], rs[:, row, i:i + 1],
                                            ALU.subtract, ALU.mult)
                ins.then_inc(ln_step, 1)

            def norm_a(q, par):
                if isinstance(q, int):
                    dve.wait_ge(x_in[par], 16 * (q // 2 + 1))
                else:
                    wait(dve, x_in[par], 8, q, 8 if par else 16)
                stats(q, xb[:, par], 0)

            def norm_b(q, par):
                wait(dve, xl_done, 1, q, 0)
                normalise(q, xb[:, par], xn, 0)
                wait(dve, ln_step, 6, q, 3)
                stats(q, xn, 1)

            def norm_c(q, par):
                wait(dve, proj_full, U_ALL, q, nth("h", 1) - U_ALL)
                normalise(q, xn, h0, 1)

            def add_log(q, par):
                wait(dve, sp_log, 1, q, 1)
                dve.tensor_tensor(dl[:, par], dl[:, par], sp[:], ALU.add).then_inc(dl_done, 1)

            def scans(c, par, n, groups):
                for g in groups:
                    k = n * G + g
                    wait(dve, exp_done, SG, c, k + 1)
                    wait(dve, dbu_done, SG, c, k + 1)
                    if g == 0:
                        wait(dve, tr_done, N * NT, c, (n - 1) * NT)
                        if par == 1 and n == 0:
                            wait(dve, carry_done, N // 2, c, N // 2)
                    init = carry[:, n, g:g + 1] if par else 0.0
                    dve.tensor_tensor_scan(ss[:, n % 2, g, :], ps_a[:, g, :], dbu[:, n % 2, g, :], init,
                                           ALU.mult, ALU.add).then_inc(scan_done, 1)

            def save(c, n):
                wait(dve, scan_done, SG, c, n * G + G)
                dve.tensor_copy(carry[:, n, :], ss[:, n % 2, :, CH - 1]).then_inc(carry_done, 1)

            def sums(c, par, n, tiles):
                for i in tiles:
                    k = n * NT + i
                    wait(dve, tr_done, N * NT, c, k + 1)
                    if n == 0:
                        if i == 0:
                            wait(dve, proj_act, U_ALL, c, nth("c"))
                            wait(dve, post_full, 6, c, -6)
                        dve.tensor_scalar(ya[:, par, i, :], ps_s[:, k % 2, :], cT[:, par, i, n:n + 1], None,
                                          ALU.mult).then_inc(sum_done, 1)
                    else:
                        wait(dve, sum_done, N * NT, c, k - NT + 1)
                        dve.scalar_tensor_tensor(ya[:, par, i, :], ps_s[:, k % 2, :], cT[:, par, i, n:n + 1],
                                                 ya[:, par, i, :], ALU.mult, ALU.add).then_inc(sum_done, 1)

            def skip_gate(q, par, g):
                wait(dve, post_full, 6, q, g + 1)
                if g == 0:
                    wait(dve, post_full, 6, q, 0)
                dve.scalar_tensor_tensor(yg[:, g, :], xc[:, par, g, :], dp[:, g:g + 1], ps_p[:, g % 2, :],
                                         ALU.mult, ALU.add).then_inc(post_dve, 1)

            def residual(q, par, j):
                wait(dve, post_full, 6, q, 5 + j)
                wait(dve, xl_done, 1, q, 1)
                dve.tensor_tensor(xl[:, par, 2 * j:2 * j + 2, :],
                                  ps_p[:, j, :].rearrange("p (i d) -> p i d", d=D),
                                  xl[:, par, 2 * j:2 * j + 2, :], ALU.add).then_inc(post_dve, 1)

            norm_a(0, 0)
            norm_b(0, 0)
            norm_c(0, 0)
            dve.wait_ge(w_in, 16 * NW)
            dve.wait_ge(a_exp, 1)
            dve.wait_ge(id_done, 1)
            dve.tensor_scalar(a_neg[:], a_neg[:], -1.0, None, ALU.mult).then_inc(const_done, 1)
            for g in range(G):
                for k in range(TAPS):
                    ins = dve.tensor_scalar(taps[:, g, k, :], ident[:], cw[:, g, k:k + 1], None, ALU.mult)
            ins.then_inc(const_done, 1)
            norm_a(1, 1)
            norm_b(1, 1)
            norm_c(1, 1)
            add_log(0, 0)

            def body(c, par):
                for s in range(2 * N):
                    n, tiles = s // 2, (0, 1) if s % 2 == 0 else (2, 3)
                    scans(c, par, n, tiles)
                    if n > 0:
                        sums(c, par, n - 1, tiles)
                    elif there(c, -1):
                        sums(c - 1, 1 - par, N - 1, tiles)
                    if par == 0 and s % 2:
                        save(c, n)
                    if there(c, -1):
                        if s in SKIP:
                            pair = range(2 * SKIP.index(s), 2 * SKIP.index(s) + 2)
                            for g in pair:
                                skip_gate(c - 1, 1 - par, g)
                        if s in RESIDUAL:
                            residual(c - 1, 1 - par, RESIDUAL.index(s))
                    if there(c, 1):
                        if s == ADD_LOG:
                            add_log(c + 1, 1 - par)
                    if there(c, 2):
                        if s == NORM[0]:
                            norm_a(c + 2, par)
                        if s == NORM[1]:
                            norm_b(c + 2, par)
                        if s == NORM[2]:
                            norm_c(c + 2, par)

            iterations(dve, body)
            sums(NC - 1, 1, N - 1, range(NT))
            for g in range(G):
                skip_gate(NC - 1, 1, g)
            residual(NC - 1, 1, 0)
            residual(NC - 1, 1, 1)

        @block.gpsimd
        def _(pool):
            pool.wait_ge(zeroed, 1)
            pool.affine_select(out=ident[:], in_=ident[:], compare_op=ALU.is_equal, fill=0.0, base=0,
                               pattern=[[-1, P]], channel_multiplier=1).then_inc(id_done, 1)

            def times_u(q, par, g):
                if g == 0:
                    wait(pool, dl_done, 1, q, 1)
                pool.tensor_tensor(du[:, par, g, :], dl[:, par, g, :], xc[:, par, g, :], ALU.mult
                                   ).then_inc(du_done, 1)

            def times_b(c, par, n, g):
                if g == 0:
                    wait(pool, bb_in[n % NB], 16 * (N // NB), c, 16 * (n // NB + 1))
                if n == 0:
                    wait(pool, du_done, G, c, g + 1)
                wait(pool, scan_done, SG, c, (n - 2) * G + g + 1)
                pool.tensor_tensor(dbu[:, n % 2, g, :], du[:, par, g, :], bb[:, n % NB, :], ALU.mult
                                   ).then_inc(dbu_done, 1)

            def gate(q, par, g):
                wait(pool, post_dve, 6, q, g + 1)
                if g == 0:
                    wait(pool, silu_z, 1, q, 1)
                pool.tensor_tensor(yg[:, g, :], yg[:, g, :], zs[:, par, g, :], ALU.mult).then_inc(gate_done, 1)

            def add_xl(q, par):
                if isinstance(q, int):
                    if q >= 2:
                        pool.wait_ge(x1_out[par], 16 * (q // 2))
                else:
                    wait(pool, x1_out[par], 8, q, -8 if par else 0)
                wait(pool, ln_step, 6, q, 3)
                pool.tensor_tensor(xl[:, par], xb[:, par], xn[:], ALU.add).then_inc(xl_done, 1)

            def inv_std(q, row):
                wait_apart(pool, passed, [(ln_step, 6, q, 3 * row + 2)])
                pool.tensor_scalar(ve[:, row, :], mv[:, row, :, 1], EPS, None, ALU.add).then_inc(rs_done, 1)
                wait(pool, rs_done, 4, q, 2 * row + 1)
                pool.tensor_tensor(rs[:, row, :], ve[:, row, :], mhalf[:], ALU.pow).then_inc(rs_done, 1)

            pool.wait_ge(zeroed, 4)
            inv_std(0, 0)
            add_xl(0, 0)
            inv_std(0, 1)
            inv_std(1, 0)
            inv_std(1, 1)
            for g in range(G):
                times_u(0, 0, g)

            def body(c, par):
                for n in range(N):
                    for g in range(G):
                        times_b(c, par, n, g)
                    if there(c, -1) and n in GATE:
                        for g in (2 * GATE.index(n), 2 * GATE.index(n) + 1):
                            gate(c - 1, 1 - par, g)
                    if there(c, 1) and n == ADD_X:
                        add_xl(c + 1, 1 - par)
                    if there(c, 2) and n in (11, 13):
                        inv_std(c + 2, (n - 11) // 2)
                    if there(c, 1) and n == N - 1:
                        for g in range(G):
                            times_u(c + 1, 1 - par, g)

            iterations(pool, body)
            for g in range(G):
                gate(NC - 1, 1, g)

        @block.scalar
        def _(act):
            def set_halo(q, par):
                wait(act, proj_full, U_ALL, q, nth("conv", 3) - U_ALL)
                if par == 0:
                    act.memzero(xin[:, :, 0:HALO]).then_inc(halo, 1)
                else:
                    act.copy(xin[:, :, 0:HALO], xin[:, :, CH:CH + HALO]).then_inc(halo, 1)

            def empty(q, par, u):
                kind, g, _ = USES[u]
                wait(act, proj_full, U_ALL, q, u + 1)
                src = ps_p[:, u % 2, :]
                if kind == "h":
                    act.activation(hT[:, g, :], src, ACT.Identity, bias=lnb[:, g:g + 1], scale=lng[:, g:g + 1]
                                   ).then_inc(proj_act, 1)
                elif kind == "x":
                    if g == 0:
                        wait(act, halo, 1, q, 1)
                    act.copy(xin[:, g, HALO:], src).then_inc(proj_act, 1)
                elif kind == "z":
                    if g == 0:
                        wait(act, gate_done, G, q, -G)
                    act.copy(zs[:, par, g, :], src).then_inc(proj_act, 1)
                elif kind == "conv":
                    if g == 0:
                        wait(act, post_dve, 6, q, 4 - 12)
                        wait(act, du_done, G, q, -G)
                    act.activation(xc[:, par, g, :], src, ACT.Identity, bias=cb[:, g:g + 1]).then_inc(proj_act, 1)
                elif kind == "dbc":
                    wait(act, b_out, 16, q, 0)
                    act.copy(dbc[0:R + 2 * N, :], src[0:R + 2 * N, :]).then_inc(proj_act, 1)
                elif kind == "dt":
                    if g == 0:
                        wait(act, exp_done, SG, q, -SG)
                        wait(act, dl_done, 1, q, 0)
                        wait(act, du_done, G, q, -G)
                    t = sp[:, g, :]
                    act.activation(dl[:, par, g, :], src, ACT.Relu).then_inc(sp_step, 1)
                    act.activation(t, src, ACT.Abs).then_inc(proj_act, 1)
                    wait(act, proj_act, U_ALL, q, u + 1)
                    act.activation(t, t, ACT.Exp, scale=-1.0).then_inc(sp_step, 1)
                else:
                    wait(act, sum_done, N * NT, q, -N * NT)
                    act.copy(cT[:, par], src[:, 0:NT * 96].rearrange("p (i n) -> p i n", n=96)[:, :, R + N:]
                             ).then_inc(proj_act, 1)

            def log_term(q):
                wait(act, sp_step, 2 * G, q, 2 * G)
                act.activation(sp[:], sp[:], ACT.Ln, bias=1.0).then_inc(sp_log, 1)

            def silu_u(q, par):
                wait(act, proj_act, U_ALL, q, nth("conv", 3))
                act.activation(xc[:, par], xc[:, par], ACT.Silu).then_inc(u_done, 1)

            def silu_gate(q, par):
                wait(act, proj_act, U_ALL, q, nth("z", 3))
                act.activation(zs[:, par], zs[:, par], ACT.Silu).then_inc(silu_z, 1)

            def exps(c, par, n, groups):
                for g in groups:
                    wait(act, scan_done, SG, c, (n - 1) * G + g + 1)
                    act.activation(ps_a[:, g, :], dl[:, par, g, :], ACT.Exp, scale=a_neg[:, g, n:n + 1]
                                   ).then_inc(exp_done, 1)

            act.wait_ge(w_in, 16 * NW)
            act.activation(a_neg[:], a_neg[:], ACT.Exp).then_inc(a_exp, 1)
            set_halo(0, 0)
            for u, (kind, g, _) in enumerate(USES):
                empty(0, 0, u)
                if (kind, g) == ("conv", 3):
                    silu_u(0, 0)
                if (kind, g) == ("dt", 3):
                    log_term(0)
            act.wait_ge(const_done, 1)

            def pieces(c, par, s):
                if s == SILU_U and there(c, 1):
                    silu_u(c + 1, 1 - par)
                if s == SILU_Z:
                    silu_gate(c, par)
                if s == LOG and there(c, 1):
                    log_term(c + 1)
                for u, (kind, g, at) in enumerate(USES):
                    if at + PARTS.get(kind, 1) - 1 + LAG == s and there(c, 1):
                        if u == 0:
                            set_halo(c + 1, 1 - par)
                        empty(c + 1, 1 - par, u)

            def body(c, par):
                for s in range(2 * N):
                    pieces(c, par, s)
                    if s == 0:
                        wait(act, dl_done, 1, c, 1)
                    exps(c, par, s // 2, (0, 1) if s % 2 == 0 else (2, 3))
                pieces(c, par, 2 * N)

            iterations(act, body)

        @block.tensor
        def _(pe):
            def project(q, par, u, part, parts, post):
                kind, g, _ = USES[u]
                if part == 0:
                    if post and u in (nth("x", 2) - 1, nth("x", 3) - 1):
                        wait(pe, post_dve, 6, q, 3 + g - 2 - 12)
                    elif post and u in (nth("dbc") - 1, nth("c") - 1):
                        wait(pe, post_dve, 6, q, 5 + (kind == "c") - 12)
                    else:
                        wait(pe, proj_act, U_ALL, q, u - 1)
                dst = ps_p[:, u % 2, :]
                if kind == "h":
                    if g == 0:
                        wait(pe, ln_step, 6, q, 6)
                    for i in range(NT):
                        ins = pe.transpose(dst[:, i * P:(i + 1) * P], h0[:, i, g * P:(g + 1) * P], ident[:])
                elif kind in "xz":
                    if (kind, g) == ("x", 0):
                        wait(pe, proj_act, U_ALL, q, nth("h", 1))
                    m = g * P + (DI if kind == "z" else 0)
                    for k in range(KD):
                        ins = pe.matmul(dst, win[:, k, m:m + P], hT[:, k, :], start=(k == 0), stop=(k == KD - 1))
                elif kind == "conv":
                    if part == 0:
                        wait(pe, proj_act, U_ALL, q, nth("x", g))
                    for k in range(TAPS * part // parts, TAPS * (part + 1) // parts):
                        ins = pe.matmul(dst, taps[:, g, k, :], xin[:, g, k:k + CH],
                                        start=(k == 0), stop=(k == TAPS - 1))
                elif kind == "dbc":
                    if part == 0:
                        wait(pe, u_done, 1, q, 1)
                    for k in range(G * part // parts, G * (part + 1) // parts):
                        ins = pe.matmul(dst[0:96, :], wxp[:, k, :], xc[:, par, k, :],
                                        start=(k == 0), stop=(k == G - 1))
                elif kind == "dt":
                    ins = pe.matmul(dst, wdt[:, g * P:(g + 1) * P], dbc[:], start=True, stop=True)
                else:
                    wait(pe, proj_act, U_ALL, q, nth("dbc"))
                    for i in range(NT):
                        ins = pe.transpose(dst[:, i * 96:(i + 1) * 96], dbc[0:96, i * P:(i + 1) * P],
                                           ident[0:96, 0:96])
                if part == parts - 1:
                    ins.then_inc(proj_full, 1)

            def turn(c, par, n, tiles):
                if 0 in tiles:
                    wait(pe, scan_done, SG, c, n * G + G)
                for i in tiles:
                    k = n * NT + i
                    wait(pe, sum_done, N * NT, c, k - 1)
                    for g in range(G):
                        ins = pe.transpose(ps_s[:, k % 2, g * P:(g + 1) * P], ss[:, n % 2, g, i * P:(i + 1) * P],
                                           ident[:])
                    ins.then_inc(tr_done, 1)

            def turn_back(q, par, g, taken):
                if g == 0:
                    wait(pe, sum_done, N * NT, q, N * NT)
                wait(pe, *taken)
                for i in range(NT):
                    ins = pe.transpose(ps_p[:, g % 2, i * P:(i + 1) * P], ya[:, par, i, g * P:(g + 1) * P], ident[:])
                ins.then_inc(post_full, 1)

            def project_out(q, i, taken):
                j = i // 2
                if i == 0:
                    wait(pe, gate_done, G, q, G)
                if i % 2 == 0:
                    wait(pe, *taken)
                for g in range(G):
                    ins = pe.matmul(ps_p[:, j, (i % 2) * D:(i % 2 + 1) * D], yg[:, g, i * P:(i + 1) * P],
                                    wout[:, g, :], start=(g == 0), stop=(g == G - 1))
                if i % 2:
                    ins.then_inc(post_full, 1)

            pe.wait_ge(w_in, 16 * NW)
            pe.wait_ge(zeroed, 4)
            pe.wait_ge(id_done, 1)
            for u in range(U_ALL):
                if u == nth("conv", 0) - 1:
                    pe.wait_ge(const_done, 2)
                project(0, 0, u, 0, 1, False)

            def body(c, par):
                post, proj = there(c, -1), there(c, 1)
                for s in range(2 * N):
                    if post and s == BACK[0]:
                        for g in range(2):
                            turn_back(c - 1, 1 - par, g,
                                      (proj_act, U_ALL, c, U_ALL + nth("x", g) if proj else U_ALL - 1 + g))
                    if post and s == BACK[1]:
                        for g in range(2, 4):
                            turn_back(c - 1, 1 - par, g, (post_dve, 6, c - 1, g - 1))
                    if post and W_OUT <= s < W_OUT + NT:
                        j = (s - W_OUT) // 2
                        project_out(c - 1, s - W_OUT, (proj_act, U_ALL, c, U_ALL + nth("conv", 2 + j)) if proj else
                                    (post_dve, 6, c - 1, 3 + j))
                    for u, (kind, _, at) in enumerate(USES):
                        parts = PARTS.get(kind, 1)
                        if at <= s < at + parts and proj:
                            project(c + 1, 1 - par, u, s - at, parts, post)
                    turn(c, par, s // 2, (0, 1) if s % 2 == 0 else (2, 3))

            iterations(pe, body)
            for g in range(G):
                turn_back(NC - 1, 1, g, (post_dve, 6, NC - 1, g - 1))
            for i in range(NT):
                project_out(NC - 1, i, (post_dve, 6, NC - 1, 3 + i // 2))


def rows_of(t, c):
    return t[c] if isinstance(c, int) else t[bass.ds(c, 1)].rearrange("c p i d -> (c p) i d")


def wait_slot(eng, sem, t, ring, slot, per=16, more=0):
    if isinstance(t, int):
        v = per * (t // ring + 1 + more)
        if v > 0:
            eng.wait_ge(sem, v)
    else:
        wait(eng, sem, per // ring, t, per * (1 + more) - per // ring * slot)


def moe_block(nc, x1_t, out_t, Wg, bg, W1, b1, W2, b2, gamma, beta, NC, D, KD):
    E = Wg.shape[1]
    F = W1.shape[2]
    KF = F // P
    GC = 4
    XR = 4
    NG = NC // GC
    GT = GC * NT
    T = NC * NT
    XW = D + 2
    REG = (T + 1) * P
    NTT = 2 * T + E - 1
    LAG = 3
    RING = 4
    PEEL = LAG + 2 + (NTT - LAG - 2) % RING
    PADS = E + NTT - 2 * T
    KR = 22
    KT = 11
    SC = 2 * NT
    NOWHERE = 1e9
    xs_dram = nc.dram_tensor("xs_scratch", (E * REG + (PADS - E) * P, XW), F32, kind="Internal").ap()
    eo_dram = nc.dram_tensor("eo_scratch", ((2 * T + NTT) * P, D), F32, kind="Internal").ap()
    eo_t = eo_dram[0:2 * T * P, :].rearrange("(k c i p) d -> k c p i d", k=2, i=NT, p=P)
    with ExitStack() as ctx:
        def sb(name, shape, dt=F32):
            return ctx.enter_context(nc.sbuf_tensor(name, shape, dt))

        def sem(name):
            return ctx.enter_context(nc.semaphore(name))

        ident = sb("e_ident", [P, P])
        below = sb("below", [P, P])
        ones = sb("ones", [P, P])
        wg = sb("wg", [P, KD, E])
        bgb = sb("bgb", [P, E])
        w1 = sb("w1", [P, KD, E * F])
        w2 = sb("w2", [P, E * KF * D])
        b1b = sb("b1b", [P, E * F])
        gm, bt = b1b[:, 0:D], b1b[:, D:2 * D]
        b2b = sb("b2b", [P, E * D])
        mhalf = sb("r_mhalf", [P, NT])
        xn = sb("r_xn", [P, NC, NT, D])
        x1 = sb("r_x1", [P, XR, NT, D])
        big = sb("big", [P, 4 * NT * XW])
        st = sb("r_st", [P, 2, NT, 6])
        mv = sb("r_mv", [P, 2, NT, 2])
        ve = sb("r_ve", [P, 2, NT])
        rs = sb("r_rs", [P, 2, NT])
        idf = sb("idf", [P, 2, NC * NT])
        run = sb("run", [P, E])
        reg = sb("reg", [P, E])
        tabi = sb("tabi", [P, 2, NTT], I32)
        sli = sb("sli", [P, 2, GT], U32)
        wt = sb("wt", [P, 2, GT])
        xt = sb("xt", [P, RING, XW])
        meta = sb("meta", [P, RING, 2])
        idx = sb("idx", [P, 2, 1], U32)
        pool_a = sb("tiles", [P, 2 * (KD * P + D + D)])
        pool_b = sb("hidden", [P, 2 * 2 * F])
        xT = pool_a[:, 0:2 * KD * P].rearrange("p (b n) -> p b n", b=2)
        ot = pool_a[:, 2 * KD * P:2 * KD * P + 2 * D].rearrange("p (b n) -> p b n", b=2)
        ow = pool_a[:, 2 * KD * P + 2 * D:].rearrange("p (b n) -> p b n", b=2)
        hb = pool_b[:, 0:2 * F].rearrange("p (b n) -> p b n", b=2)
        hT = pool_b[:, 2 * F:].rearrange("p (b n) -> p b n", b=2)
        W = GT * E
        lg, eq, cn, slot, both, first, cum, excl = (pool_a[:, j * W:(j + 1) * W].rearrange("p (i e) -> p i e", e=E)
                                                    for j in range(8))
        sel = pool_a[:, 8 * W:10 * W].rearrange("p (k i e) -> p k i e", k=2, e=E)
        pick = pool_a[:, 10 * W:12 * W].rearrange("p (k i e) -> p k i e", k=2, e=E)
        rT = pool_b[:, 0:KD * CH].rearrange("p (k n) -> p k n", k=KD)
        tot, start = (pool_b[:, KD * CH + j * W:KD * CH + (j + 1) * W].rearrange("p (e i) -> p e i", e=E)
                      for j in range(2))
        small = pool_b[:, KD * CH + 2 * W:]
        mx = small[:, 0:2 * GT].rearrange("p (k i) -> p k i", k=2)
        ex = small[:, 2 * GT:3 * GT]
        den = small[:, 3 * GT:4 * GT]
        slf = small[:, 4 * GT:6 * GT].rearrange("p (k i) -> p k i", k=2)
        pad = small[:, 6 * GT:6 * GT + XW]
        xflat = x1[:].rearrange("p b i d -> p (b i d)")
        over = xflat[:, 0:E * T].rearrange("p (e t) -> p e t", e=E)
        cmp = xflat[:, E * T:E * (T + NTT)].rearrange("p (t e) -> p t e", e=E)
        tf, eid, row = (xflat[:, E * (T + NTT) + k * NTT:E * (T + NTT) + (k + 1) * NTT] for k in range(3))
        jf = xflat[:, (E + 3) * (T + NTT):(E + 3) * (T + NTT) + T]
        stage = big[:].rearrange("p (b k i w) -> p b k i w", b=2, k=2, w=XW)
        ee = big[:, 0:4 * NT * D].rearrange("p (b k i d) -> p b k i d", b=2, k=2, d=D)
        ints = sb("ints", [P, max(NTT, 2 * T)], I32)
        cnt = sb("cnt", [P, E])
        ntl = sb("ntl", [P, E])
        end = sb("end", [P, E])
        skip = sb("skip", [P, E])
        padi = sb("padi", [P, E], I32)
        aside = sb("aside", [P, NTT])

        ps_x = ctx.enter_context(nc.psum_tensor("e_ps_x", [P, 2, CH], F32))
        ps_h = ctx.enter_context(nc.psum_tensor("e_ps_h", [P, 2, F], F32))
        ps_t = ctx.enter_context(nc.psum_tensor("e_ps_t", [P, 2, F], F32))
        ps_o = ctx.enter_context(nc.psum_tensor("e_ps_o", [P, 2, CH], F32))
        ps_l, ps_r, ps_n = ps_h[:, 0, :], ps_t[:, 0, :], ps_o[:, 0, :]

        COUNTS = ((P, 2 * T, 0, 1), (P, NTT, 2 * T * P, 1), (P, T, 0, 0), (1, NTT, 0, 0))

        passed = sem("e_passed")
        counted = sem("counted")
        r_in = sem("router_loaded")
        w_in = sem("experts_loaded")
        made = sem("masks_made")
        mem = sem("memsets")
        x_in = [sem(f"m_x1_loaded{i}") for i in range(XR)]
        stat = sem("stats")
        rs_done = sem("m_rs_done")
        xn_done = sem("xn_done")
        turned = sem("xn_turned")
        copied = sem("xn_copied")
        kept = sem("xn_kept")
        logit = sem("logits_done")
        step = sem("route_step")
        e_done = sem("e_done")
        ranked = sem("ranked")
        staged = sem("rows_staged")
        scat = [sem(f"rows_scattered{i}") for i in range(2)]
        tabs = sem("table_step")
        pad_done = sem("padding_made")
        pad_out = sem("pads_stored")
        t_in = [sem(f"tile_loaded{i}") for i in range(RING)]
        x_turned = sem("x_turned")
        x_copied = sem("x_copied")
        h_full = sem("h_full")
        h_done = sem("h_done")
        h_turned = sem("h_turned")
        h_relu = sem("h_relu")
        o_full = sem("o_full")
        o_done = sem("o_done")
        o_weighed = sem("o_weighed")
        idx_done = sem("idx_done")
        t_out = [sem(f"tile_stored{i}") for i in range(2)]
        g_in = sem("gamma_beta_loaded")
        x1_in = [sem(f"c_x1_loaded{i}") for i in range(XR)]
        c_in = [sem(f"c_loaded{i}") for i in range(2)]
        o_out = [sem(f"out_stored{i}") for i in range(XR)]
        summed = sem("summed")
        c_stat = sem("c_stats")
        c_rs = sem("c_rs_done")
        scaled = sem("scaled")
        biased = sem("biased")
        done = sem("c_done")
        LD = 2

        block = ctx.enter_context(nc.Block())

        def groups(eng, body):
            body(0)
            body(1)
            with eng.Fori(2, NG - 1) as j:
                body(j)
            body(NG - 1)

        def last_group(j):
            return isinstance(j, int) and j == NG - 1

        def chunks(eng, body):
            for c in range(XR):
                body(c, c)
            with eng.Fori(1, NC // XR) as i:
                for q in range(XR):
                    body(i * XR + q, q)

        def tiles(eng, body):
            for s in range(PEEL):
                body(s, s % RING)
            with eng.Fori(0, (NTT - PEEL) // RING) as i:
                for r in range(PEEL, PEEL + RING):
                    body(i * RING + r, r % RING)
            for s in range(NTT, NTT + LAG):
                body(s, s % RING)

        def real(t):
            return not isinstance(t, int) or 0 <= t < NTT

        def at(t, c):
            return t[:, c] if isinstance(c, int) else t[:, bass.ds(c, 1)].rearrange("p c i d -> p (c i) d")

        @block.sync
        def _(sync):
            with nc.allow_non_contiguous_dma(reason="small weights"):
                sync.dma_start(wg[:], Wg.rearrange("(k p) e -> p k e", p=P)).then_inc(r_in, 16)
                sync.dma_start(bgb[:], bg.partition_broadcast(P)).then_inc(r_in, 16)

            def load_x1(j):
                for q in range(GC):
                    wait_apart(sync, passed, [(turned, KD, j * GC + q, KD - KD * XR),
                                              (kept, 1, j * GC + q, 1 - XR)])
                    sync.dma_start(x1[:, q], rows_of(x1_t, j * GC + q)).then_inc(x_in[q], 16)

            groups(sync, load_x1)

            sync.wait_ge(pad_done, 2)
            for j in range(E, PADS):
                r = E * REG + (j - E) * P
                sync.dma_start(xs_dram[r:r + P, :], pad).then_inc(pad_out, 16)
            sync.wait_ge(tabs, 2)
            for e in range(E):
                end_row = sync.value_load(padi[0:1, e:e + 1], min_val=0, max_val=E * REG - P)
                sync.dma_start(xs_dram[bass.ds(end_row, P), :], pad).then_inc(pad_out, 16)
            sync.wait_ge(pad_out, 16 * PADS)
            for par in range(2):
                sync.wait_ge(scat[par], 16 * SC * NC // 2)
            sync.wait_ge(tabs, KT)

            def load_tile(t, slot):
                off = sync.value_load(tabi[0:1, 0, bass.ds(t, 1)], min_val=0, max_val=xs_dram.shape[0] - P)
                wait_apart(sync, passed, [(x_copied, 1, t, 1 - RING)])
                sync.dma_start(xt[:, slot, :], xs_dram[bass.ds(off, P), :]).then_inc(t_in[slot], 16)

            for q in range(XR):
                sync.dma_start(x1[:, q], rows_of(x1_t, q)).then_inc(x1_in[q], 16)

            tiles(sync, lambda s, slot: load_tile(s, slot) if real(s) else None)

            sync.wait_ge(t_out[0], 16 * ((NTT + 1) // 2))
            sync.wait_ge(t_out[1], 16 * (NTT // 2))

            def load_chunk(c, q):
                par = q % 2
                wait_apart(sync, passed, [(done, 1, c, -1)])
                for k in range(2):
                    sync.dma_start(ee[:, par, k], rows_of(eo_t[k], c)).then_inc(c_in[par], 16)
                if not isinstance(c, int):
                    wait_apart(sync, passed, [(o_out[q], 16 // XR, c, -16 // XR * q)])
                    sync.dma_start(x1[:, q], rows_of(x1_t, c)).then_inc(x1_in[q], 16)

            sync.wait_ge(h_done, NTT)
            sync.dma_start(gm, gamma.partition_broadcast(P)).then_inc(g_in, 16)
            sync.dma_start(bt, beta.partition_broadcast(P)).then_inc(g_in, 16)
            chunks(sync, load_chunk)

        @block.vector
        def _(dve):
            dve.memset(ident[:], 1.0).then_inc(mem, 1)
            dve.memset(below[:], 1.0).then_inc(mem, 1)
            dve.memset(ones[:], 1.0).then_inc(mem, 1)
            dve.memset(mhalf[:], -0.5).then_inc(mem, 1)
            dve.memset(first, 1.0).then_inc(mem, 1)
            dve.memset(start, 1.0).then_inc(mem, 1)
            dve.wait_ge(mem, 6)
            dve.memset(first[:, :, 0], 0.0).then_inc(mem, 1)
            dve.memset(start[:, :, 0], 0.0).then_inc(mem, 1)
            for e in range(E):
                dve.memset(run[:, e:e + 1], float(e * REG)).then_inc(mem, 1)
                dve.memset(reg[:, e:e + 1], float(e * REG)).then_inc(mem, 1)
            dve.wait_ge(mem, 8 + 2 * E)

            def take_row(n, dst):
                dve.wait_ge(made, 3 + n)
                dve.tensor_copy(dst, ints[:, 0:COUNTS[n][1]]).then_inc(counted, 1)

            take_row(0, idf[:].rearrange("p k t -> p (k t)"))
            take_row(1, aside[:])
            dve.memset(pad[:, 0:D + 1], 0.0).then_inc(pad_done, 1)
            dve.memset(pad[:, D + 1:], NOWHERE).then_inc(pad_done, 1)
            dve.wait_ge(r_in, 32)

            def stats(c, q):
                par = q % 2
                wait_slot(dve, x_in[q], c, XR, q)
                for i in range(NT):
                    ins = dve.bn_stats(st[:, par, i, :], x1[:, q, i, :])
                ins.then_inc(stat, 1)
                wait_apart(dve, passed, [(stat, 2, c, 1)])
                for i in range(NT):
                    ins = dve.bn_aggr(mv[:, par, i, :], st[:, par, i, :])
                ins.then_inc(stat, 1)

            def normalise(c, q):
                par = q % 2
                wait(dve, rs_done, 2, c, 2)
                for i in range(NT):
                    ins = dve.tensor_scalar(x1[:, q, i, :], x1[:, q, i, :], mv[:, par, i, 0:1],
                                            rs[:, par, i:i + 1], ALU.subtract, ALU.mult)
                ins.then_inc(xn_done, 1)

            def route(j):
                count = [0]

                def link(ins):
                    count[0] += 1
                    ins.then_inc(step, 1)
                    wait(dve, step, KR, j, count[0])

                wait(dve, logit, GC, j, GC)
                link(dve.tensor_tensor(lg, ps_l[:, 0:W].rearrange("p (i e) -> p i e", e=E),
                                       bgb[:].unsqueeze(1).broadcast_to([P, GT, E]), ALU.add))
                for k in range(2):
                    link(dve.tensor_reduce(mx[:, k, :], lg, AX.X, ALU.max))
                    link(dve.tensor_tensor(eq, lg, mx[:, k, :].unsqueeze(2).broadcast_to([P, GT, E]),
                                           ALU.is_equal))
                    link(dve.tensor_tensor_scan(cn.rearrange("p i e -> p (i e)"),
                                                first.rearrange("p i e -> p (i e)"),
                                                eq.rearrange("p i e -> p (i e)"), 0.0, ALU.mult, ALU.add))
                    link(dve.scalar_tensor_tensor(sel[:, k], cn, 1.0, eq, ALU.is_equal, ALU.mult))
                    if k == 0:
                        link(dve.scalar_tensor_tensor(lg, sel[:, 0], -3e38, lg, ALU.mult, ALU.add))
                link(dve.tensor_tensor(both, sel[:, 0], sel[:, 1], ALU.add))
                assert count[0] == 11
                link(dve.tensor_tensor(ex, mx[:, 1, :], mx[:, 0, :], ALU.subtract))
                wait(dve, ranked, 1, j, 1)
                link(dve.tensor_copy(tot, ps_n[:, 0:W].rearrange("p (i e) -> p e i", e=E)))
                link(dve.tensor_tensor_scan(cum.rearrange("p i e -> p (i e)"),
                                            start.rearrange("p e i -> p (e i)"),
                                            tot.rearrange("p e i -> p (e i)"), 0.0, ALU.mult, ALU.add))
                cum_ei = cum.rearrange("p i e -> p (i e)").rearrange("p (e i) -> p e i", e=E)
                dve.tensor_tensor(excl.rearrange("p i e -> p e i"), cum_ei, tot, ALU.subtract)
                wait(dve, e_done, 1, j, 1)
                link(dve.tensor_scalar(den, ex, 1.0, None, ALU.add))
                link(dve.tensor_tensor(excl, excl, run[:].unsqueeze(1).broadcast_to([P, GT, E]), ALU.add))
                dve.tensor_tensor(slot, ps_r[:, 0:W].rearrange("p (i e) -> p i e", e=E), excl, ALU.add)
                link(dve.tensor_tensor(run[:], cum_ei[:, :, GT - 1], run[:], ALU.add))
                for k in range(2):
                    ins = dve.tensor_tensor(pick[:, k], sel[:, k], slot, ALU.mult)
                link(ins)
                for k in range(2):
                    ins = dve.tensor_reduce(slf[:, k, :], pick[:, k], AX.X, ALU.add)
                link(ins)
                wait(dve, staged, GC, j, 0)
                for par in range(2):
                    wait(dve, scat[par], 16 * SC * GC // 2, j, 0)
                link(dve.reciprocal(wt[:, 0, :], den))
                link(dve.tensor_tensor(wt[:, 1, :], wt[:, 0, :], ex, ALU.mult))
                link(dve.tensor_copy(sli[:], slf))
                assert count[0] == KR, count

            def group(j):
                for q in range(GC):
                    if q + 1 < GC or not last_group(j):
                        stats(j * GC + q + 1, (q + 1) % GC)
                    normalise(j * GC + q, q)
                route(j)

            stats(0, 0)
            groups(dve, group)

            count = [0]

            def link(ins):
                count[0] += 1
                ins.then_inc(tabs, 1)
                dve.wait_ge(tabs, count[0])

            for n, dst in ((2, jf), (3, tf)):
                take_row(n, dst)
            dve.wait_ge(counted, 4)
            link(dve.tensor_tensor(cnt[:], run[:], reg[:], ALU.subtract))
            link(dve.tensor_copy(padi[:], run[:]))
            link(dve.tensor_tensor(over, cnt[:].unsqueeze(2).broadcast_to([P, E, T]),
                                   jf.unsqueeze(1).broadcast_to([P, E, T]), ALU.is_gt))
            link(dve.tensor_reduce(ntl[:], over, AX.X, ALU.add))
            link(dve.tensor_tensor_scan(end[:], ones[:, 0:E], ntl[:], 0.0, ALU.mult, ALU.add))
            link(dve.tensor_scalar(skip[:], ntl[:], float(-P), float(REG), ALU.mult, ALU.add))
            link(dve.tensor_tensor(cmp, end[:].unsqueeze(1).broadcast_to([P, NTT, E]),
                                   tf.unsqueeze(2).broadcast_to([P, NTT, E]), ALU.is_le))
            link(dve.tensor_reduce(eid, cmp, AX.X, ALU.add))
            link(dve.tensor_tensor(cmp, cmp, skip[:].unsqueeze(1).broadcast_to([P, NTT, E]), ALU.mult))
            link(dve.tensor_reduce(row, cmp, AX.X, ALU.add))
            dve.tensor_scalar(tabi[:, 1, :], eid, float(E - 1), None, ALU.min)
            link(dve.scalar_tensor_tensor(tabi[:, 0, :], tf, float(P), row, ALU.mult, ALU.add))
            assert count[0] == KT, count

            dve.wait_ge(w_in, 16 * (3 + KD))

            def tile_step(s, slot):
                par = slot % 2
                if real(s - 1):
                    t = s - 1
                    e = dve.value_load(tabi[0:1, 1, bass.ds(t, 1)], min_val=0, max_val=E - 1)
                    wait(dve, h_full, 1, t, 1)
                    wait(dve, h_turned, 1, t, -1)
                    dve.tensor_tensor(hb[:, 1 - par, :], ps_h[:, 1 - par, :], b1b[:, bass.ds(e * F, F)], ALU.add
                                      ).then_inc(h_done, 1)
                if real(s - 3):
                    t = s - 3
                    e = dve.value_load(tabi[0:1, 1, bass.ds(t, 1)], min_val=0, max_val=E - 1)
                    wait_slot(dve, t_out[1 - par], t, 2, 1 - par, more=-1)
                    wait(dve, x_copied, 1, t, 1)
                    dve.tensor_tensor(idx[:, 1 - par, :], meta[:, (slot + 1) % RING, 1:], aside[:, bass.ds(t, 1)],
                                      ALU.min).then_inc(idx_done, 1)
                    wait(dve, o_full, 1, t, 1)
                    wait(dve, o_weighed, 1, t, -1)
                    dve.tensor_tensor(ot[:, 1 - par, :], ps_o[:, 1 - par, 0:D], b2b[:, bass.ds(e * D, D)], ALU.add
                                      ).then_inc(o_done, 1)

            tiles(dve, tile_step)

            def combine(c, q):
                par = q % 2
                wait(dve, summed, 2, c, 1)
                dve.tensor_tensor(ee[:, par, 0], ee[:, par, 0], at(xn, c), ALU.add).then_inc(summed, 1)
                wait(dve, summed, 2, c, 2)
                for i in range(NT):
                    ins = dve.bn_stats(st[:, par, i, :], ee[:, par, 0, i, :])
                ins.then_inc(c_stat, 1)
                wait_apart(dve, passed, [(c_stat, 2, c, 1)])
                for i in range(NT):
                    ins = dve.bn_aggr(mv[:, par, i, :], st[:, par, i, :])
                ins.then_inc(c_stat, 1)
                wait(dve, c_stat, 2, c, 2)
                for i in range(NT):
                    ins = dve.scalar_tensor_tensor(ee[:, par, 1, i, :], ee[:, par, 0, i, :], mv[:, par, i, 0:1],
                                                   gm, ALU.subtract, ALU.mult)
                ins.then_inc(scaled, 1)

            def finish(c, q):
                par = q % 2
                wait(dve, scaled, 1, c, 1)
                wait(dve, c_rs, 2, c, 2)
                wait(dve, biased, 1, c, 1)
                for i in range(NT):
                    ins = dve.scalar_tensor_tensor(x1[:, q, i, :], ee[:, par, 1, i, :], rs[:, par, i:i + 1],
                                                   x1[:, q, i, :], ALU.mult, ALU.add)
                ins.then_inc(done, 1)

            def both_steps(c, q):
                combine(c, q)
                finish(c, q)

            dve.wait_ge(g_in, 32)
            chunks(dve, both_steps)

        @block.gpsimd
        def _(pool):
            pool.wait_ge(mem, 2)
            pool.affine_select(out=ident[:], in_=ident[:], compare_op=ALU.is_equal, fill=0.0, base=0,
                               pattern=[[-1, P]], channel_multiplier=1).then_inc(made, 1)
            pool.affine_select(out=below[:], in_=below[:], compare_op=ALU.is_ge, fill=0.0, base=-1,
                               pattern=[[1, P]], channel_multiplier=-1).then_inc(made, 1)
            pool.wait_ge(mem, 4)
            def make_row(n):
                step_by, width, base, up = COUNTS[n]
                if n:
                    pool.wait_ge(counted, n)
                pool.iota(ints[:, 0:width], pattern=[[step_by, width]], base=base, channel_multiplier=up
                          ).then_inc(made, 1)

            make_row(0)
            make_row(1)

            def inv_std(c, par, stat, rs_done):
                wait_apart(pool, passed, [(stat, 2, c, 2)])
                pool.tensor_scalar(ve[:, par, :], mv[:, par, :, 1], EPS, None, ALU.add).then_inc(rs_done, 1)
                wait(pool, rs_done, 2, c, 1)
                pool.tensor_tensor(rs[:, par, :], ve[:, par, :], mhalf[:], ALU.pow).then_inc(rs_done, 1)

            def scatter(j, q):
                wait_apart(pool, passed, [(step, KR, j, KR), (staged, GC, j, q + 1)])
                for i in range(NT):
                    for k in range(2):
                        pool.indirect_dma_start(
                            out=xs_dram,
                            out_offset=bass.IndirectOffsetOnAxis(ap=sli[:, k, q * NT + i:q * NT + i + 1], axis=0),
                            in_=stage[:, q % 2, k, i, :], in_offset=None).then_inc(scat[q % 2], 16)

            def group(j):
                for q, rest in ((0, (1,)), (1, (2, 3)), (2, () if last_group(j) else (GC,)), (3, ())):
                    if not isinstance(j, int) or j > 0:
                        scatter(j - 1, q)
                    for q1 in rest:
                        inv_std(j * GC + q1, q1 % 2, stat, rs_done)

            inv_std(0, 0, stat, rs_done)
            groups(pool, group)
            make_row(2)
            make_row(3)
            for q in range(GC):
                scatter(NG - 1, q)

            def store_tile(s, slot):
                if real(s - 3):
                    t, par = s - 3, slot % 2
                    wait_apart(pool, passed, [(o_weighed, 1, t, 1), (idx_done, 1, t, 1)])
                    pool.indirect_dma_start(
                        out=eo_dram, out_offset=bass.IndirectOffsetOnAxis(ap=idx[:, 1 - par, :], axis=0),
                        in_=ow[:, 1 - par, :], in_offset=None).then_inc(t_out[1 - par], 16)

            tiles(pool, store_tile)

            pool.wait_ge(g_in, 32)

            def combine(c, q):
                par = q % 2
                wait_slot(pool, c_in[par], c, 2, par, per=16 * LD)
                pool.tensor_tensor(ee[:, par, 0], ee[:, par, 0], ee[:, par, 1], ALU.add).then_inc(summed, 1)
                wait_slot(pool, x1_in[q], c, XR, q)
                for i in range(NT):
                    ins = pool.tensor_tensor(x1[:, q, i, :], x1[:, q, i, :], bt, ALU.add)
                ins.then_inc(biased, 1)
                inv_std(c, par, c_stat, c_rs)

            chunks(pool, combine)

        @block.scalar
        def _(act):
            act.wait_ge(counted, 1)

            def stage_rows(j, q):
                par, c = q % 2, j * GC + q
                if q == 0:
                    wait(act, step, KR, j, KR)
                wait(act, kept, 1, c, 1)
                wait_slot(act, scat[par], c, 2, par, per=16 * SC, more=-1)
                for k in range(2):
                    act.copy(stage[:, par, k, :, 0:D], at(xn, c))
                act.copy(stage[:, par, :, :, D], wt[:, :, q * NT:(q + 1) * NT])
                act.copy(stage[:, par, :, :, D + 1], idf[:, :, bass.ds(c * NT, NT)]).then_inc(staged, 1)

            def load_experts():
                for k in range(KD):
                    act.dma_start(w1[:, k, :].rearrange("p (e f) -> p e f", e=E),
                                  W1[:, k * P:(k + 1) * P, :].rearrange("e p f -> p e f")).then_inc(w_in, 16)
                act.dma_start(w2[:].rearrange("p (e k d) -> p e k d", e=E, k=KF),
                              W2.rearrange("e (k p) d -> p e k d", p=P)).then_inc(w_in, 16)
                act.dma_start(b1b[:], b1.rearrange("e f -> (e f)").partition_broadcast(P)).then_inc(w_in, 16)
                act.dma_start(b2b[:], b2.rearrange("e d -> (e d)").partition_broadcast(P)).then_inc(w_in, 16)

            def keep(c, q):
                wait(act, xn_done, 1, c, 1)
                act.copy(at(xn, c), x1[:, q]).then_inc(kept, 1)
                for k in range(KD):
                    wait(act, turned, KD, c, k + 1)
                    if k == 0:
                        wait(act, logit, 1, c, 0)
                    act.copy(rT[:, k, :], ps_x[:, k, :]).then_inc(copied, 1)

            def group(j):
                after = not isinstance(j, int) or j > 0
                if after:
                    stage_rows(j - 1, 0)
                    stage_rows(j - 1, 1)
                for q in range(GC):
                    if after and q == 2:
                        stage_rows(j - 1, 2)
                    keep(j * GC + q, q)
                if after:
                    stage_rows(j - 1, 3)
                else:
                    load_experts()
                wait(act, step, KR, j, 12)
                act.activation(ex, ex, ACT.Exp).then_inc(e_done, 1)

            groups(act, group)
            for q in range(GC):
                stage_rows(NG - 1, q)

            def tile_step(s, slot):
                par = slot % 2
                if real(s):
                    wait(act, x_turned, 1, s, 1)
                    wait(act, idx_done, 1, s, 1 - RING)
                    wait(act, o_weighed, 1, s, 1 - RING)
                    act.copy(meta[:, slot, :], xt[:, slot, D:])
                    wait(act, h_full, 1, s, -1)
                    act.copy(xT[:, par, :], ps_x[:, par, 0:KD * P]).then_inc(x_copied, 1)
                if real(s - 2):
                    t = s - 2
                    wait(act, h_turned, 1, t, 1)
                    wait(act, o_full, 1, t, -1)
                    act.activation(hT[:, par, :], ps_t[:, par, :], ACT.Relu).then_inc(h_relu, 1)
                if real(s - 3):
                    t = s - 3
                    wait(act, o_done, 1, t, 1)
                    wait_slot(act, t_out[1 - par], t, 2, 1 - par, more=-1)
                    wait(act, x_copied, 1, t, 1)
                    act.mul(ow[:, 1 - par, :], ot[:, 1 - par, :], meta[:, (slot + 1) % RING, 0:1]
                            ).then_inc(o_weighed, 1)

            act.wait_ge(tabs, KT)
            tiles(act, tile_step)

            def store(c, q):
                wait(act, done, 1, c, 1)
                act.dma_start(rows_of(out_t, c), x1[:, q]).then_inc(o_out[q], 16)

            chunks(act, store)
            for q in range(XR):
                act.wait_ge(o_out[q], 16 * NC // XR)

        @block.tensor
        def _(pe):
            pe.wait_ge(r_in, 32)
            pe.wait_ge(made, 2)
            pe.wait_ge(mem, 3)

            def group(j):
                for q in range(GC):
                    c = j * GC + q
                    wait(pe, xn_done, 1, c, 1)
                    for k in range(KD):
                        wait(pe, copied, KD, c, k + 1 - KD)
                        for i in range(NT):
                            ins = pe.transpose(ps_x[:, k, i * P:(i + 1) * P], x1[:, q, i, k * P:(k + 1) * P],
                                               ident[:])
                        ins.then_inc(turned, 1)
                    wait(pe, copied, KD, c, KD)
                    if q == 0:
                        wait(pe, step, KR, j, 1 - KR)
                    for i in range(NT):
                        m = (q * NT + i) * E
                        for k in range(KD):
                            ins = pe.matmul(ps_l[:, m:m + E], rT[:, k, i * P:(i + 1) * P], wg[:, k, :],
                                            start=(k == 0), stop=(k == KD - 1))
                    ins.then_inc(logit, 1)
                wait(pe, step, KR, j, 11)
                pe.matmul(ps_r[:, 0:W], below[:], both.rearrange("p i e -> p (i e)"), start=True, stop=True)
                pe.matmul(ps_n[:, 0:W], ones[:], both.rearrange("p i e -> p (i e)"), start=True, stop=True
                          ).then_inc(ranked, 1)

            groups(pe, group)
            pe.wait_ge(step, KR * NG)
            pe.wait_ge(tabs, KT)
            pe.wait_ge(w_in, 16 * (3 + KD))

            def tile_step(s, slot):
                par = slot % 2
                if real(s):
                    wait_slot(pe, t_in[slot], s, RING, slot)
                    wait(pe, x_copied, 1, s, -1)
                    for k in range(KD):
                        ins = pe.transpose(ps_x[:, par, k * P:(k + 1) * P], xt[:, slot, k * P:(k + 1) * P], ident[:])
                    ins.then_inc(x_turned, 1)
                if real(s - 1):
                    t = s - 1
                    e = pe.value_load(tabi[0:1, 1, bass.ds(t, 1)], min_val=0, max_val=E - 1)
                    wait(pe, x_copied, 1, t, 1)
                    wait(pe, h_done, 1, t, -1)
                    for k in range(KD):
                        ins = pe.matmul(ps_h[:, 1 - par, :], xT[:, 1 - par, k * P:(k + 1) * P],
                                        w1[:, k, bass.ds(e * F, F)], start=(k == 0), stop=(k == KD - 1))
                    ins.then_inc(h_full, 1)
                if real(s - 2):
                    t = s - 2
                    wait(pe, h_done, 1, t, 1)
                    wait(pe, h_relu, 1, t, -1)
                    for k in range(KF):
                        ins = pe.transpose(ps_t[:, par, k * P:(k + 1) * P], hb[:, par, k * P:(k + 1) * P], ident[:])
                    ins.then_inc(h_turned, 1)
                if real(s - 3):
                    t = s - 3
                    e = pe.value_load(tabi[0:1, 1, bass.ds(t, 1)], min_val=0, max_val=E - 1)
                    wait(pe, h_relu, 1, t, 1)
                    wait(pe, o_done, 1, t, -1)
                    for k in range(KF):
                        ins = pe.matmul(ps_o[:, 1 - par, 0:D], hT[:, 1 - par, k * P:(k + 1) * P],
                                        w2[:, bass.ds((e * KF + k) * D, D)], start=(k == 0), stop=(k == KF - 1))
                    ins.then_inc(o_full, 1)

            tiles(pe, tile_step)


_INS = ['L0_attn_x', 'L0_attn_ln_g', 'L0_attn_ln_b', 'L0_attn_W_in', 'L0_attn_conv_w', 'L0_attn_conv_b',
        'L0_attn_W_xproj', 'L0_attn_W_dt', 'L0_attn_b_dt', 'L0_attn_A_log', 'L0_attn_D_param', 'L0_attn_W_out',
        'L0_ffn_Wg', 'L0_ffn_bg', 'L0_ffn_W1', 'L0_ffn_b1', 'L0_ffn_W2', 'L0_ffn_b2', 'L0_ffn_gamma',
        'L0_ffn_beta']
_OUTS = [((8, 1024, 256), 'float32')]


def kernel(**inputs):
    import numpy as _np
    import concourse.bacc as _bacc
    from concourse import mybir as _mybir
    from concourse.bass_utils import run_bass_kernel_spmd as _run

    nc = _bacc.Bacc("TRN2", target_bir_lowering=False, num_devices=1)
    arrays, args = {}, []
    for name in _INS:
        a = _np.ascontiguousarray(inputs[name])
        arrays[f"in_{name}_dram"] = a
        args.append(nc.dram_tensor(f"in_{name}_dram", a.shape, _mybir.dt.from_np(a.dtype), kind="ExternalInput").ap())
    for i, (shape, dtype) in enumerate(_OUTS):
        dt = _mybir.dt.from_np(_np.dtype(dtype))
        args.append(nc.dram_tensor(f"out_{i}_dram", shape, dt, kind="ExternalOutput").ap())
    mamba_moe_kernel(nc, *args)
    r = _run(nc, [arrays], core_ids=[0])
    got = tuple(r.results[0][f"out_{i}_dram"] for i in range(len(_OUTS)))
    return got[0]
```
